# Optimizing a Trainium2 kernel written in Bass

```python
import numpy as np
import jax
import jax.numpy as jnp

def _softmax(x, axis=-1):
    return jax.nn.softmax(x, axis=axis)

def _gelu(x):
    return jax.nn.gelu(x, approximate=True)

def _silu(x):
    return jax.nn.silu(x)

def _sigmoid(x):
    return jax.nn.sigmoid(x)

def _layernorm(x, axis=-1, eps=1e-05):
    m = jnp.mean(x, axis=axis, keepdims=True)
    v = jnp.var(x, axis=axis, keepdims=True)
    return (x - m) / jnp.sqrt(v + eps)

def _scatter_add(tgt, idx, src, axis=0):
    return tgt.at[idx].add(src)

def _segment_sum(src, seg, n):
    return jax.ops.segment_sum(src, seg, n)
kernel_name = 'mk_early_fusion_d1_tok_img768_r4_a8b857'

def setup_inputs(seed: int=0):
    np.random.seed(seed)
    _w = jnp.asarray

    def _rec_inputs():
        import jax
        import jax.numpy as jnp
        _rk = jax.random.key(seed)
        x = 7.57192e-06 + 1.00007 * jax.random.normal(jax.random.fold_in(_rk, 1), (32, 224, 224, 3), jnp.float32)
        txt = -0.000241419 + 1.20654 * jax.random.normal(jax.random.fold_in(_rk, 2), (32, 77, 192), jnp.float32)
        return (x, txt)
    x, txt = _rec_inputs()

    def _L0_tok_setup():
        import jax, jax.numpy as jnp
        import numpy as np
        IMG = 224
        P = 16
        HP = P // 2
        D = 192
        C_IN = 3
        B = 64

        def _crop_shift_pad(images, oh, ow):
            th = IMG - HP
            tw = IMG - HP
            out = jnp.zeros_like(images)
            return out.at[:, oh:oh + th, ow:ow + tw, :].set(images[:, oh:oh + th, ow:ow + tw, :])
        key = jax.random.key(seed)
        k1, k2 = jax.random.split(key, 2)
        images = jax.random.normal(k1, (B, IMG, IMG, C_IN), dtype=jnp.float32)
        pvs = P * P * C_IN * 5
        W = jax.random.normal(k2, (pvs, D), dtype=jnp.float32) * 0.02
        b = jnp.zeros((D,), dtype=jnp.float32)
        return {'images': images, 'W': W, 'b': b}
    _L0_tok_all = _L0_tok_setup()
    _L0_tok_in = {k: v for k, v in _L0_tok_all.items() if k in ('W', 'b')}
    del _L0_tok_all

    def _L0_attn_setup():
        import jax, jax.numpy as jnp
        import numpy as np
        import math
        D_MODEL = 192
        N_HEADS = 12
        D_HEAD = D_MODEL // N_HEADS
        LATENT = 128
        HIDDEN = 512
        B, L = (1, 512)

        def _w(key, shape, scale=0.02):
            return jax.random.normal(key, shape, dtype=jnp.float32) * scale

        def rmsnorm(x, w, eps=1e-06):
            xf = x.astype(jnp.float32)
            rms = jax.lax.rsqrt(jnp.mean(xf * xf, axis=-1, keepdims=True) + eps)
            return w * (xf * rms).astype(x.dtype)

        def rope(x):
            Lx, Dh = (x.shape[1], x.shape[3])
            inv_freq = 1.0 / 10000.0 ** (jnp.arange(0, Dh, 2, dtype=jnp.float32) / Dh)
            t = jnp.arange(Lx, dtype=jnp.float32)
            freqs = jnp.outer(t, inv_freq)
            emb = jnp.concatenate([freqs, freqs], -1)
            cos = jnp.cos(emb)[None, :, None, :]
            sin = jnp.sin(emb)[None, :, None, :]
            x1, x2 = jnp.split(x, 2, axis=-1)
            x_rot = jnp.concatenate([-x2, x1], axis=-1)
            return x * cos + x_rot * sin
        key = jax.random.key(seed)
        ks = jax.random.split(key, 12)
        return {'x': jax.random.normal(ks[0], (B, L, D_MODEL), dtype=jnp.float32), 'ln_w': jnp.ones((D_MODEL,), jnp.float32), 'w_comp': _w(ks[1], (D_MODEL, LATENT)), 'w_qkv': _w(ks[2], (LATENT, 3 * D_MODEL)), 'w_reso': _w(ks[3], (LATENT, N_HEADS * 4)), 'qn_w': jnp.ones((D_HEAD,), jnp.float32), 'kn_w': jnp.ones((D_HEAD,), jnp.float32), 'w_outgate': _w(ks[4], (LATENT, D_MODEL)), 'head_decay': jnp.linspace(-3.0, 1.0, N_HEADS, dtype=jnp.float32), 'temperature': jnp.ones((1,), jnp.float32) * 0.5, 'w_proj': _w(ks[5], (D_MODEL, D_MODEL)), 'memn_w': jnp.ones((D_MODEL,), jnp.float32), 'ffn_ln_w': jnp.ones((D_MODEL,), jnp.float32), 'w1': _w(ks[6], (D_MODEL, HIDDEN)), 'w2': _w(ks[7], (D_MODEL, HIDDEN)), 'w3': _w(ks[8], (HIDDEN, D_MODEL))}
    _L0_attn_all = _L0_attn_setup()
    _L0_attn_in = {k: v for k, v in _L0_attn_all.items() if k in ('ln_w', 'w_comp', 'w_qkv', 'w_reso', 'qn_w', 'kn_w', 'w_outgate', 'head_decay', 'temperature', 'w_proj', 'memn_w', 'ffn_ln_w', 'w1', 'w2', 'w3')}
    del _L0_attn_all

    def _L0_ffn_setup():
        import jax, jax.numpy as jnp
        import numpy as np
        E, C, F, K = (8, 192, 768, 2)
        key = jax.random.key(seed)
        k0, k1, k2, k3 = jax.random.split(key, 4)
        B, T = (8, 512)
        return {'x': jax.random.normal(k0, (B, T, C), jnp.float32), 'router_w': jax.random.normal(k1, (E, C), jnp.float32) * 0.02, 'w1': jax.random.normal(k2, (E, C, F), jnp.float32) * 0.02, 'b1': jnp.zeros((E, F), jnp.float32), 'w2': jax.random.normal(k3, (E, F, C), jnp.float32) * 0.02, 'b2': jnp.zeros((E, C), jnp.float32)}
    _L0_ffn_all = _L0_ffn_setup()
    _L0_ffn_in = {k: v for k, v in _L0_ffn_all.items() if k in ('router_w', 'w1', 'b1', 'w2', 'b2')}
    del _L0_ffn_all
    return {'x': x, 'txt': txt, 'L0_tok_W': _L0_tok_in['W'], 'L0_tok_b': _L0_tok_in['b'], 'L0_attn_ln_w': _L0_attn_in['ln_w'], 'L0_attn_w_comp': _L0_attn_in['w_comp'], 'L0_attn_w_qkv': _L0_attn_in['w_qkv'], 'L0_attn_w_reso': _L0_attn_in['w_reso'], 'L0_attn_qn_w': _L0_attn_in['qn_w'], 'L0_attn_kn_w': _L0_attn_in['kn_w'], 'L0_attn_w_outgate': _L0_attn_in['w_outgate'], 'L0_attn_head_decay': _L0_attn_in['head_decay'], 'L0_attn_temperature': _L0_attn_in['temperature'], 'L0_attn_w_proj': _L0_attn_in['w_proj'], 'L0_attn_memn_w': _L0_attn_in['memn_w'], 'L0_attn_ffn_ln_w': _L0_attn_in['ffn_ln_w'], 'L0_attn_w1': _L0_attn_in['w1'], 'L0_attn_w2': _L0_attn_in['w2'], 'L0_attn_w3': _L0_attn_in['w3'], 'L0_ffn_router_w': _L0_ffn_in['router_w'], 'L0_ffn_w1': _L0_ffn_in['w1'], 'L0_ffn_b1': _L0_ffn_in['b1'], 'L0_ffn_w2': _L0_ffn_in['w2'], 'L0_ffn_b2': _L0_ffn_in['b2']}

def reference(x, txt, L0_tok_W, L0_tok_b, L0_attn_ln_w, L0_attn_w_comp, L0_attn_w_qkv, L0_attn_w_reso, L0_attn_qn_w, L0_attn_kn_w, L0_attn_w_outgate, L0_attn_head_decay, L0_attn_temperature, L0_attn_w_proj, L0_attn_memn_w, L0_attn_ffn_ln_w, L0_attn_w1, L0_attn_w2, L0_attn_w3, L0_ffn_router_w, L0_ffn_w1, L0_ffn_b1, L0_ffn_w2, L0_ffn_b2):
    import jax
    import jax.numpy as jnp

    def _L0_tok_ref(images, W, b):
        import jax, jax.numpy as jnp
        import numpy as np
        IMG = 224
        P = 16
        HP = P // 2
        D = 192
        C_IN = 3
        B = 64

        def _crop_shift_pad(images, oh, ow):
            th = IMG - HP
            tw = IMG - HP
            out = jnp.zeros_like(images)
            return out.at[:, oh:oh + th, ow:ow + tw, :].set(images[:, oh:oh + th, ow:ow + tw, :])
        offsets = [(0, 0), (HP, 0), (0, HP), (HP, HP)]
        concat = jnp.concatenate([images] + [_crop_shift_pad(images, oh, ow) for oh, ow in offsets], axis=-1)
        Bn, _, _, C = concat.shape
        g = IMG // P
        x = concat.reshape(Bn, g, P, g, P, C)
        x = x.transpose(0, 1, 3, 2, 4, 5).reshape(Bn, g * g, P * P * C)
        return x @ W + b

    def _L0_attn_ref(x, ln_w, w_comp, w_qkv, w_reso, qn_w, kn_w, w_outgate, head_decay, temperature, w_proj, memn_w, ffn_ln_w, w1, w2, w3):
        import jax, jax.numpy as jnp
        import numpy as np
        import math
        D_MODEL = 192
        N_HEADS = 12
        D_HEAD = D_MODEL // N_HEADS
        LATENT = 128
        HIDDEN = 512
        B, L = (1, 512)

        def _w(key, shape, scale=0.02):
            return jax.random.normal(key, shape, dtype=jnp.float32) * scale

        def rmsnorm(x, w, eps=1e-06):
            xf = x.astype(jnp.float32)
            rms = jax.lax.rsqrt(jnp.mean(xf * xf, axis=-1, keepdims=True) + eps)
            return w * (xf * rms).astype(x.dtype)

        def rope(x):
            Lx, Dh = (x.shape[1], x.shape[3])
            inv_freq = 1.0 / 10000.0 ** (jnp.arange(0, Dh, 2, dtype=jnp.float32) / Dh)
            t = jnp.arange(Lx, dtype=jnp.float32)
            freqs = jnp.outer(t, inv_freq)
            emb = jnp.concatenate([freqs, freqs], -1)
            cos = jnp.cos(emb)[None, :, None, :]
            sin = jnp.sin(emb)[None, :, None, :]
            x1, x2 = jnp.split(x, 2, axis=-1)
            x_rot = jnp.concatenate([-x2, x1], axis=-1)
            return x * cos + x_rot * sin
        Bx, Lx, D = x.shape
        H, Dh = (N_HEADS, D_HEAD)
        x_norm = rmsnorm(x, ln_w)
        latent = jax.nn.silu(x_norm @ w_comp)
        qkv = latent @ w_qkv
        q, k, v = jnp.split(qkv, 3, axis=-1)
        q = q.reshape(Bx, Lx, H, Dh)
        k = k.reshape(Bx, Lx, H, Dh)
        v = v.reshape(Bx, Lx, H, Dh)
        q = rope(rmsnorm(q, qn_w))
        k = rope(rmsnorm(k, kn_w))
        q_f = jax.nn.elu(q.astype(jnp.float32)) + 1.0
        k_f = jax.nn.elu(k.astype(jnp.float32)) + 1.0
        v_f = v.astype(jnp.float32)
        params = (latent @ w_reso).reshape(Bx, Lx, H, 4)
        sem_amp = jax.nn.sigmoid(params[..., 0])
        sem_phase = jax.nn.sigmoid(params[..., 1]) * math.pi
        ctx_amp = jax.nn.sigmoid(params[..., 2])
        ctx_phase = jax.nn.sigmoid(params[..., 3]) * math.pi
        raw_decay = 0.3 + 0.65 * jax.nn.sigmoid(head_decay.reshape(1, 1, H))
        decay_rate = jnp.clip(raw_decay, 1e-05, 0.999)
        dt = 1.0 - decay_rate
        base_gate = jax.nn.sigmoid(sem_amp * ctx_amp * jnp.cos(sem_phase - ctx_phase) * temperature)
        gate = jnp.clip(base_gate * 1.2 - 0.1, 0.05, 0.95)
        kv_input = jnp.einsum('blhd,blhe->blhde', k_f, v_f) * gate[..., None, None]
        kv_input = kv_input * dt[..., None, None]
        z_input = k_f * dt[..., None]
        log_decay = jnp.log(decay_rate)[..., None]
        cum_log_decay = jnp.cumsum(jnp.broadcast_to(log_decay, (Bx, Lx, H, 1)), axis=1)
        df = jnp.exp(cum_log_decay)
        safe_df_z = df + 1e-08
        kv_states = jnp.cumsum(kv_input / safe_df_z[..., None], axis=1) * df[..., None]
        z_states = jnp.cumsum(z_input / safe_df_z, axis=1) * df
        out_num = jnp.einsum('blhd,blhde->blhe', q_f, kv_states)
        den = jnp.clip(jnp.sum(q_f * z_states, axis=-1, keepdims=True), 1e-05, None)
        out = (out_num / den).reshape(Bx, Lx, D)
        out = rmsnorm(out, memn_w)
        attn_out = out @ w_proj * jax.nn.silu(latent @ w_outgate)
        x = x + attn_out
        xn = rmsnorm(x, ffn_ln_w)
        ffn_out = jax.nn.silu(xn @ w1) * (xn @ w2) @ w3
        return x + ffn_out

    def _L0_ffn_ref(x, router_w, w1, b1, w2, b2):
        import jax, jax.numpy as jnp
        import numpy as np
        E, C, F, K = (8, 192, 768, 2)
        B, T, Cc = x.shape
        flat = x.reshape(-1, Cc)
        logits = flat @ router_w.T
        probs = jax.nn.softmax(logits.astype(jnp.float32), axis=-1)
        top_w, top_i = jax.lax.top_k(probs, K)
        top_w = (top_w / top_w.sum(-1, keepdims=True)).astype(x.dtype)
        out = jnp.zeros_like(flat)
        for e in range(E):
            w_e = jnp.sum(top_w * (top_i == e), axis=-1)[:, None]
            h = jax.nn.gelu(flat @ w1[e] + b1[e], approximate=False)
            out = out + w_e * (h @ w2[e] + b2[e])
        return out.reshape(B, T, Cc)
    h = _L0_tok_ref(x, L0_tok_W, L0_tok_b)
    h = jnp.concatenate([h, txt], axis=1)
    h = h + _L0_attn_ref(_layernorm(h, axis=-1), L0_attn_ln_w, L0_attn_w_comp, L0_attn_w_qkv, L0_attn_w_reso, L0_attn_qn_w, L0_attn_kn_w, L0_attn_w_outgate, L0_attn_head_decay, L0_attn_temperature, L0_attn_w_proj, L0_attn_memn_w, L0_attn_ffn_ln_w, L0_attn_w1, L0_attn_w2, L0_attn_w3)
    h = h + _L0_ffn_ref(_layernorm(h, axis=-1), L0_ffn_router_w, L0_ffn_w1, L0_ffn_b1, L0_ffn_w2, L0_ffn_b2)
    return h

_drawn_inputs = setup_inputs


def setup_inputs(seed=0):
    import zlib

    import numpy as np

    out = dict(_drawn_inputs(seed))
    spreads = {'L0_tok_b': (0.0, 0.1),
     'L0_attn_ln_w': (1.0, 0.6),
     'L0_attn_qn_w': (1.0, 0.6),
     'L0_attn_kn_w': (1.0, 0.6),
     'L0_attn_memn_w': (1.0, 0.6),
     'L0_attn_ffn_ln_w': (1.0, 0.6),
     'L0_ffn_b1': (0.0, 2.0),
     'L0_ffn_b2': (0.0, 0.8)}
    factors = {'L0_attn_w_comp': 8.0,
     'L0_attn_w_qkv': 8.0,
     'L0_attn_w_reso': 8.0,
     'L0_attn_w_outgate': 8.0,
     'L0_attn_head_decay': 8.0,
     'L0_attn_w_proj': 8.0,
     'L0_attn_w1': 6.311,
     'L0_attn_w2': 6.359,
     'L0_attn_w3': 6.277,
     'L0_ffn_router_w': 3.771,
     'L0_ffn_w1': 8.0,
     'L0_ffn_w2': 3.411}
    for name, (base, spread) in spreads.items():
        noise = np.random.default_rng([zlib.crc32(name.encode()), seed]).standard_normal(out[name].shape)
        drawn = base * np.exp(spread * noise) if base else spread * noise
        out[name] = jnp.asarray(drawn.astype(out[name].dtype))
    for name, factor in factors.items():
        out[name] = (out[name] * factor).astype(out[name].dtype)
    return out
```

```python
import concourse.bass as bass
from concourse import mybir
from contextlib import ExitStack
import numpy as np

B, IMG, P16, CIN, D = 32, 224, 16, 3, 192
G = IMG // P16
NPATCH, NTXT = G * G, 77
L = NPATCH + NTXT
CH = 91
NCH = L // CH
H, DH = 12, 16
GR = 3
KD = 96
LAT, HID = 128, 512
E, F = 8, 768
NTOK = B * L
T = 384
TC = T // 128
CAP = NTOK + T
NTASK = (2 * NTOK + E * (T - 1)) // T
IDLE = NTASK - (2 * NTOK + T - 1) // T
ROW = D + 2
VE = DH + 1
RSTEPS = (NTOK + T - 1) // T
assert L == CH * NCH and H == 4 * GR and D == 2 * KD and 128 % P16 == 0

f32, i32, u32 = mybir.dt.float32, mybir.dt.int32, mybir.dt.uint32
ALU, ACT, AX = mybir.AluOpType, mybir.ActivationFunctionType, mybir.AxisListType

_nodes = 2 + 2 * np.cos(np.pi * (np.arange(400) + 0.5) / 400)
COS_POLY = [float(c) for c in np.polynomial.chebyshev.Chebyshev.fit(
    _nodes, np.cos(np.pi / 2 * np.sqrt(_nodes)), 7, domain=[0, 4]).convert(kind=np.polynomial.Polynomial).coef]


def constants():
    parts = {}
    s, t = np.arange(CH)[:, None], np.arange(CH)[None, :]
    parts["ident"] = np.eye(128)
    parts["causal"] = (s <= t)
    parts["before"] = (s < t)
    parts["ones"] = np.ones((CH, CH))
    slot = np.arange(128)[:, None] // 32
    parts["headblock"] = slot == (np.arange(4 * VE)[None, :] // VE)
    inv = 1.0 / 10000.0 ** (np.arange(0, DH, 2, dtype=np.float32) / np.float32(DH))
    pos = np.arange(L, dtype=np.float32)
    ang = np.outer(pos, inv.astype(np.float32)).astype(np.float32)
    cos, sin = np.cos(ang), np.sin(ang)
    tok = lambda a: a.reshape(NCH, CH, -1).transpose(1, 0, 2).reshape(CH, -1)
    parts["cos"] = tok(np.concatenate([cos, cos], 1))
    parts["sin"] = tok(np.concatenate([-sin, sin], 1))
    parts["pos1"] = tok((pos + 1)[:, None])
    parts["tokno"] = tok(pos[:, None])
    px = np.arange(128) % P16
    parts["right_half"] = (px >= P16 // 2)[:, None]
    parts["left_half"] = (px < P16 // 2)[:, None]
    parts["expert"] = np.tile(np.arange(E), (128, 1))
    parts["base"] = np.tile(np.arange(E) * CAP, (128, NCH))
    parts["steps"] = np.tile(np.arange(RSTEPS) * T, (1, 1))
    parts["upto"] = np.tril(np.ones((E, E))).reshape(1, -1)
    parts["task"] = np.arange(NTASK)[None, :]
    parts["padid"] = NTOK + np.arange(128)[:, None] + 128 * np.arange(TC)[None, :]
    at, cols = {}, []
    n = 0
    for k, a in parts.items():
        a = np.asarray(a, np.float32)
        full = np.zeros((128, a.shape[1]), np.float32)
        full[:a.shape[0]] = a
        at[k] = (n, n + a.shape[1])
        n += a.shape[1]
        cols.append(full)
    return np.concatenate(cols, 1), at


CONST, CONST_AT = constants()


class Memory:

    def __init__(self, nc, ctx):
        self.nc, self.ctx = nc, ctx
        self.ps = [ctx.enter_context(nc.psum_tensor(f"bank{i}", [128, 512], f32)) for i in range(8)]
        self.X, self.Y = self.ps[:4], [self.ps[4:6], self.ps[6:8]]
        self.cst = self.sb("cst", [128, CONST.shape[1]])
        self.pad = self.sb("idle_rows", [128, TC, ROW])
        self.base = self.sb("expert_fill", [CH, NCH, E])
        self.h0 = nc.dram_tensor("tokens", (B + 2, L, D), f32, kind="Internal").ap()
        self.xs = nc.dram_tensor("dispatched", (E * CAP + T * (IDLE + 1), ROW), f32, kind="Internal").ap()

    def sb(self, name, shape, dt=f32):
        return self.ctx.enter_context(self.nc.sbuf_tensor(name, shape, dt))

    def sem(self, name):
        return self.ctx.enter_context(self.nc.semaphore(name))

    def c(self, name, p=128):
        a, b = CONST_AT[name]
        return self.cst[0:p, a:b]


def patches(nc, mem, I):
    NG, HALF, WH = 4, G // 2, IMG * CIN // 2
    with ExitStack() as ctx:
        mem.ctx = ctx
        sb, sem, X, Y = mem.sb, mem.sem, mem.X, mem.Y
        xi = [sb(f"pixels{i}", [128, P16, WH]) for i in range(2)]
        wr = sb("w_raw", [128, 2, 5, CIN * D])
        wv = sb("w_class", [128, 2, 2, 3, CIN * D])
        tmp = sb("w_tmp", [128, 4, CIN * D])
        xt = sb("pixels_t", [128, 2, 2, CIN * 128])
        xp = sb("pixels_packed", [128, 2, CIN * P16 * P16])
        os_ = [sb(f"emb{i}", [128, HALF * D]) for i in range(2)]
        bias = sb("tok_bias", [128, D])
        ld_w, ld_c = sem("tok_w_loaded"), sem("const_loaded")
        ld_x = [sem(f"pixels_loaded{i}") for i in range(2)]
        xi_free, w_ready, wstep = sem("pixels_free"), sem("w_class_ready"), sem("w_step")
        tp, ev_a, ev_d, mm, ob = (sem("pix_transposed"), sem("pix_copied_act"), sem("pix_copied_dve"),
                                  sem("emb_done"), sem("emb_copied"))
        packed, xp_free = sem("pix_packed"), sem("packed_free")
        os_free, st = sem("emb_free"), [sem(f"emb_stored{i}") for i in range(2)]
        st_txt = sem("txt_copied")
        NT, U = 3, G
        xr = I["x"].rearrange("b (gy py) w c -> b gy py (w c)", py=P16)
        h0 = mem.h0
        block = ctx.enter_context(nc.Block())

        @block.sync
        def _(sp):
            sp.dma_start(mem.cst[:, :], I["const"]).then_inc(ld_c, 16)
            for hh in range(2):
                for k in range(5):
                    src = I["tok_W"].rearrange("(h p k c) d -> h k p c d", h=2, k=5, c=CIN)[hh, k]
                    sp.dma_start(wr[:, hh, k, :].rearrange("p (c d) -> p c d", c=CIN), src).then_inc(ld_w, 16)
            sp.dma_start(bias[:, :], I["tok_b"].partition_broadcast(128)).then_inc(ld_w, 16)

            def load(half, rows):
                for g, gy in enumerate(rows):
                    sp.dma_start(xi[half][32 * g:32 * g + 32, :, :],
                                 xr[:, gy, :, half * WH:(half + 1) * WH]).then_inc(ld_x[half], 16)

            def store(half, rows):
                for g, gy in enumerate(rows):
                    dst = h0[0:B, bass.ds(gy * G + half * HALF, HALF), :].rearrange("b l d -> b (l d)")
                    sp.dma_start(dst, os_[half][32 * g:32 * g + 32, :]).then_inc(st[half], 16)

            for half in range(2):
                load(half, [1 + g for g in range(NG)])
            sp.dma_start(h0[0:B, NPATCH:L, :], I["txt"]).then_inc(st_txt, 16)
            sp.dma_start(h0[B:B + 2, :, :].rearrange("b l d -> (b l d)"),
                         I["txt"].rearrange("b l d -> (b l d)")[0:2 * L * D]).then_inc(st_txt, 16)
            with sp.Fori(0, NT - 1) as t:
                for half in range(2):
                    sp.wait_ge(xi_free, t * 2 + half + 1)
                    load(half, [t * NG + 5 + g for g in range(NG)])
                for half in range(2):
                    sp.wait_ge(ob, t * U + (half + 1) * HALF)
                    store(half, [t * NG + 1 + g for g in range(NG)])
                    sp.wait_ge(st[half], (t + 1) * NG * 16)
                    sp.sem_inc(os_free, 1)
            edges = [0, G - 1]
            for half in range(2):
                sp.wait_ge(xi_free, 2 * (NT - 1) + half + 1)
                load(half, edges)
            for half in range(2):
                sp.wait_ge(ob, (NT - 1) * U + (half + 1) * HALF)
                store(half, [(NT - 1) * NG + 1 + g for g in range(NG)])
                sp.wait_ge(st[half], NT * NG * 16)
                sp.sem_inc(os_free, 1)
            for half in range(2):
                sp.wait_ge(ob, NT * U + (half + 1) * HALF)
                store(half, edges)
            for half in range(2):
                sp.wait_ge(st[half], (NT * NG + 2) * 16)
            sp.wait_ge(st_txt, 32)

        @block.vector
        def _(dve):
            dve.wait_ge(ld_c, 16)
            dve.wait_ge(ld_w, 16 * 11)
            n = 0

            def step(ins):
                ins.then_inc(wstep, 1)
                dve.wait_ge(wstep, n + 1)
                return n + 1

            add = lambda o, a, b: nc.vector.tensor_tensor(o, a, b, ALU.add)
            mask_add = lambda o, a, m, b: nc.vector.scalar_tensor_tensor(o, a, mem.c(m), b, ALU.mult, ALU.add)
            for hh in range(2):
                w0, w00, w80, w08, w88 = [wr[:, hh, k, :] for k in range(5)]
                for edge in range(2):
                    o = wv[:, hh, edge]
                    if edge:
                        a0, a8 = (w00, w08) if hh == 0 else (w80, w88)
                    else:
                        a0, a8 = tmp[:, 0, :], tmp[:, 1, :]
                        n = step(add(a0, w00, w80))
                        n = step(add(a8, w08, w88))
                    n = step(add(tmp[:, 2, :], w0, a0))
                    n = step(add(tmp[:, 3, :], w0, a8))
                    n = step(add(o[:, 1, :], tmp[:, 2, :], a8))
                    n = step(mask_add(o[:, 0, :], a8, "right_half", tmp[:, 2, :]))
                    n = step(mask_add(o[:, 2, :], a0, "left_half", tmp[:, 3, :]))
            dve.sem_inc(w_ready, 1)

            def tile(base, rows, edge, os_wait):
                def copy_out(u):
                    half, at = u // HALF, u % HALF
                    if at == 0 and os_wait is not None:
                        dve.wait_ge(os_free, os_wait + half)
                    dve.wait_ge(mm, base + u + 1)
                    nc.vector.tensor_tensor(os_[half][0:rows, at * D:(at + 1) * D],
                                            Y[(u // 2) % 2][u % 2][0:rows, 0:D],
                                            bias[0:rows, :], ALU.add).then_inc(ob, 1)
                for u in range(U):
                    dve.wait_ge(tp, base + u + 1)
                    nc.vector.tensor_copy(xt[:, u % 2, 1, :].rearrange("p (c r) -> p c r", c=CIN)[:, :, 0:rows],
                                          X[2 * (u % 2) + 1][:, 0:CIN * 128].rearrange("p (c r) -> p c r", c=CIN)[:, :, 0:rows]
                                          ).then_inc(ev_d, 1)
                    if u:
                        copy_out(u - 1)
                copy_out(U - 1)
            dve.sem_inc(os_free, 2)
            with dve.Fori(0, NT) as t:
                tile(t * U, 128, False, t * 2 + 1)
            tile(NT * U, 64, True, NT * 2 + 1)

        @block.scalar
        def _(act):
            def tile(base, loads, rows):
                def pack(u):
                    half, at = u // HALF, u % HALF
                    if at == 0:
                        act.wait_ge(ld_x[half], loads)
                    act.wait_ge(xp_free, base + u + 1)
                    src = xi[half][0:rows, :, at * 48:(at + 1) * 48].rearrange("p y (x c) -> p c y x", c=CIN)
                    nc.scalar.activation(xp[0:rows, u % 2, :].rearrange("p (c y x) -> p c y x", c=CIN, y=P16),
                                         src, ACT.Copy).then_inc(packed, 1)
                    if at == HALF - 1:
                        act.wait_ge(packed, base + u + 1)
                        act.sem_inc(xi_free, 1)
                pack(0)
                pack(1)
                for u in range(U):
                    act.wait_ge(tp, base + u + 1)
                    nc.scalar.activation(xt[:, u % 2, 0, :].rearrange("p (c r) -> p c r", c=CIN)[:, :, 0:rows],
                                         X[2 * (u % 2)][:, 0:CIN * 128].rearrange("p (c r) -> p c r", c=CIN)[:, :, 0:rows],
                                         ACT.Copy).then_inc(ev_a, 1)
                    if u + 2 < U:
                        pack(u + 2)
            with act.Fori(0, NT) as t:
                tile(t * U, t * (16 * NG) + 16 * NG, 128)
            tile(NT * U, 16 * (NT * NG + 2), 64)

        @block.tensor
        def _(pe):
            pe.wait_ge(ld_c, 16)
            ident = mem.c("ident")

            def transposes(u, base, rows):
                pe.wait_ge(packed, base + u + 1)
                for hh in range(2):
                    for c in range(CIN):
                        src = xp[0:rows, u % 2, (2 * c + hh) * 128:(2 * c + hh + 1) * 128]
                        last = nc.tensor.transpose(X[2 * (u % 2) + hh][:, c * 128:c * 128 + rows], src,
                                                   ident[0:rows, 0:rows])
                last.then_inc(tp, 1)
                pe.wait_ge(tp, base + u + 1)
                pe.sem_inc(xp_free, 1)

            def products(u, base, rows, edge):
                pe.wait_ge(ev_a, base + u + 1)
                pe.wait_ge(ev_d, base + u + 1)
                col = 0 if u == 0 else 2 if u == G - 1 else 1
                bank = Y[(u // 2) % 2][u % 2]
                parts = [(0, 32, (1, 0)), (32, 64, (0, 1))] if edge else [(0, rows, (0, 0))]
                for r0, r1, rowclass in parts:
                    for k in range(2 * CIN):
                        hh, c = k // CIN, k % CIN
                        last = nc.tensor.matmul(bank[r0:r1, 0:D],
                                                xt[:, u % 2, hh, c * 128 + r0:c * 128 + r1],
                                                wv[:, hh, rowclass[hh], col, c * D:(c + 1) * D],
                                                start=(k == 0), stop=(k == 2 * CIN - 1))
                last.then_inc(mm, 1)

            def tile(base, rows, edge):
                transposes(0, base, rows)
                for u in range(U):
                    if u + 1 < U:
                        transposes(u + 1, base, rows)
                    products(u, base, rows, edge)
            pe.sem_inc(xp_free, 2)
            pe.wait_ge(w_ready, 1)
            with pe.Fori(0, NT) as t:
                tile(t * U, 128, False)
            tile(NT * U, 64, True)



def sequences(nc, mem, I, out):
    NP = B // 2
    NQK, NPAR = 2 * D, 4 * H
    NREST = NPAR + 2 * D
    SCALE_MEAN = float(D) ** -0.5
    with ExitStack() as ctx:
        mem.ctx = ctx
        sb, sem, X, Y, c = mem.sb, mem.sem, mem.X, mem.Y, mem.c
        wcomp, wproj = sb("w_comp", [KD, 2, LAT]), sb("w_proj", [KD, 2, D])
        wlat = sb("w_latent", [LAT, NQK + NREST])
        w12, w3 = sb("w_12", [KD, 2, 2, HID]), sb("w_3", [128, HID // 128, D])
        wr = sb("w_router", [KD, 2, E])
        lnw = sb("norm_weights", [KD, 3, 2])
        qkw = sb("qk_norm_w", [CH, 2, DH])
        temp, decay, logd = sb("temperature", [CH, 1]), sb("decay", [CH, H]), sb("log_decay", [CH, H])
        COS, SIN = sb("cos_w", [CH, NCH, 2, DH]), sb("sin_w", [CH, NCH, 2, DH])
        df, idf = sb("decay_to", [CH, NCH, H]), sb("decay_from", [CH, NCH, H])
        mhalf = sb("minus_half", [CH, NCH * 2 * H])
        tokno, base, pad_x = sb("token_number", [CH, 2, NCH]), mem.base, mem.pad
        hh, xln, xn = [sb(n, [CH, 2, NCH, D]) for n in ("h", "x_ln", "x_n")]
        xt = sb("x_t", [KD, 2, 2, L])
        stat, mv = sb("bn", [CH, 2, NCH, 6]), sb("mean_var", [CH, 2, NCH, 2])
        ve2, rs = sb("var_eps", [CH, 2, 2 * NCH]), sb("rstd", [CH, 2, 2 * NCH])
        tl, lat = sb("tanh_latent", [LAT, 2, L]), sb("latent", [LAT, 2, L])
        tg, v, g2 = sb("tanh_rest", [CH, 2, NCH, NPAR + D]), sb("v", [CH, 2, NCH, D]), sb("out_gate", [CH, 2, NCH, D])
        gt = sb("gate_tmp", [CH, 2, 6, NCH * H])
        ve = sb("v_ext", [CH, 2, NCH, H, VE])
        qa, qb, qc = [sb(n, [CH, 2, NCH * NQK]) for n in ("qk", "qk_sq", "qk_rot")]
        ss, rq = sb("qk_ss", [CH, 2, NCH * 2 * H]), sb("qk_rstd", [CH, 2, NCH * 2 * H])
        qf = sb("qk_feat", [CH, 2, NCH * 2 * H, 32])
        qt = sb("qk_feat_t", [128, 2, 2, GR, L])
        states = sb("states", [128, 2, 2 * GR, 4 * VE])
        sm = sb("scores", [CH, 2, 4, GR * CH])
        dn = sb("den", [CH, 2, NCH, H])
        att, sa = sb("att", [CH, 2, NCH, D]), sb("sumsq", [CH, 2, 2, NCH])
        rr = sb("rstd2", [CH, 2, 2, NCH])
        x1, hx, h2 = [sb(n, [CH, 2, NCH, D]) for n in ("x1", "h_plus_x1", "h2")]
        th, hid = sb("tanh_h1", [128, 2, L]), sb("ffn_hidden", [128, 2, HID // 128, L])
        row = sb("rows", [CH, 2, 2, NCH, ROW])
        lg = sb("logits", [CH, 2, NCH, E])
        mx, mi = sb("top_logits", [CH, 2, NCH, 8]), sb("top_experts", [CH, 2, NCH, 8], u32)
        tf, oh = sb("top_f", [CH, 2, NCH, 2]), sb("one_hot", [CH, 2, NCH, 2, E])
        ohs, rk = sb("picked", [CH, 2, NCH, E]), sb("rank", [CH, 2, NCH, E])
        rp, de = sb("rank_picked", [CH, 2, NCH, 2, E]), sb("dest_f", [CH, 2, NCH, 2])
        di = sb("dest", [CH, 2, NCH, 2], i32)
        ew = sb("top_w", [CH, 2, 2, NCH])

        ld, setup, tables, act_tables = sem("weights_loaded"), sem("setup_step"), sem("tables_ready"), sem("act_tables")
        ld_h, st_h, sent = ([sem(f"{n}{b}") for b in range(2)] for n in ("h_loaded", "h2_stored", "rows_sent"))
        st_pad, pad_ready = sem("idle_rows_stored"), sem("idle_rows_ready")
        h_used, h2_free, row_free = sem("h_used"), sem("h2_free"), sem("rows_free")
        var_done, rstd_done, xn_done = sem("var"), sem("rstd_done"), sem("xn_done")
        xn_t, xt_a, xt_d = sem("xn_transposed"), sem("xt_copied_act"), sem("xt_copied_dve")
        lat_mm, lat_th, lat_done = sem("latent_mm"), sem("latent_tanh"), sem("latent_done")
        rest_mm, rest_a, rest_d = sem("rest_mm"), sem("rest_act"), sem("rest_dve")
        qk_mm, qk_sq, qk_cp, qk_ss, qk_rs = sem("qk_mm"), sem("qk_squared"), sem("qk_copied"), sem("qk_sums"), sem("qk_rstds")
        qk_n, qk_cos, qk_rot, qk_exp, qf_done = sem("qk_normed"), sem("qk_times_cos"), sem("qk_rotated"), sem("qk_exp"), sem("qk_features")
        gate_arg, gate_th, gate_w, ve_done = sem("gate_arg"), sem("gate_tanh"), sem("gate_weights"), sem("v_weighted")
        tq_mm, tq_a, tq_d = sem("qk_transposed"), sem("qt_copied"), sem("kt_copied")
        st_mm, st_d, sc_mm, sc_d, pv_mm = sem("state_mm"), sem("state_masked"), sem("score_mm"), sem("score_masked"), sem("pv_mm")
        att_done, att_ss, att_rs = sem("att_done"), sem("att_sumsq"), sem("att_rstd")
        at_t, at_a, at_d, pr_mm, pr_d = sem("att_transposed"), sem("att_t_act"), sem("att_t_dve"), sem("proj_mm"), sem("proj_gated")
        x1_done, x1_ss, x1_rs, xn2_done = sem("x1_done"), sem("x1_sumsq"), sem("x1_rstd"), sem("xn2_done")
        x2_t, x2_a, x2_d = sem("xn2_transposed"), sem("xn2_t_act"), sem("xn2_t_dve")
        f_mm, f_th, f_d, w3_mm, h2_done = sem("ffn_mm"), sem("ffn_tanh"), sem("ffn_hidden_done"), sem("ffn_out_mm"), sem("h2_done")
        var2_done, rstd2_done, flat_done = sem("var2"), sem("rstd2_done"), sem("flat_done")
        fl_t, fl_a, fl_d, lg_mm = sem("flat_transposed"), sem("flat_t_act"), sem("flat_t_dve"), sem("logits_mm")
        top_done, ew_exp, oh_done, rk_mm, dest_done = sem("top_done"), sem("top_exp"), sem("one_hot_done"), sem("rank_mm"), sem("dest_done")
        waited = sem("waits_apart")
        dve_step, pool_step, tok_step, rows_numbered = sem("dve_step"), sem("pool_step"), sem("token_step"), sem("rows_numbered")
        block = ctx.enter_context(nc.Block())

        def apart(eng):
            eng.sem_inc(waited, 1)

        def waiter(eng, i):
            return lambda s, k, per=2: eng.wait_ge(s, i * per + (k + 1))

        @block.sync
        def _(sp):
            def w(dst, src, **how):
                sp.dma_start(dst, src, **how).then_inc(ld, 16)
            w(wcomp[:, :, :], I["attn_w_comp"].rearrange("(k p) n -> p k n", k=2))
            w(wproj[:, :, :], I["attn_w_proj"].rearrange("(k p) n -> p k n", k=2))
            w(wlat[:, 0:NQK], I["attn_w_qkv"][:, 0:NQK])
            w(wlat[:, NQK:NQK + NPAR], I["attn_w_reso"])
            w(wlat[:, NQK + NPAR:NQK + NPAR + D], I["attn_w_outgate"])
            w(wlat[:, NQK + NPAR + D:], I["attn_w_qkv"][:, NQK:])
            w(w12[:, :, 0, :], I["attn_w1"].rearrange("(k p) n -> p k n", k=2))
            w(w12[:, :, 1, :], I["attn_w2"].rearrange("(k p) n -> p k n", k=2))
            w(w3[:, :, :], I["attn_w3"].rearrange("(k p) n -> p k n", p=128))
            for k in range(2):
                w(wr[:, k, :], I["ffn_router_w"].rearrange("e (k p) -> k p e", k=2)[k], allow_slow_non_contiguous=True)
            for j, n in enumerate(("attn_ln_w", "attn_memn_w", "attn_ffn_ln_w")):
                w(lnw[:, j, :], I[n].rearrange("(k p) -> p k", k=2), allow_slow_non_contiguous=True)
            w(qkw[:, 0, :], I["attn_qn_w"].partition_broadcast(CH))
            w(qkw[:, 1, :], I["attn_kn_w"].partition_broadcast(CH))
            w(temp[:, :], I["attn_temperature"].partition_broadcast(CH))
            w(decay[:, :], I["attn_head_decay"].partition_broadcast(CH))

            def load(b, n):
                sp.dma_start(hh[:, b], mem.h0[n].rearrange("(c p) d -> p c d", c=NCH)).then_inc(ld_h[b], 16)
            load(0, 0)
            load(1, 1)
            sp.wait_ge(pad_ready, 1)
            for k in range(IDLE + 1):
                sp.dma_start(mem.xs[E * CAP + k * T:E * CAP + (k + 1) * T, :].rearrange("(c p) d -> p c d", c=TC),
                             pad_x[:, :, :]).then_inc(st_pad, 16)
            sp.dma_start(out[NTOK:NTOK + T, :].rearrange("(c p) d -> p c d", c=TC), pad_x[:, :, 0:D]).then_inc(st_pad, 16)
            with sp.Fori(0, NP) as i:
                wait = waiter(sp, i)
                for b in range(2):
                    wait(h_used, b)
                    sp.dma_start(hh[:, b], mem.h0[bass.ds(i * 2 + (b + 2), 1), :, :].rearrange(
                        "o (c p) d -> p (o c) d", c=NCH)).then_inc(ld_h[b], 16)
                for b in range(2):
                    wait(h2_done, b)
                    sp.dma_start(out[bass.ds(i * (2 * L) + b * L, L), :].rearrange("(c p) d -> p c d", c=NCH),
                                 h2[:, b]).then_inc(st_h[b], 16)
                for b in range(2):
                    sp.wait_ge(st_h[b], i * 16 + 16)
                    sp.sem_inc(h2_free, 1)
            for b in range(2):
                sp.wait_ge(ld_h[b], 16 * (NP + 1))
                sp.wait_ge(st_h[b], 16 * NP)
            sp.wait_ge(st_pad, 16 * (IDLE + 2))

        @block.vector
        def _(dve):
            V = nc.vector
            n = [0]

            def s(ins):
                ins.then_inc(setup, 1)
                n[0] += 1
                dve.wait_ge(setup, n[0])
            s(V.memset(pad_x[:, :, :], 0.0))
            V.tensor_copy(pad_x[:, :, D], c("padid")).then_inc(pad_ready, 1)
            s(V.memset(mhalf[:, :], -0.5))
            s(V.memset(qf[:, :, :, :], 0.0))
            for b in range(2):
                s(V.tensor_scalar(tokno[:, b, :], c("tokno", CH), float(b * L - 2 * L), None, ALU.add))
            s(V.tensor_copy(base[:, :, :].rearrange("p c e -> p (c e)"), c("base", CH)))
            dve.wait_ge(ld, 16 * 18)
            for k in range(2):
                s(V.tensor_scalar(wcomp[:, k, :], wcomp[:, k, :], lnw[:, 0, k:k + 1], None, ALU.mult))
                s(V.tensor_scalar(wproj[:, k, :], wproj[:, k, :], lnw[:, 1, k:k + 1], None, ALU.mult))
                for j in range(2):
                    s(V.tensor_scalar(w12[:, k, j, :], w12[:, k, j, :], lnw[:, 2, k:k + 1], None, ALU.mult))
            s(V.tensor_scalar(wproj[:, :, :], wproj[:, :, :], 0.5, None, ALU.mult))
            s(V.tensor_scalar(wlat[:, :], wlat[:, :], 0.5, None, ALU.mult))
            s(V.tensor_scalar(w3[:, :, :], w3[:, :, :], 0.5, None, ALU.mult))
            s(V.tensor_scalar(temp[:, :], temp[:, :], 0.125, None, ALU.mult))
            cosc, sinc = [c(k, CH).rearrange("p (c d) -> p c d", c=NCH) for k in ("cos", "sin")]
            for k in range(2):
                wb = qkw[:, k, :].unsqueeze(1).to_broadcast([CH, NCH, DH])
                s(V.tensor_tensor(COS[:, :, k, :], cosc, wb, ALU.mult))
                for half in range(2):
                    o = slice(half * 8, half * 8 + 8)
                    wp = qkw[:, k, 8 - half * 8:16 - half * 8].unsqueeze(1).to_broadcast([CH, NCH, 8])
                    s(V.tensor_tensor(SIN[:, :, k, o], sinc[:, :, o], wp, ALU.mult))
            dve.wait_ge(act_tables, 1)
            s(V.tensor_scalar(decay[:, :], decay[:, :], 0.325, 0.625, ALU.mult, ALU.add))
            s(V.tensor_scalar(decay[:, :], decay[:, :], 1e-5, 0.999, ALU.max, ALU.min))
            dve.sem_inc(tables, 1)
            dve.wait_ge(act_tables, 2 + NCH)
            s(V.tensor_scalar(idf[:, :, :], df[:, :, :], 1e-8, None, ALU.add))
            s(V.reciprocal(idf[:, :, :], idf[:, :, :]))
            s(V.tensor_scalar(decay[:, :], decay[:, :], -1.0, 1.0, ALU.mult, ALU.add))
            s(V.tensor_tensor(idf[:, :, :], idf[:, :, :], decay[:, :].unsqueeze(1).to_broadcast([CH, NCH, H]), ALU.mult))
            for b in range(2):
                s(V.tensor_copy(ve[:, b, :, :, DH], idf[:, :, :]))
            dve.sem_inc(tables, 1)

            LINKS = 76
            with dve.Fori(0, NP) as i:
                wait = waiter(dve, i)
                k = [0]

                def link(ins):
                    ins.then_inc(dve_step, 1)
                    k[0] += 1
                    dve.wait_ge(dve_step, i * LINKS + k[0])

                def layer_stats(src, b):
                    for q in range(NCH):
                        last = V.bn_stats(stat[:, b, q, :], src[:, b, q, :])
                    link(last)
                    apart(dve)
                    for q in range(NCH):
                        last = V.bn_aggr(mv[:, b, q, :], stat[:, b, q, :])
                    link(last)

                for b in range(2):
                    dve.wait_ge(ld_h[b], i * 16 + 16)
                    layer_stats(hh, b)
                    V.tensor_scalar(ve2[:, b, 0:NCH], mv[:, b, :, 1], 1e-5, None, ALU.add)
                    V.tensor_scalar(ve2[:, b, NCH:], mv[:, b, :, 1], 1.0 + 1e-6, 1e-11, ALU.mult, ALU.add).then_inc(var_done, 1)
                for b in range(2):
                    wait(rstd_done, b)
                    for q in range(NCH):
                        for j, dst in ((0, xln), (1, xn)):
                            last = V.tensor_scalar(dst[:, b, q, :], hh[:, b, q, :], mv[:, b, q, 0:1],
                                                   rs[:, b, j * NCH + q:j * NCH + q + 1], ALU.subtract, ALU.mult)
                    last.then_inc(xn_done, 1)
                for b in range(2):
                    wait(xn_t, b)
                    V.tensor_copy(xt[:, b, 1, :], Y[b][1][0:KD, 0:L]).then_inc(xt_d, 1)
                for b in range(2):
                    wait(lat_th, b)
                    V.scalar_tensor_tensor(lat[:, b, :], tl[:, b, :], 1.0, X[b][:, 0:L], ALU.add, ALU.mult).then_inc(lat_done, 1)
                for u in range(6):
                    b, q = u // 3, u % 3
                    wait(rest_a, u, 6)
                    bank = (Y[b][0], Y[b][1], X[2 + b])[q]
                    V.scalar_tensor_tensor(g2[:, b, q, :], tg[:, b, q, NPAR:], 1.0, bank[0:CH, NPAR:NPAR + D],
                                           ALU.add, ALU.mult).then_inc(rest_d, 1)
                for u in range(6):
                    b, q = u // 3, u % 3
                    wait(qk_mm, u, 6)
                    V.tensor_copy(qa[:, b, q * NQK:(q + 1) * NQK], X[u % 4][0:CH, 0:NQK]).then_inc(qk_cp, 1)
                for b in range(2):
                    wait(qk_sq, 3 * b + 2, 6)
                    link(V.tensor_reduce(ss[:, b, :], qb[:, b, :].rearrange("p (h d) -> p h d", d=DH), AX.X, ALU.add))
                    V.tensor_scalar(ss[:, b, :], ss[:, b, :], 1.0 / DH, 1e-6, ALU.mult, ALU.add).then_inc(qk_ss, 1)
                for b in range(2):
                    par = tg[:, b, :, 0:NPAR].rearrange("p c (h j) -> p c h j", j=4)
                    g = [gt[:, b, j, :] for j in range(6)]
                    g3 = lambda a: a.rearrange("p (c h) -> p c h", c=NCH)
                    link(V.tensor_tensor(g3(g[0]), par[:, :, :, 1], par[:, :, :, 3], ALU.subtract))
                    V.tensor_scalar(g3(g[3]), par[:, :, :, 2], 1.0, None, ALU.add)
                    link(V.tensor_tensor(g[1], g[0], g[0], ALU.mult))
                    V.scalar_tensor_tensor(g3(g[3]), par[:, :, :, 0], 1.0, g3(g[3]), ALU.add, ALU.mult)
                    link(V.tensor_scalar(g[2], g[1], COS_POLY[7], None, ALU.mult))
                    for p in range(6, 0, -1):
                        link(V.scalar_tensor_tensor(g[2], g[2], COS_POLY[p], g[1], ALU.add, ALU.mult))
                    V.scalar_tensor_tensor(g[2], g[2], COS_POLY[0], g[3], ALU.add, ALU.mult).then_inc(gate_arg, 1)
                for b in range(2):
                    wait(qk_rs, b)
                    hd = lambda t: t[:, b, :].rearrange("p (h d) -> p h d", d=DH)
                    V.tensor_tensor(hd(qa), hd(qa), rq[:, b, :].unsqueeze(2).to_broadcast([CH, NCH * 2 * H, DH]),
                                    ALU.mult).then_inc(qk_n, 1)
                for b in range(2):
                    wait(qk_n, b)
                    for q in range(NCH):
                        for half in range(2):
                            a, o = [t[:, b, q * NQK:(q + 1) * NQK].rearrange("p (k h d) -> p k h d", k=2, d=DH) for t in (qa, qb)]
                            o1, o2 = slice(half * 8, half * 8 + 8), slice(8 - half * 8, 16 - half * 8)
                            last = V.tensor_tensor(o[:, :, :, o1], a[:, :, :, o2],
                                                   SIN[:, q, :, o1].unsqueeze(2).to_broadcast([CH, 2, H, 8]), ALU.mult)
                    link(last)
                    wait(qk_cos, b)
                    V.tensor_tensor(qc[:, b, :], qc[:, b, :], qb[:, b, :], ALU.add).then_inc(qk_rot, 1)
                for b in range(2):
                    wait(gate_th, b)
                    link(V.tensor_scalar(gt[:, b, 4, :], gt[:, b, 4, :], 0.6, 0.5, ALU.mult, ALU.add))
                    link(V.tensor_scalar(gt[:, b, 4, :], gt[:, b, 4, :], 0.05, 0.95, ALU.max, ALU.min))
                    V.tensor_tensor(gt[:, b, 5, :], gt[:, b, 4, :], idf[:, :, :].rearrange("p c h -> p (c h)"),
                                    ALU.mult).then_inc(gate_w, 1)
                for b in range(2):
                    wait(qk_exp, b)
                    hd = lambda t: t[:, b, :].rearrange("p (h d) -> p h d", d=DH)
                    V.scalar_tensor_tensor(qf[:, b, :, 0:DH], hd(qb), 1.0, hd(qa), ALU.min, ALU.add).then_inc(qf_done, 1)
                for j in range(6):
                    q, b = j // 2, j % 2
                    wait(tq_mm, j, 6)
                    V.tensor_copy(qt[:, b, 1, :, q * CH:(q + 1) * CH],
                                  Y[b][1][:, 0:GR * CH].rearrange("p (g t) -> p g t", g=GR)).then_inc(tq_d, 1)
                for b in range(2):
                    wait(st_mm, b)
                    V.tensor_tensor(states[:, b], X[b][:, 0:2 * GR * 4 * VE].rearrange("p (s n) -> p s n", s=2 * GR),
                                    c("headblock").unsqueeze(1).to_broadcast([128, 2 * GR, 4 * VE]), ALU.mult).then_inc(st_d, 1)
                for j in range(6):
                    for r in range(4):
                        wait(sc_mm, 4 * j + r, 24)
                        V.tensor_tensor(sm[:, j % 2, r, :].rearrange("p (g t) -> p g t", g=GR),
                                        X[r][0:CH, 0:GR * CH].rearrange("p (g t) -> p g t", g=GR),
                                        c("causal", CH).unsqueeze(1).to_broadcast([CH, GR, CH]), ALU.mult).then_inc(sc_d, 1)
                for b in range(2):
                    wait(pv_mm, b)
                    o0 = Y[b][0][0:CH, 0:2 * H * VE].rearrange("p (c h e) -> p c h e", c=2, e=VE)
                    o1 = Y[b][1][0:CH, 0:H * VE].rearrange("p (h e) -> p h e", e=VE)
                    V.tensor_tensor(dn[:, b, 0:2, :], o0[:, :, :, DH], df[:, 0:2, :], ALU.mult)
                    link(V.tensor_tensor(dn[:, b, 2, :], o1[:, :, DH], df[:, 2, :], ALU.mult))
                    link(V.tensor_scalar(dn[:, b], dn[:, b], 1e-5, None, ALU.max))
                    link(V.reciprocal(dn[:, b], dn[:, b]))
                    link(V.tensor_tensor(dn[:, b], dn[:, b], df[:, :, :], ALU.mult))
                    a4 = att[:, b].rearrange("p c (h d) -> p c h d", d=DH)
                    V.tensor_tensor(a4[:, 0:2], o0[:, :, :, 0:DH], dn[:, b, 0:2, :].unsqueeze(3).to_broadcast([CH, 2, H, DH]), ALU.mult)
                    V.tensor_tensor(a4[:, 2], o1[:, :, 0:DH], dn[:, b, 2, :].unsqueeze(2).to_broadcast([CH, H, DH]),
                                    ALU.mult).then_inc(att_done, 1)
                for b in range(2):
                    wait(at_t, b)
                    V.tensor_copy(xt[:, b, 1, :], X[2 * b + 1][0:KD, 0:L]).then_inc(at_d, 1)
                for b in range(2):
                    wait(att_rs, b)
                    wait(pr_mm, b)
                    for q in range(NCH):
                        bank = Y[b][q // 2][0:CH, (q % 2) * D:(q % 2 + 1) * D]
                        last = V.scalar_tensor_tensor(x1[:, b, q, :], bank, rr[:, b, 0, q:q + 1], g2[:, b, q, :], ALU.mult, ALU.mult)
                    last.then_inc(pr_d, 1)
                for b in range(2):
                    wait(x1_rs, b)
                    for q in range(NCH):
                        last = V.tensor_scalar(xn[:, b, q, :], x1[:, b, q, :], rr[:, b, 1, q:q + 1], None, ALU.mult)
                    last.then_inc(xn2_done, 1)
                for b in range(2):
                    wait(x2_t, b)
                    V.tensor_copy(xt[:, b, 1, :], X[2 * b + 1][0:KD, 0:L]).then_inc(x2_d, 1)
                for u in range(8):
                    b, m = u // 4, u % 4
                    wait(f_th, u, 8)
                    link(V.scalar_tensor_tensor(hid[:, b, m, :], th[:, u % 2, :], 1.0, X[2 * (u % 2)][:, 0:L], ALU.add, ALU.mult))
                    V.tensor_tensor(hid[:, b, m, :], hid[:, b, m, :], X[2 * (u % 2) + 1][:, 0:L], ALU.mult).then_inc(f_d, 1)
                for b in range(2):
                    wait(h2_free, b)
                    wait(h_used, b)
                    wait(w3_mm, b)
                    V.tensor_tensor(h2[:, b, 0:2, :], hx[:, b, 0:2, :], Y[b][0][0:CH, 0:2 * D].rearrange("p (c d) -> p c d", c=2), ALU.add)
                    V.tensor_tensor(h2[:, b, 2, :], hx[:, b, 2, :], Y[b][1][0:CH, 0:D], ALU.add).then_inc(h2_done, 1)
                for b in range(2):
                    wait(h2_done, b)
                    layer_stats(h2, b)
                    V.tensor_scalar(ve2[:, b, 0:NCH], mv[:, b, :, 1], 1e-5, None, ALU.add).then_inc(var2_done, 1)
                for b in range(2):
                    wait(rstd2_done, b)
                    wait(row_free, b)
                    for q in range(NCH):
                        last = V.tensor_scalar(row[:, b, 0, q, 0:D], h2[:, b, q, :], mv[:, b, q, 0:1], rs[:, b, q:q + 1],
                                               ALU.subtract, ALU.mult)
                    last.then_inc(flat_done, 1)
                for b in range(2):
                    wait(fl_t, b)
                    V.tensor_copy(xt[:, b, 1, :], X[2 * b + 1][0:KD, 0:L]).then_inc(fl_d, 1)
                for b in range(2):
                    wait(lg_mm, b)
                    link(V.tensor_copy(lg[:, b], Y[b][0][0:CH, 0:NCH * E].rearrange("p (c e) -> p c e", c=NCH)))
                    apart(dve)
                    for q in range(NCH):
                        last = V.max(mx[:, b, q, :], lg[:, b, q, :])
                    link(last)
                    apart(dve)
                    for q in range(NCH):
                        last = V.max_index(mi[:, b, q, :], mx[:, b, q, :], lg[:, b, q, :])
                    link(last)
                    V.tensor_tensor(ew[:, b, 0, :], mx[:, b, :, 1], mx[:, b, :, 0], ALU.subtract).then_inc(top_done, 1)
                    link(V.tensor_copy(tf[:, b], mi[:, b, :, 0:2]))
                    link(V.tensor_tensor(oh[:, b], c("expert", CH).unsqueeze(1).unsqueeze(1).to_broadcast([CH, NCH, 2, E]),
                                         tf[:, b].unsqueeze(3).to_broadcast([CH, NCH, 2, E]), ALU.is_equal))
                    V.tensor_tensor(ohs[:, b], oh[:, b, :, 0, :], oh[:, b, :, 1, :], ALU.add).then_inc(oh_done, 1)
                for b in range(2):
                    wait(rk_mm, b)
                    before = Y[b][1][0:CH, 0:NCH * E].rearrange("p (c e) -> p c e", c=NCH)
                    total = Y[b][1][0:CH, 32:32 + NCH * E].rearrange("p (c e) -> p c e", c=NCH)
                    link(V.tensor_tensor(base[:, 1, :], base[:, 0, :], total[:, 0, :], ALU.add))
                    link(V.tensor_tensor(base[:, 2, :], base[:, 1, :], total[:, 1, :], ALU.add))
                    link(V.tensor_tensor(rk[:, b], before, base[:, :, :], ALU.add))
                    link(V.tensor_tensor(base[:, 0, :], base[:, 2, :], total[:, 2, :], ALU.add))
                    link(V.tensor_tensor(rp[:, b], oh[:, b], rk[:, b].unsqueeze(2).to_broadcast([CH, NCH, 2, E]), ALU.mult))
                    link(V.tensor_reduce(de[:, b], rp[:, b], AX.X, ALU.add))
                    V.tensor_copy(di[:, b], de[:, b])
                    wait(ew_exp, b)
                    link(V.tensor_scalar(ew[:, b, 0, :], ew[:, b, 1, :], 1.0, None, ALU.add))
                    link(V.reciprocal(row[:, b, 0, :, D + 1], ew[:, b, 0, :]))
                    V.tensor_tensor(row[:, b, 1, :, D + 1], ew[:, b, 1, :], row[:, b, 0, :, D + 1], ALU.mult).then_inc(dest_done, 1)
                assert k[0] == LINKS, k[0]

        @block.scalar
        def _(act):
            A = nc.scalar.activation
            act.wait_ge(ld, 16 * 18)
            A(decay[:, :], decay[:, :], ACT.Tanh, scale=0.5).then_inc(act_tables, 1)
            act.wait_ge(tables, 1)
            A(logd[:, :], decay[:, :], ACT.Ln).then_inc(act_tables, 1)
            act.wait_ge(act_tables, 2)
            for q in range(NCH):
                A(df[:, q, :], logd[:, :], ACT.Exp, scale=c("pos1", CH)[:, q:q + 1]).then_inc(act_tables, 1)

            with act.Fori(0, NP) as i:
                wait = waiter(act, i)
                for b in range(2):
                    wait(xn_t, b)
                    A(xt[:, b, 0, :], Y[b][0][0:KD, 0:L], ACT.Copy).then_inc(xt_a, 1)
                for b in range(2):
                    wait(lat_mm, b)
                    A(tl[:, b, :], X[b][:, 0:L], ACT.Tanh, scale=0.5).then_inc(lat_th, 1)
                for u in range(6):
                    b, q = u // 3, u % 3
                    wait(rest_mm, u, 6)
                    bank = (Y[b][0], Y[b][1], X[2 + b])[q]
                    A(tg[:, b, q, :], bank[0:CH, 0:NPAR + D], ACT.Tanh, scale=0.5)
                    A(v[:, b, q, :], bank[0:CH, NPAR + D:NREST], ACT.Copy).then_inc(rest_a, 1)
                for u in range(6):
                    b, q = u // 3, u % 3
                    wait(qk_cp, u, 6)
                    A(qb[:, b, q * NQK:(q + 1) * NQK], qa[:, b, q * NQK:(q + 1) * NQK], ACT.Square).then_inc(qk_sq, 1)
                for b in range(2):
                    wait(gate_arg, b)
                    A(gt[:, b, 4, :], gt[:, b, 2, :], ACT.Tanh, scale=temp[:, :]).then_inc(gate_th, 1)
                for b in range(2):
                    wait(qk_rot, b)
                    A(qb[:, b, :], qc[:, b, :], ACT.Exp)
                    A(qa[:, b, :], qc[:, b, :], ACT.Relu).then_inc(qk_exp, 1)
                for j in range(6):
                    q, b = j // 2, j % 2
                    wait(tq_mm, j, 6)
                    A(qt[:, b, 0, :, q * CH:(q + 1) * CH],
                      Y[b][0][:, 0:GR * CH].rearrange("p (g t) -> p g t", g=GR), ACT.Copy).then_inc(tq_a, 1)
                for b in range(2):
                    wait(at_t, b)
                    A(xt[:, b, 0, :], X[2 * b][0:KD, 0:L], ACT.Copy).then_inc(at_a, 1)
                for b in range(2):
                    wait(att_done, b)
                    for q in range(NCH):
                        last = A(qc[:, b, q * D:(q + 1) * D], att[:, b, q, :], ACT.Square, scale=SCALE_MEAN, accum_out=sa[:, b, 0, q:q + 1])
                    last.then_inc(att_ss, 1)
                for b in range(2):
                    wait(x1_done, b)
                    for q in range(NCH):
                        last = A(qc[:, b, (NCH + q) * D:(NCH + q + 1) * D], x1[:, b, q, :], ACT.Square, scale=SCALE_MEAN, accum_out=sa[:, b, 1, q:q + 1])
                    last.then_inc(x1_ss, 1)
                for b in range(2):
                    wait(x2_t, b)
                    A(xt[:, b, 0, :], X[2 * b][0:KD, 0:L], ACT.Copy).then_inc(x2_a, 1)
                for u in range(8):
                    wait(f_mm, u, 8)
                    A(th[:, u % 2, :], X[2 * (u % 2)][:, 0:L], ACT.Tanh, scale=0.5).then_inc(f_th, 1)
                for b in range(2):
                    wait(fl_t, b)
                    A(xt[:, b, 0, :], X[2 * b][0:KD, 0:L], ACT.Copy).then_inc(fl_a, 1)
                for b in range(2):
                    wait(top_done, b)
                    A(ew[:, b, 1, :], ew[:, b, 0, :], ACT.Exp).then_inc(ew_exp, 1)

        @block.gpsimd
        def _(pool):
            PO = nc.gpsimd
            pool.sem_inc(row_free, 2)
            pool.sem_inc(h2_free, 2)
            pool.wait_ge(tables, 2)
            LINKS = 2 * 2
            with pool.Fori(0, NP) as i:
                wait = waiter(pool, i)
                k = [0]

                def link(ins):
                    ins.then_inc(pool_step, 1)
                    k[0] += 1
                    pool.wait_ge(pool_step, i * LINKS + k[0])
                for b in range(2):
                    wait(var_done, b)
                    PO.tensor_tensor(rs[:, b, :], ve2[:, b, :], mhalf[:, 0:2 * NCH], ALU.pow).then_inc(rstd_done, 1)
                for b in range(2):
                    wait(qk_ss, b)
                    PO.tensor_tensor(rq[:, b, :], ss[:, b, :], mhalf[:, :], ALU.pow).then_inc(qk_rs, 1)
                for b in range(2):
                    wait(qk_n, b)
                    for q in range(NCH):
                        a, o = [t[:, b, q * NQK:(q + 1) * NQK].rearrange("p (k h d) -> p k h d", k=2, d=DH) for t in (qa, qc)]
                        last = PO.tensor_tensor(o, a, COS[:, q, :, :].unsqueeze(2).to_broadcast([CH, 2, H, DH]), ALU.mult)
                    last.then_inc(qk_cos, 1)
                for b in range(2):
                    wait(gate_w, b)
                    wait(rest_a, 3 * b + 2, 6)
                    PO.tensor_tensor(ve[:, b, :, :, 0:DH], v[:, b].rearrange("p c (h d) -> p c h d", d=DH),
                                     gt[:, b, 5, :].rearrange("p (c h) -> p c h", c=NCH).unsqueeze(3).to_broadcast([CH, NCH, H, DH]),
                                     ALU.mult).then_inc(ve_done, 1)
                for b in range(2):
                    wait(att_ss, b)
                    apart(pool)
                    link(PO.tensor_scalar(sa[:, b, 0, :], sa[:, b, 0, :], 1e-6, None, ALU.add))
                    PO.tensor_tensor(rr[:, b, 0, :], sa[:, b, 0, :], mhalf[:, 0:NCH], ALU.pow).then_inc(att_rs, 1)
                for b in range(2):
                    wait(pr_d, b)
                    PO.tensor_tensor(x1[:, b], x1[:, b], xln[:, b], ALU.add).then_inc(x1_done, 1)
                for b in range(2):
                    wait(x1_done, b)
                    PO.tensor_tensor(hx[:, b], hh[:, b], x1[:, b], ALU.add).then_inc(h_used, 1)
                    wait(x1_ss, b)
                    apart(pool)
                    link(PO.tensor_scalar(sa[:, b, 1, :], sa[:, b, 1, :], 1e-6, None, ALU.add))
                    PO.tensor_tensor(rr[:, b, 1, :], sa[:, b, 1, :], mhalf[:, 0:NCH], ALU.pow).then_inc(x1_rs, 1)
                for b in range(2):
                    wait(var2_done, b)
                    PO.tensor_tensor(rs[:, b, 0:NCH], ve2[:, b, 0:NCH], mhalf[:, 0:NCH], ALU.pow).then_inc(rstd2_done, 1)
                for b in range(2):
                    wait(flat_done, b)
                    apart(pool)
                    PO.tensor_copy(row[:, b, 1, :, 0:D], row[:, b, 0, :, 0:D])
                    PO.tensor_scalar(tokno[:, b, :], tokno[:, b, :], float(2 * L), None, ALU.add).then_inc(tok_step, 1)
                    wait(tok_step, b)
                    apart(pool)
                    for j in range(2):
                        last = PO.tensor_copy(row[:, b, j, :, D], tokno[:, b, :])
                    last.then_inc(rows_numbered, 1)
                for b in range(2):
                    wait(dest_done, b)
                    wait(rows_numbered, b)
                    apart(pool)
                    for q in range(NCH):
                        for j in range(2):
                            PO.indirect_dma_start(out=mem.xs, out_offset=bass.IndirectOffsetOnAxis(ap=di[:, b, q, j:j + 1], axis=0),
                                                  in_=row[:, b, j, q, :], in_offset=None).then_inc(sent[b], 16)
                for b in range(2):
                    pool.wait_ge(sent[b], i * (16 * 2 * NCH) + 16 * 2 * NCH)
                    pool.sem_inc(row_free, 1)

        @block.tensor
        def _(pe):
            MM, TR = nc.tensor.matmul, nc.tensor.transpose
            ident = c("ident", CH)[:, 0:CH]
            pe.wait_ge(tables, 2)
            with pe.Fori(0, NP) as i:
                wait = waiter(pe, i)

                def transpose_rows(src, banks, done):
                    for kk in range(2):
                        for q in range(NCH):
                            last = TR(banks[kk][0:KD, q * CH:(q + 1) * CH], src(q)[:, kk * KD:(kk + 1) * KD], ident)
                    last.then_inc(done, 1)

                for b in range(2):
                    wait(xn_done, b)
                    transpose_rows(lambda q: xn[:, b, q, :], Y[b], xn_t)
                for b in range(2):
                    wait(xt_a, b)
                    wait(xt_d, b)
                    for kk in range(2):
                        last = MM(X[b][:, 0:L], wcomp[:, kk, :], xt[:, b, kk, :], start=(kk == 0), stop=(kk == 1))
                    last.then_inc(lat_mm, 1)
                for b in range(2):
                    wait(lat_done, b)
                    for q in range(NCH):
                        bank = (Y[b][0], Y[b][1], X[2 + b])[q]
                        MM(bank[0:CH, 0:NREST], lat[:, b, q * CH:(q + 1) * CH], wlat[:, NQK:], start=True, stop=True).then_inc(rest_mm, 1)
                for u in range(6):
                    b, q = u // 3, u % 3
                    if u in (2, 3):
                        wait(rest_a, 3 * (u - 2) + 2, 6)
                        wait(rest_d, 3 * (u - 2) + 2, 6)
                    if u >= 4:
                        wait(qk_cp, u - 4, 6)
                    MM(X[u % 4][0:CH, 0:NQK], lat[:, b, q * CH:(q + 1) * CH], wlat[:, 0:NQK], start=True, stop=True).then_inc(qk_mm, 1)
                for j in range(6):
                    q, b = j // 2, j % 2
                    if q == 0:
                        wait(qf_done, b)
                    else:
                        wait(tq_a, j - 2, 6)
                        wait(tq_d, j - 2, 6)
                    for kk in range(2):
                        for g in range(GR):
                            h0 = (q * 2 + kk) * H + 4 * g
                            last = TR(Y[b][kk][:, g * CH:(g + 1) * CH],
                                      qf[:, b, h0:h0 + 4, :].rearrange("p h d -> p (h d)"), ident)
                    last.then_inc(tq_mm, 1)
                for b in range(2):
                    wait(ve_done, b)
                    for s_ in range(2):
                        for g in range(GR):
                            for q in range(s_ + 1):
                                h0 = (q * 2 + 1) * H + 4 * g
                                last = MM(X[b][:, (s_ * GR + g) * 4 * VE:(s_ * GR + g + 1) * 4 * VE],
                                          qf[:, b, h0:h0 + 4, :].rearrange("p h d -> p (h d)"),
                                          ve[:, b, q, 4 * g:4 * g + 4, :].rearrange("p h e -> p (h e)"),
                                          start=(q == 0), stop=(q == s_))
                    last.then_inc(st_mm, 1)

                def scores(j):
                    q, b = j // 2, j % 2
                    if j == 0:
                        wait(tq_a, 5, 6)
                        wait(tq_d, 5, 6)
                    tok = slice(q * CH, (q + 1) * CH)
                    for r in range(4):
                        if j == 0 and r < 2:
                            wait(st_d, r)
                        if j:
                            wait(sc_d, 4 * (j - 1) + r, 24)
                        for g in range(GR):
                            last = MM(X[r][0:CH, g * CH:(g + 1) * CH], qt[32 * r:32 * r + DH, b, 1, g, tok],
                                      qt[32 * r:32 * r + DH, b, 0, g, tok], start=True, stop=True)
                        last.then_inc(sc_mm, 1)

                def values(j):
                    q, b = j // 2, j % 2
                    wait(sc_d, 4 * j + 3, 24)
                    bank, o = Y[b][q // 2], (q % 2) * H * VE
                    for g in range(GR):
                        if q:
                            MM(bank[0:CH, o + g * 4 * VE:o + (g + 1) * 4 * VE], qt[:, b, 0, g, q * CH:(q + 1) * CH],
                               states[:, b, (q - 1) * GR + g, :], start=True, stop=False)
                        for r in range(4):
                            h = 4 * g + r
                            last = MM(bank[0:CH, o + h * VE:o + (h + 1) * VE], sm[:, j % 2, r, g * CH:(g + 1) * CH],
                                      ve[:, b, q, h, :], start=(q == 0), stop=(q == 0 or r == 3))
                    if q == NCH - 1:
                        last.then_inc(pv_mm, 1)
                scores(0)
                for j in range(6):
                    if j < 5:
                        scores(j + 1)
                    values(j)
                for b in range(2):
                    wait(att_done, b)
                    transpose_rows(lambda q: att[:, b, q, :], X[2 * b:2 * b + 2], at_t)

                def rows_out(w, ks, src, done, b):
                    for q in range(NCH):
                        for kk in range(ks):
                            last = MM(Y[b][q // 2][0:CH, (q % 2) * D:(q % 2 + 1) * D], src[:, b, kk, q * CH:(q + 1) * CH],
                                      w[:, kk, :], start=(kk == 0), stop=(kk == ks - 1))
                    last.then_inc(done, 1)
                for b in range(2):
                    wait(at_a, b)
                    wait(at_d, b)
                    rows_out(wproj, 2, xt, pr_mm, b)
                for b in range(2):
                    wait(xn2_done, b)
                    transpose_rows(lambda q: xn[:, b, q, :], X[2 * b:2 * b + 2], x2_t)
                for u in range(8):
                    b, m = u // 4, u % 4
                    if u < 2:
                        wait(x2_a, u)
                        wait(x2_d, u)
                    else:
                        wait(f_d, u - 2, 8)
                    for j in range(2):
                        for kk in range(2):
                            last = MM(X[2 * (u % 2) + j][:, 0:L], w12[:, kk, j, m * 128:(m + 1) * 128], xt[:, b, kk, :],
                                      start=(kk == 0), stop=(kk == 1))
                    last.then_inc(f_mm, 1)
                for b in range(2):
                    wait(f_d, 4 * b + 3, 8)
                    rows_out(w3, HID // 128, hid, w3_mm, b)
                for b in range(2):
                    wait(flat_done, b)
                    transpose_rows(lambda q: row[:, b, 0, q, :], X[2 * b:2 * b + 2], fl_t)
                for b in range(2):
                    wait(fl_a, b)
                    wait(fl_d, b)
                    for q in range(NCH):
                        for kk in range(2):
                            last = MM(Y[b][0][0:CH, q * E:(q + 1) * E], xt[:, b, kk, q * CH:(q + 1) * CH], wr[:, kk, :],
                                      start=(kk == 0), stop=(kk == 1))
                    last.then_inc(lg_mm, 1)
                for b in range(2):
                    wait(oh_done, b)
                    src = ohs[:, b].rearrange("p c e -> p (c e)")
                    MM(Y[b][1][0:CH, 0:NCH * E], c("before", CH), src, start=True, stop=True)
                    MM(Y[b][1][0:CH, 32:32 + NCH * E], c("ones", CH), src, start=True, stop=True).then_inc(rk_mm, 1)


def experts(nc, mem, I, out):
    NM = F // 128
    NPAIR, LAST = NTASK // 2, NTASK % 2
    assert LAST == 1
    with ExitStack() as ctx:
        mem.ctx = ctx
        sb, sem, X, Y, c = mem.sb, mem.sem, mem.X, mem.Y, mem.c
        xr = sb("task_rows", [128, 2, TC, ROW])
        w1, w2 = sb("task_w1", [KD, 2, 2, F]), sb("task_w2", [128, 2, NM, D])
        b1, b2 = sb("task_b1", [128, 2, NM]), sb("task_b2", [128, 2, D])
        xt = sb("task_x_t", [KD, 2, 2, T])
        hid = sb("task_hidden", [128, 2, NM, T])
        wt, ids = sb("task_weight", [128, 2, TC]), sb("task_ids", [128, 2, TC], i32)
        ys = sb("task_out", [128, 2, TC, D])
        cnt, tiles, cum = sb("count", [1, E]), sb("tiles", [1, E]), sb("tiles_upto", [1, E])
        cmp_, mix = sb("over_steps", [1, E, RSTEPS]), sb("mix", [1, E, E])
        ind, indt = sb("expert_past", [1, NTASK, E]), sb("expert_past_tiles", [1, NTASK, E])
        ej, bef, off = sb("task_expert_f", [1, NTASK]), sb("task_before", [1, NTASK]), sb("task_row_f", [1, NTASK])
        table, tail = sb("task_table", [1, 2, NTASK], i32), sb("tail_row", [1, E], i32)
        step, table_ready, tails = sem("table_step"), sem("table_ready"), sem("tails_stored")
        ld_x, ld_w = ([sem(f"{n}{p}") for p in range(2)] for n in ("task_rows_loaded", "task_weights_loaded"))
        x_free, w1_free, w2_free, y_free = sem("task_rows_free"), sem("w1_free"), sem("w2_free"), sem("task_out_free")
        tr, xt_a, xt_d = sem("task_transposed"), sem("task_xt_act"), sem("task_xt_dve")
        l1, gelu, l2, y_add, y_done = sem("up_mm"), sem("gelu_done"), sem("down_mm"), sem("bias_added"), sem("task_out_done")
        waited = sem("task_waits_apart")
        added = [sem(f"out_added{p}") for p in range(2)]
        block = ctx.enter_context(nc.Block())
        UP = [X[2], X[3], Y[0][0], Y[0][1]]
        DOWN = Y[1]

        @block.sync
        def _(sp):
            sp.wait_ge(table_ready, 1)
            for e in range(E):
                r = sp.value_load(tail[0:1, e:e + 1], min_val=0, max_val=E * CAP - T)
                sp.dma_start(mem.xs[bass.ds(r, T), :].rearrange("(c p) d -> p c d", c=TC), mem.pad[:, :, :]).then_inc(tails, 16)
            sp.wait_ge(tails, 16 * E)

            def load(j, p):
                row0 = sp.value_load(table[0:1, 0, bass.ds(j, 1)], min_val=0, max_val=E * CAP + IDLE * T)
                e = sp.value_load(table[0:1, 1, bass.ds(j, 1)], min_val=0, max_val=E - 1)
                sp.wait_ge(x_free, j + 1)
                sp.dma_start(xr[:, p], mem.xs[bass.ds(row0, T), :].rearrange("(c p) d -> p c d", c=TC)).then_inc(ld_x[p], 16)
                sp.wait_ge(w1_free, j + 1)
                sp.dma_start(w1[:, p], I["ffn_w1"][bass.ds(e, 1), :, :].rearrange("o (k p) n -> p (o k) n", k=2)).then_inc(ld_w[p], 16)
                sp.wait_ge(w2_free, j + 1)
                sp.dma_start(b1[:, p], I["ffn_b1"][bass.ds(e, 1), :].rearrange("o (p m) -> p (o m)", m=NM)).then_inc(ld_w[p], 16)
                sp.dma_start(w2[:, p], I["ffn_w2"][bass.ds(e, 1), :, :].rearrange("o (p m) n -> p (o m) n", m=NM)).then_inc(ld_w[p], 16)
                sp.dma_start(b2[:, p, :], I["ffn_b2"][bass.ds(e, 1), :].rearrange("o n -> (o n)").partition_broadcast(128)).then_inc(ld_w[p], 16)
            with sp.Fori(0, NPAIR) as i:
                for p in range(2):
                    load(i * 2 + p, p)
            load(NTASK - 1, 0)

        @block.vector
        def _(dve):
            V = nc.vector
            n = [0]

            def s(ins):
                ins.then_inc(step, 1)
                n[0] += 1
                dve.wait_ge(step, n[0])
            first = lambda name, m=None: c(name, 1)[:, 0:m]
            s(V.tensor_tensor(cnt[:, :], mem.base[0:1, 0, :], first("base", E), ALU.subtract))
            s(V.tensor_copy(tail[:, :], mem.base[0:1, 0, :]))
            s(V.tensor_tensor(cmp_[:, :, :], cnt[:, :].unsqueeze(2).to_broadcast([1, E, RSTEPS]),
                              first("steps", RSTEPS).unsqueeze(1).to_broadcast([1, E, RSTEPS]), ALU.is_gt))
            s(V.tensor_reduce(tiles[:, :], cmp_[:, :, :], AX.X, ALU.add))
            s(V.tensor_tensor(mix[:, :, :], tiles[:, :].unsqueeze(1).to_broadcast([1, E, E]),
                              first("upto", E * E).rearrange("o (a b) -> o a b", a=E), ALU.mult))
            s(V.tensor_reduce(cum[:, :], mix[:, :, :], AX.X, ALU.add))
            task = first("task", NTASK)
            s(V.tensor_tensor(ind[:, :, :], cum[:, :].unsqueeze(1).to_broadcast([1, NTASK, E]),
                              task.unsqueeze(2).to_broadcast([1, NTASK, E]), ALU.is_le))
            s(V.tensor_reduce(ej[:, :], ind[:, :, :], AX.X, ALU.add))
            s(V.tensor_tensor(indt[:, :, :], ind[:, :, :], tiles[:, :].unsqueeze(1).to_broadcast([1, NTASK, E]), ALU.mult))
            s(V.tensor_reduce(bef[:, :], indt[:, :, :], AX.X, ALU.add))
            s(V.tensor_tensor(bef[:, :], task, bef[:, :], ALU.subtract))
            s(V.tensor_scalar(bef[:, :], bef[:, :], float(T), None, ALU.mult))
            s(V.scalar_tensor_tensor(off[:, :], ej[:, :], float(CAP), bef[:, :], ALU.mult, ALU.add))
            s(V.tensor_copy(table[:, 0, :], off[:, :]))
            s(V.tensor_scalar(ej[:, :], ej[:, :], float(E - 1), None, ALU.min))
            s(V.tensor_copy(table[:, 1, :], ej[:, :]))
            dve.sem_inc(table_ready, 1)

            def rows_in(j, p):
                dve.wait_ge(tr, j + 1)
                V.tensor_copy(xt[:, p, 1, :], X[1][0:KD, 0:T]).then_inc(xt_d, 1)
                V.tensor_copy(wt[:, p, :], xr[:, p, :, D + 1])
                dve.wait_ge(y_free, j + 1)
                V.tensor_copy(ids[:, p, :], xr[:, p, :, D]).then_inc(x_free, 1)

            def rows_out(j, p):
                for q in range(TC):
                    dve.wait_ge(l2, j * TC + q + 1)
                    V.tensor_tensor(ys[:, p, q, :], DOWN[q % 2][:, 0:D], b2[:, p, :], ALU.add).then_inc(y_add, 1)
                    dve.wait_ge(y_add, j * TC + q + 1)
                    V.tensor_scalar(ys[:, p, q, :], ys[:, p, q, :], wt[:, p, q:q + 1], None, ALU.mult).then_inc(y_done, 1)
                dve.wait_ge(y_done, j * TC + TC)
            rows_in(0, 0)
            with dve.Fori(0, NPAIR) as i:
                for p in range(2):
                    rows_in(i * 2 + (p + 1), 1 - p)
                    rows_out(i * 2 + p, p)
            rows_out(NTASK - 1, 0)

        @block.scalar
        def _(act):
            def rows_in(j, p):
                act.wait_ge(tr, j + 1)
                nc.scalar.activation(xt[:, p, 0, :], X[0][0:KD, 0:T], ACT.Copy).then_inc(xt_a, 1)

            def up(j, p, loads):
                act.wait_ge(ld_w[p], loads)
                for m in range(NM):
                    act.wait_ge(l1, j * NM + m + 1)
                    nc.scalar.activation(hid[:, p, m, :], UP[m % 4][:, 0:T], ACT.Gelu, bias=b1[:, p, m:m + 1]).then_inc(gelu, 1)
            rows_in(0, 0)
            with act.Fori(0, NPAIR) as i:
                for p in range(2):
                    up(i * 2 + p, p, i * 64 + 64)
                    rows_in(i * 2 + (p + 1), 1 - p)
            up(NTASK - 1, 0, (NPAIR + 1) * 64)

        @block.gpsimd
        def _(pool):
            pool.sem_inc(x_free, 2)
            pool.sem_inc(w1_free, 2)
            pool.sem_inc(w2_free, 2)
            pool.sem_inc(y_free, 2)

            def add(j, p, sent):
                for q in range(TC):
                    pool.wait_ge(y_done, j * TC + q + 1)
                    pool.sem_inc(waited, 1)
                    nc.gpsimd.indirect_dma_start(out=out, out_offset=bass.IndirectOffsetOnAxis(ap=ids[:, p, q:q + 1], axis=0),
                                                 in_=ys[:, p, q, :], in_offset=None, compute_op=ALU.add).then_inc(added[p], 16)
                pool.wait_ge(added[p], sent)
                pool.sem_inc(y_free, 1)
            with pool.Fori(0, NPAIR) as i:
                for p in range(2):
                    add(i * 2 + p, p, i * (16 * TC) + 16 * TC)
            add(NTASK - 1, 0, (NPAIR + 1) * 16 * TC)

        @block.tensor
        def _(pe):
            MM, TR = nc.tensor.matmul, nc.tensor.transpose
            ident = c("ident")

            def rows_in(p, loads):
                pe.wait_ge(ld_x[p], loads)
                for kk in range(2):
                    for q in range(TC):
                        last = TR(X[kk][0:KD, q * 128:(q + 1) * 128], xr[:, p, q, kk * KD:(kk + 1) * KD], ident)
                last.then_inc(tr, 1)

            def up(j, p, loads):
                pe.wait_ge(xt_a, j + 1)
                pe.wait_ge(xt_d, j + 1)
                pe.wait_ge(ld_w[p], loads)
                for m in range(NM):
                    if m >= 4:
                        pe.wait_ge(gelu, j * NM + (m - 3))
                    for kk in range(2):
                        last = MM(UP[m % 4][:, 0:T], w1[:, p, kk, m::NM], xt[:, p, kk, :], start=(kk == 0), stop=(kk == 1))
                    last.then_inc(l1, 1)
                pe.wait_ge(l1, j * NM + NM)
                pe.sem_inc(w1_free, 1)

            def down(j, p):
                pe.wait_ge(gelu, j * NM + NM)
                for q in range(TC):
                    if q >= 2:
                        pe.wait_ge(y_add, j * TC + (q - 1))
                    for m in range(NM):
                        last = MM(DOWN[q % 2][:, 0:D], hid[:, p, m, q * 128:(q + 1) * 128], w2[:, p, m, :],
                                  start=(m == 0), stop=(m == NM - 1))
                    last.then_inc(l2, 1)
                pe.wait_ge(y_add, j * TC + TC)
                pe.sem_inc(w2_free, 1)
            rows_in(0, 16)
            with pe.Fori(0, NPAIR) as i:
                for p in range(2):
                    up(i * 2 + p, p, i * 64 + 64)
                    rows_in(1 - p, i * 16 + 16 * (p + 1))
                    down(i * 2 + p, p)
            up(NTASK - 1, 0, (NPAIR + 1) * 64)
            down(NTASK - 1, 0)


def program(nc, I, out):
    with ExitStack() as ctx:
        mem = Memory(nc, ctx)
        patches(nc, mem, I)
        sequences(nc, mem, I, out)
        experts(nc, mem, I, out)


_INS = {"x": "x", "txt": "txt"}
_INS |= {"L0_" + n: n for n in ["tok_W", "tok_b"] + ["attn_" + n for n in (
    "ln_w", "w_comp", "w_qkv", "w_reso", "qn_w", "kn_w", "w_outgate", "head_decay", "temperature", "w_proj", "memn_w",
    "ffn_ln_w", "w1", "w2", "w3")] + ["ffn_" + n for n in ("router_w", "w1", "b1", "w2", "b2")]}


def kernel(**inputs):
    import numpy as _np
    import concourse.bacc as _bacc
    from concourse import mybir as _mybir
    from concourse.bass_utils import run_bass_kernel_spmd as _run

    nc = _bacc.Bacc("TRN2", target_bir_lowering=False, num_devices=1)
    arrays = {f"in_{short}": _np.ascontiguousarray(inputs[name]) for name, short in _INS.items()}
    arrays["in_const"] = CONST
    aps = {k[3:]: nc.dram_tensor(k, a.shape, _mybir.dt.from_np(a.dtype), kind="ExternalInput").ap() for k, a in arrays.items()}
    out = nc.dram_tensor("out", (NTOK + T, D), _mybir.dt.float32, kind="ExternalOutput").ap()
    program(nc, aps, out)
    r = _run(nc, [arrays], core_ids=[0])
    return r.results[0]["out"][:NTOK].reshape(B, L, D)
```

```python
import concourse.bass as bass
from concourse import mybir
from contextlib import ExitStack
import numpy as np

B, IMG, P16, CIN, D = 32, 224, 16, 3, 192
G = IMG // P16
NPATCH, NTXT = G * G, 77
L = NPATCH + NTXT
CH = 91
NCH = L // CH
H, DH = 12, 16
GR = 3
KD = 96
LAT, HID = 128, 512
E, F = 8, 768
NTOK = B * L
T = 384
TC = T // 128
CAP = NTOK + T
NTASK = (2 * NTOK + E * (T - 1)) // T
IDLE = NTASK - (2 * NTOK + T - 1) // T
ROW = D + 2
VE = DH + 1
RSTEPS = (NTOK + T - 1) // T
assert L == CH * NCH and H == 4 * GR and D == 2 * KD and 128 % P16 == 0

f32, i32, u32 = mybir.dt.float32, mybir.dt.int32, mybir.dt.uint32
ALU, ACT, AX = mybir.AluOpType, mybir.ActivationFunctionType, mybir.AxisListType

_nodes = 2 + 2 * np.cos(np.pi * (np.arange(400) + 0.5) / 400)
COS_POLY = [float(c) for c in np.polynomial.chebyshev.Chebyshev.fit(
    _nodes, np.cos(np.pi / 2 * np.sqrt(_nodes)), 7, domain=[0, 4]).convert(kind=np.polynomial.Polynomial).coef]


def constants():
    parts = {}
    s, t = np.arange(CH)[:, None], np.arange(CH)[None, :]
    parts["ident"] = np.eye(128)
    parts["causal"] = (s <= t)
    parts["before"] = (s < t)
    parts["ones"] = np.ones((CH, CH))
    slot = np.arange(128)[:, None] // 32
    parts["headblock"] = slot == (np.arange(4 * VE)[None, :] // VE)
    inv = 1.0 / 10000.0 ** (np.arange(0, DH, 2, dtype=np.float32) / np.float32(DH))
    pos = np.arange(L, dtype=np.float32)
    ang = np.outer(pos, inv.astype(np.float32)).astype(np.float32)
    cos, sin = np.cos(ang), np.sin(ang)
    tok = lambda a: a.reshape(NCH, CH, -1).transpose(1, 0, 2).reshape(CH, -1)
    parts["cos"] = tok(np.concatenate([cos, cos], 1))
    parts["sin"] = tok(np.concatenate([-sin, sin], 1))
    parts["pos1"] = tok((pos + 1)[:, None])
    parts["tokno"] = tok(pos[:, None])
    px = np.arange(128) % P16
    parts["right_half"] = (px >= P16 // 2)[:, None]
    parts["left_half"] = (px < P16 // 2)[:, None]
    parts["expert"] = np.tile(np.arange(E), (128, 1))
    parts["base"] = np.tile(np.arange(E) * CAP, (128, NCH))
    parts["steps"] = np.tile(np.arange(RSTEPS) * T, (1, 1))
    parts["upto"] = np.tril(np.ones((E, E))).reshape(1, -1)
    parts["task"] = np.arange(NTASK)[None, :]
    parts["padid"] = NTOK + np.arange(128)[:, None] + 128 * np.arange(TC)[None, :]
    at, cols = {}, []
    n = 0
    for k, a in parts.items():
        a = np.asarray(a, np.float32)
        full = np.zeros((128, a.shape[1]), np.float32)
        full[:a.shape[0]] = a
        at[k] = (n, n + a.shape[1])
        n += a.shape[1]
        cols.append(full)
    return np.concatenate(cols, 1), at


CONST, CONST_AT = constants()


class Memory:

    def __init__(self, nc, ctx):
        self.nc, self.ctx = nc, ctx
        self.psum = ctx.enter_context(nc.psum_tensor("psum", [128, 8, 512], f32))
        self.ps = [self.psum[:, k, :] for k in range(8)]
        self.X, self.Y = self.ps[:4], [self.ps[4:6], self.ps[6:8]]
        self.cst = self.sb("cst", [128, CONST.shape[1]])
        self.pad = self.sb("idle_rows", [128, TC, ROW])
        self.base = self.sb("expert_fill", [CH, NCH, E])
        self.h0 = nc.dram_tensor("tokens", (B + 2, L, D), f32, kind="Internal").ap()
        self.xs = nc.dram_tensor("dispatched", (E * CAP + T * (IDLE + 1), ROW), f32, kind="Internal").ap()

    def sb(self, name, shape, dt=f32):
        return self.ctx.enter_context(self.nc.sbuf_tensor(name, shape, dt))

    def sem(self, name):
        return self.ctx.enter_context(self.nc.semaphore(name))

    def c(self, name, p=128):
        a, b = CONST_AT[name]
        return self.cst[0:p, a:b]


def patches(nc, mem, I):
    NG, HALF, WH = 4, G // 2, IMG * CIN // 2
    with ExitStack() as ctx:
        mem.ctx = ctx
        sb, sem, X, Y = mem.sb, mem.sem, mem.X, mem.Y
        xi = [sb(f"pixels{i}", [128, P16, WH]) for i in range(2)]
        wr = sb("w_raw", [128, 2, 5, CIN * D])
        wv = sb("w_class", [128, 2, 2, 3, CIN * D])
        tmp = sb("w_tmp", [128, 4, CIN * D])
        xt = sb("pixels_t", [128, 2, 2, CIN * 128])
        xp = sb("pixels_packed", [128, 2, CIN * P16 * P16])
        os_ = [sb(f"emb{i}", [128, HALF * D]) for i in range(2)]
        bias = sb("tok_bias", [128, D])
        ld_w, ld_c = sem("tok_w_loaded"), sem("const_loaded")
        ld_x = [sem(f"pixels_loaded{i}") for i in range(2)]
        xi_free, w_ready, wstep = sem("pixels_free"), sem("w_class_ready"), sem("w_step")
        tp, ev_a, ev_d, mm, ob = (sem("pix_transposed"), sem("pix_copied_act"), sem("pix_copied_dve"),
                                  sem("emb_done"), sem("emb_copied"))
        packed, xp_free = sem("pix_packed"), sem("packed_free")
        os_free, st = sem("emb_free"), [sem(f"emb_stored{i}") for i in range(2)]
        st_txt = sem("txt_copied")
        NT, U = 3, G
        xr = I["x"].rearrange("b (gy py) w c -> b gy py (w c)", py=P16)
        h0 = mem.h0
        block = ctx.enter_context(nc.Block())

        @block.sync
        def _(sp):
            sp.dma_start(mem.cst[:, :], I["const"]).then_inc(ld_c, 16)
            for hh in range(2):
                for k in range(5):
                    src = I["tok_W"].rearrange("(h p k c) d -> h k p c d", h=2, k=5, c=CIN)[hh, k]
                    sp.dma_start(wr[:, hh, k, :].rearrange("p (c d) -> p c d", c=CIN), src).then_inc(ld_w, 16)
            sp.dma_start(bias[:, :], I["tok_b"].partition_broadcast(128)).then_inc(ld_w, 16)

            def load(half, rows):
                for g, gy in enumerate(rows):
                    sp.dma_start(xi[half][32 * g:32 * g + 32, :, :],
                                 xr[:, gy, :, half * WH:(half + 1) * WH]).then_inc(ld_x[half], 16)

            def store(half, rows):
                for g, gy in enumerate(rows):
                    dst = h0[0:B, bass.ds(gy * G + half * HALF, HALF), :].rearrange("b l d -> b (l d)")
                    sp.dma_start(dst, os_[half][32 * g:32 * g + 32, :]).then_inc(st[half], 16)

            for half in range(2):
                load(half, [1 + g for g in range(NG)])
            sp.dma_start(h0[0:B, NPATCH:L, :], I["txt"]).then_inc(st_txt, 16)
            sp.dma_start(h0[B:B + 2, :, :].rearrange("b l d -> (b l d)"),
                         I["txt"].rearrange("b l d -> (b l d)")[0:2 * L * D]).then_inc(st_txt, 16)
            with sp.Fori(0, NT - 1) as t:
                for half in range(2):
                    sp.wait_ge(xi_free, t * 2 + half + 1)
                    load(half, [t * NG + 5 + g for g in range(NG)])
                for half in range(2):
                    sp.wait_ge(ob, t * U + (half + 1) * HALF)
                    store(half, [t * NG + 1 + g for g in range(NG)])
                    sp.wait_ge(st[half], (t + 1) * NG * 16)
                    sp.sem_inc(os_free, 1)
            edges = [0, G - 1]
            for half in range(2):
                sp.wait_ge(xi_free, 2 * (NT - 1) + half + 1)
                load(half, edges)
            for half in range(2):
                sp.wait_ge(ob, (NT - 1) * U + (half + 1) * HALF)
                store(half, [(NT - 1) * NG + 1 + g for g in range(NG)])
                sp.wait_ge(st[half], NT * NG * 16)
                sp.sem_inc(os_free, 1)
            for half in range(2):
                sp.wait_ge(ob, NT * U + (half + 1) * HALF)
                store(half, edges)
            for half in range(2):
                sp.wait_ge(st[half], (NT * NG + 2) * 16)
            sp.wait_ge(st_txt, 32)

        @block.vector
        def _(dve):
            dve.wait_ge(ld_c, 16)
            dve.wait_ge(ld_w, 16 * 11)
            n = 0

            def step(ins):
                ins.then_inc(wstep, 1)
                dve.wait_ge(wstep, n + 1)
                return n + 1

            add = lambda o, a, b: nc.vector.tensor_tensor(o, a, b, ALU.add)
            mask_add = lambda o, a, m, b: nc.vector.scalar_tensor_tensor(o, a, mem.c(m), b, ALU.mult, ALU.add)
            for hh in range(2):
                w0, w00, w80, w08, w88 = [wr[:, hh, k, :] for k in range(5)]
                for edge in range(2):
                    o = wv[:, hh, edge]
                    if edge:
                        a0, a8 = (w00, w08) if hh == 0 else (w80, w88)
                    else:
                        a0, a8 = tmp[:, 0, :], tmp[:, 1, :]
                        n = step(add(a0, w00, w80))
                        n = step(add(a8, w08, w88))
                    n = step(add(tmp[:, 2, :], w0, a0))
                    n = step(add(tmp[:, 3, :], w0, a8))
                    n = step(add(o[:, 1, :], tmp[:, 2, :], a8))
                    n = step(mask_add(o[:, 0, :], a8, "right_half", tmp[:, 2, :]))
                    n = step(mask_add(o[:, 2, :], a0, "left_half", tmp[:, 3, :]))
            dve.sem_inc(w_ready, 1)

            def tile(base, rows, edge, os_wait):
                def copy_out(u):
                    half, at = u // HALF, u % HALF
                    if at == 0 and os_wait is not None:
                        dve.wait_ge(os_free, os_wait + half)
                    dve.wait_ge(mm, base + u + 1)
                    nc.vector.tensor_tensor(os_[half][0:rows, at * D:(at + 1) * D],
                                            Y[(u // 2) % 2][u % 2][0:rows, 0:D],
                                            bias[0:rows, :], ALU.add).then_inc(ob, 1)
                for u in range(U):
                    dve.wait_ge(tp, base + u + 1)
                    nc.vector.tensor_copy(xt[:, u % 2, 1, :].rearrange("p (c r) -> p c r", c=CIN)[:, :, 0:rows],
                                          X[2 * (u % 2) + 1][:, 0:CIN * 128].rearrange("p (c r) -> p c r", c=CIN)[:, :, 0:rows]
                                          ).then_inc(ev_d, 1)
                    if u:
                        copy_out(u - 1)
                copy_out(U - 1)
            dve.sem_inc(os_free, 2)
            with dve.Fori(0, NT) as t:
                tile(t * U, 128, False, t * 2 + 1)
            tile(NT * U, 64, True, NT * 2 + 1)

        @block.scalar
        def _(act):
            def tile(base, loads, rows):
                def pack(u):
                    half, at = u // HALF, u % HALF
                    if at == 0:
                        act.wait_ge(ld_x[half], loads)
                    act.wait_ge(xp_free, base + u + 1)
                    src = xi[half][0:rows, :, at * 48:(at + 1) * 48].rearrange("p y (x c) -> p c y x", c=CIN)
                    nc.scalar.activation(xp[0:rows, u % 2, :].rearrange("p (c y x) -> p c y x", c=CIN, y=P16),
                                         src, ACT.Copy).then_inc(packed, 1)
                    if at == HALF - 1:
                        act.wait_ge(packed, base + u + 1)
                        act.sem_inc(xi_free, 1)
                pack(0)
                pack(1)
                for u in range(U):
                    act.wait_ge(tp, base + u + 1)
                    nc.scalar.activation(xt[:, u % 2, 0, :].rearrange("p (c r) -> p c r", c=CIN)[:, :, 0:rows],
                                         X[2 * (u % 2)][:, 0:CIN * 128].rearrange("p (c r) -> p c r", c=CIN)[:, :, 0:rows],
                                         ACT.Copy).then_inc(ev_a, 1)
                    if u + 2 < U:
                        pack(u + 2)
            with act.Fori(0, NT) as t:
                tile(t * U, t * (16 * NG) + 16 * NG, 128)
            tile(NT * U, 16 * (NT * NG + 2), 64)

        @block.tensor
        def _(pe):
            pe.wait_ge(ld_c, 16)
            ident = mem.c("ident")

            def transposes(u, base, rows):
                pe.wait_ge(packed, base + u + 1)
                for hh in range(2):
                    for c in range(CIN):
                        src = xp[0:rows, u % 2, (2 * c + hh) * 128:(2 * c + hh + 1) * 128]
                        last = nc.tensor.transpose(X[2 * (u % 2) + hh][:, c * 128:c * 128 + rows], src,
                                                   ident[0:rows, 0:rows])
                last.then_inc(tp, 1)
                pe.wait_ge(tp, base + u + 1)
                pe.sem_inc(xp_free, 1)

            def products(u, base, rows, edge):
                pe.wait_ge(ev_a, base + u + 1)
                pe.wait_ge(ev_d, base + u + 1)
                col = 0 if u == 0 else 2 if u == G - 1 else 1
                bank = Y[(u // 2) % 2][u % 2]
                parts = [(0, 32, (1, 0)), (32, 64, (0, 1))] if edge else [(0, rows, (0, 0))]
                for r0, r1, rowclass in parts:
                    for k in range(2 * CIN):
                        hh, c = k // CIN, k % CIN
                        last = nc.tensor.matmul(bank[r0:r1, 0:D],
                                                xt[:, u % 2, hh, c * 128 + r0:c * 128 + r1],
                                                wv[:, hh, rowclass[hh], col, c * D:(c + 1) * D],
                                                start=(k == 0), stop=(k == 2 * CIN - 1))
                last.then_inc(mm, 1)

            def tile(base, rows, edge):
                transposes(0, base, rows)
                for u in range(U):
                    if u + 1 < U:
                        transposes(u + 1, base, rows)
                    products(u, base, rows, edge)
            pe.sem_inc(xp_free, 2)
            pe.wait_ge(w_ready, 1)
            with pe.Fori(0, NT) as t:
                tile(t * U, 128, False)
            tile(NT * U, 64, True)



def sequences(nc, mem, I, out):
    NP = B // 2
    NQK, NPAR = 2 * D, 4 * H
    NREST = NPAR + 2 * D
    SCALE_MEAN = float(D) ** -0.5
    CW = 96
    LP = L + CW - CH
    SC, REST, QK, FB = (0, 1, 4, 5), (4, 5, 6), (7, 4, 5), (0, 6, 4, 0)
    with ExitStack() as ctx:
        mem.ctx = ctx
        sb, sem, X, Y, c = mem.sb, mem.sem, mem.X, mem.Y, mem.c
        wcomp, wproj = sb("w_comp", [KD, 2, LAT]), sb("w_proj", [KD, 2, D])
        wlat = sb("w_latent", [LAT, NQK + NREST])
        w12, w3 = sb("w_12", [KD, 2, 2, HID]), sb("w_3", [128, HID // 128, D])
        wr = sb("w_router", [KD, 2, E])
        lnw = sb("norm_weights", [KD, 3, 2])
        qkw = sb("qk_norm_w", [CH, 2, DH])
        temp, decay, logd = sb("temperature", [CH, 1]), sb("decay", [CH, H]), sb("log_decay", [CH, H])
        COS, SIN = sb("cos_w", [CH, NCH, 2, DH]), sb("sin_w", [CH, NCH, 2, DH])
        df, idf = sb("decay_to", [CH, NCH, H]), sb("decay_from", [CH, NCH, H])
        mhalf = sb("minus_half", [CH, NCH * 2 * H])
        tokno, base, pad_x = sb("token_number", [CH, NCH]), mem.base, mem.pad
        hh, xln, att, g2, h2 = [sb(n, [CH, 2, NCH, D]) for n in ("h", "x_ln", "att", "out_gate", "h2")]
        xn, xn2, v, x1, hx = [sb(n, [CH, NCH, D]) for n in ("x_n", "x_n2", "v", "x1", "h_plus_x1")]
        xt, xb = sb("x_t", [KD, 2, L]), sb("back_t", [KD, 2, L])
        stat, mv = sb("bn", [CH, 2, NCH, 6]), sb("mean_var", [CH, 2, NCH, 2])
        ve2, rs = sb("var_eps", [CH, 2, 2 * NCH]), sb("rstd", [CH, 2, 2 * NCH])
        tl, lat = sb("tanh_latent", [LAT, L]), sb("latent", [LAT, L])
        tg = sb("tanh_rest", [CH, NCH, NPAR + D])
        gt = sb("gate_tmp", [CH, 6, NCH * H])
        ve = sb("v_ext", [CH, NCH, H, 32])
        qa, qb, qc = [sb(n, [CH, NCH * NQK]) for n in ("qk", "qk_sq", "qk_rot")]
        ss, rq, nt = sb("qk_ss", [CH, NCH * 2 * H]), sb("qk_rstd", [CH, NCH * 2 * H]), sb("newton", [CH, NCH * 2 * H])
        qf = sb("qk_feat", [CH, NCH * 2 * H, 32])
        qt = sb("qk_feat_t", [128, 2, GR, LP])
        states = sb("states", [128, 2, GR, 4, 32])
        sm = sb("scores", [CH, 2, 4, GR * CH])
        ot = sb("att_sum_t", [128, NCH, GR * CH])
        dn, limit = sb("den", [CH, NCH, H]), sb("den_limit", [CH, NCH, H])
        sa, sae, rr = sb("sumsq", [CH, 2, NCH]), sb("meansq_eps", [CH, 2, NCH]), sb("rstd2", [CH, 2, NCH])
        junk = sb("squares", [CH, 2, NCH, D])
        th, hid = sb("tanh_h1", [128, HID // 128, L]), sb("ffn_hidden", [128, HID // 128, L])
        row = sb("rows", [CH, 2, 2, NCH, ROW])
        lg = sb("logits", [CH, NCH, E])
        mx, mi = sb("top_logits", [CH, NCH, 8]), sb("top_experts", [CH, NCH, 8], u32)
        tf, oh = sb("top_f", [CH, NCH, 2]), sb("one_hot", [CH, NCH, 2, E])
        ohs, rk = sb("picked", [CH, NCH, E]), sb("rank", [CH, NCH, E])
        rp, de = sb("rank_picked", [CH, NCH, 2, E]), sb("dest_f", [CH, NCH, 2])
        di = sb("dest", [CH, 2, NCH, 2], i32)
        ew = sb("top_w", [CH, 2, NCH])

        ld, setup, tables, act_tables = sem("weights_loaded"), sem("setup_step"), sem("tables_ready"), sem("act_tables")
        ld_h, st_h, sent = ([sem(f"{n}{b}") for b in range(2)] for n in ("h_loaded", "h2_stored", "rows_sent"))
        st_pad, pad_ready = sem("idle_rows_stored"), sem("idle_rows_ready")
        h_used, h2_free, row_free = sem("h_used"), sem("h2_free"), sem("rows_free")
        var_done, rstd_done, xn_done = sem("var"), sem("rstd_done"), sem("xn_done")
        xn_t, xt_done = sem("xn_transposed"), sem("xt_copied")
        lat_mm, lat_th, lat_done = sem("latent_mm"), sem("latent_tanh"), sem("latent_done")
        rest_mm, rest_a, rest_d = sem("rest_mm"), sem("rest_act"), sem("rest_dve")
        qk_mm, qk_sq = sem("qk_mm"), sem("qk_squared")
        qk_n, qk_cos, qk_rot, qk_exp, qf_done = sem("qk_normed"), sem("qk_times_cos"), sem("qk_rotated"), sem("qk_exp"), sem("qk_features")
        gate_arg, gate_th, gate_w, ve_done = sem("gate_arg"), sem("gate_tanh"), sem("gate_weights"), sem("v_weighted")
        tq_mm, tq_a = sem("qk_transposed"), sem("qkt_copied")
        st_mm, st_d, sc_mm, sc_d, pv_mm = sem("state_mm"), sem("state_masked"), sem("score_mm"), sem("score_masked"), sem("pv_mm")
        ot_a, ot_mm = sem("att_sum_copied"), sem("att_sum_transposed")
        att_done, att_ss, att_rs = sem("att_done"), sem("att_sumsq"), sem("att_rstd")
        at_t, at_a, pr_mm, pr_d = sem("att_transposed"), sem("att_t_copied"), sem("proj_mm"), sem("proj_gated")
        x1_done, x1_ss, x1_rs, xn2_done = sem("x1_done"), sem("x1_sumsq"), sem("x1_rstd"), sem("xn2_done")
        x2_t, x2_a = sem("xn2_transposed"), sem("xn2_t_copied")
        f_mm, f_th, f_d, w3_mm, h2_done = sem("ffn_mm"), sem("ffn_tanh"), sem("ffn_hidden_done"), sem("ffn_out_mm"), sem("h2_done")
        var2_done, rstd2_done, flat_done = sem("var2"), sem("rstd2_done"), sem("flat_done")
        fl_t, fl_a, lg_mm = sem("flat_transposed"), sem("flat_t_copied"), sem("logits_mm")
        top_done, ew_exp, oh_done, rk_mm, rk_read, dest_done = (sem("top_done"), sem("top_exp"), sem("one_hot_done"), sem("rank_mm"),
                                                                sem("rank_read"), sem("dest_done"))
        waited = sem("waits_apart")
        ln_step, front_step, back_step = sem("norm_step"), sem("front_step"), sem("back_step")
        row_copied = sem("row_copied")
        att_step, x1_step, tok_step, rows_numbered = sem("att_var_step"), sem("x1_var_step"), sem("token_step"), sem("rows_numbered")
        block = ctx.enter_context(nc.Block())
        bank = mem.ps
        two = lambda k, n: mem.psum[0:KD, k:k + 2, 0:n]

        def apart(eng):
            eng.sem_inc(waited, 1)

        def waiter(eng, n):
            return lambda s, k=0, per=1: eng.wait_ge(s, n * per + (k + 1))

        @block.sync
        def _(sp):
            def w(dst, src, **how):
                sp.dma_start(dst, src, **how).then_inc(ld, 16)
            w(wcomp[:, :, :], I["attn_w_comp"].rearrange("(k p) n -> p k n", k=2))
            w(wproj[:, :, :], I["attn_w_proj"].rearrange("(k p) n -> p k n", k=2))
            w(wlat[:, 0:NQK], I["attn_w_qkv"][:, 0:NQK])
            w(wlat[:, NQK:NQK + NPAR], I["attn_w_reso"])
            w(wlat[:, NQK + NPAR:NQK + NPAR + D], I["attn_w_outgate"])
            w(wlat[:, NQK + NPAR + D:], I["attn_w_qkv"][:, NQK:])
            w(w12[:, :, 0, :], I["attn_w1"].rearrange("(k p) n -> p k n", k=2))
            w(w12[:, :, 1, :], I["attn_w2"].rearrange("(k p) n -> p k n", k=2))
            w(w3[:, :, :], I["attn_w3"].rearrange("(k p) n -> p k n", p=128))
            for k in range(2):
                w(wr[:, k, :], I["ffn_router_w"].rearrange("e (k p) -> k p e", k=2)[k], allow_slow_non_contiguous=True)
            for j, n in enumerate(("attn_ln_w", "attn_memn_w", "attn_ffn_ln_w")):
                w(lnw[:, j, :], I[n].rearrange("(k p) -> p k", k=2), allow_slow_non_contiguous=True)
            w(qkw[:, 0, :], I["attn_qn_w"].partition_broadcast(CH))
            w(qkw[:, 1, :], I["attn_kn_w"].partition_broadcast(CH))
            w(temp[:, :], I["attn_temperature"].partition_broadcast(CH))
            w(decay[:, :], I["attn_head_decay"].partition_broadcast(CH))

            def load(b, n):
                sp.dma_start(hh[:, b], mem.h0[n].rearrange("(c p) d -> p c d", c=NCH)).then_inc(ld_h[b], 16)
            load(0, 0)
            load(1, 1)
            sp.wait_ge(pad_ready, 1)
            for k in range(IDLE + 1):
                sp.dma_start(mem.xs[E * CAP + k * T:E * CAP + (k + 1) * T, :].rearrange("(c p) d -> p c d", c=TC),
                             pad_x[:, :, :]).then_inc(st_pad, 16)
            sp.dma_start(out[NTOK:NTOK + T, :].rearrange("(c p) d -> p c d", c=TC), pad_x[:, :, 0:D]).then_inc(st_pad, 16)
            with sp.Fori(0, NP) as i:
                for b in range(2):
                    n = i * 2 + b
                    wait = waiter(sp, n)
                    wait(h_used)
                    sp.dma_start(hh[:, b], mem.h0[bass.ds(i * 2 + (b + 2), 1), :, :].rearrange(
                        "o (c p) d -> p (o c) d", c=NCH)).then_inc(ld_h[b], 16)
                    wait(h2_done)
                    sp.dma_start(out[bass.ds(i * (2 * L) + b * L, L), :].rearrange("(c p) d -> p c d", c=NCH),
                                 h2[:, b]).then_inc(st_h[b], 16)
                    sp.wait_ge(st_h[b], i * 16 + 16)
                    sp.sem_inc(h2_free, 1)
            for b in range(2):
                sp.wait_ge(ld_h[b], 16 * (NP + 1))
            sp.wait_ge(st_pad, 16 * (IDLE + 2))

        @block.vector
        def _(dve):
            V = nc.vector
            n = [0]

            def s(ins):
                ins.then_inc(setup, 1)
                n[0] += 1
                dve.wait_ge(setup, n[0])
            s(V.memset(pad_x[:, :, :], 0.0))
            V.tensor_copy(pad_x[:, :, D], c("padid")).then_inc(pad_ready, 1)
            s(V.memset(mhalf[:, :], -0.5))
            s(V.memset(qf[:, :, :], 0.0))
            s(V.memset(ve[:, :, :, :], 0.0))
            s(V.memset(states[:, :, :, :, :], 0.0))
            s(V.memset(qt[:, :, :, L:], 0.0))
            s(V.tensor_scalar(tokno[:, :], c("tokno", CH), float(-L), None, ALU.add))
            s(V.tensor_copy(base[:, :, :].rearrange("p c e -> p (c e)"), c("base", CH)))
            dve.wait_ge(ld, 16 * 18)
            for k in range(2):
                s(V.tensor_scalar(wcomp[:, k, :], wcomp[:, k, :], lnw[:, 0, k:k + 1], None, ALU.mult))
                s(V.tensor_scalar(wproj[:, k, :], wproj[:, k, :], lnw[:, 1, k:k + 1], None, ALU.mult))
                for j in range(2):
                    s(V.tensor_scalar(w12[:, k, j, :], w12[:, k, j, :], lnw[:, 2, k:k + 1], None, ALU.mult))
            s(V.tensor_scalar(wproj[:, :, :], wproj[:, :, :], 0.5, None, ALU.mult))
            s(V.tensor_scalar(wlat[:, :], wlat[:, :], 0.5, None, ALU.mult))
            s(V.tensor_scalar(w3[:, :, :], w3[:, :, :], 0.5, None, ALU.mult))
            s(V.tensor_scalar(temp[:, :], temp[:, :], 0.125, None, ALU.mult))
            cosc, sinc = [c(k, CH).rearrange("p (c d) -> p c d", c=NCH) for k in ("cos", "sin")]
            for k in range(2):
                wb = qkw[:, k, :].unsqueeze(1).to_broadcast([CH, NCH, DH])
                s(V.tensor_tensor(COS[:, :, k, :], cosc, wb, ALU.mult))
                for half in range(2):
                    o = slice(half * 8, half * 8 + 8)
                    wp = qkw[:, k, 8 - half * 8:16 - half * 8].unsqueeze(1).to_broadcast([CH, NCH, 8])
                    s(V.tensor_tensor(SIN[:, :, k, o], sinc[:, :, o], wp, ALU.mult))
            dve.wait_ge(act_tables, 1)
            s(V.tensor_scalar(decay[:, :], decay[:, :], 0.325, 0.625, ALU.mult, ALU.add))
            s(V.tensor_scalar(decay[:, :], decay[:, :], 1e-5, 0.999, ALU.max, ALU.min))
            dve.sem_inc(tables, 1)
            dve.wait_ge(act_tables, 2 + NCH)
            s(V.tensor_scalar(limit[:, :, :], df[:, :, :], 1e-35, None, ALU.max))
            s(V.reciprocal(limit[:, :, :], limit[:, :, :]))
            s(V.tensor_scalar(limit[:, :, :], limit[:, :, :], 1e-5, None, ALU.mult))
            s(V.tensor_scalar(idf[:, :, :], df[:, :, :], 1e-8, None, ALU.add))
            s(V.reciprocal(idf[:, :, :], idf[:, :, :]))
            s(V.tensor_scalar(decay[:, :], decay[:, :], -1.0, 1.0, ALU.mult, ALU.add))
            s(V.tensor_tensor(idf[:, :, :], idf[:, :, :], decay[:, :].unsqueeze(1).to_broadcast([CH, NCH, H]), ALU.mult))
            s(V.tensor_copy(ve[:, :, :, DH], idf[:, :, :]))
            dve.sem_inc(tables, 1)

            dve.sem_inc(rk_read, 1)

            def stats(src, j, s_, count):
                for q in range(NCH):
                    last = V.bn_stats(stat[:, j, q, :], src[:, q, :])
                last.then_inc(s_, 1)
                dve.wait_ge(s_, count)
                apart(dve)
                for q in range(NCH):
                    last = V.bn_aggr(mv[:, j, q, :], stat[:, j, q, :])
                last.then_inc(s_, 1)
                dve.wait_ge(s_, count + 1)

            def norm_in(n, lane, loads):
                dve.wait_ge(ld_h[lane], loads)
                stats(hh[:, lane], 0, ln_step, n * 2 + 1)
                V.tensor_scalar(ve2[:, 0, 0:NCH], mv[:, 0, :, 1], 1e-5, None, ALU.add)
                V.tensor_scalar(ve2[:, 0, NCH:], mv[:, 0, :, 1], 1.0 + 1e-6, 1e-11, ALU.mult, ALU.add).then_inc(var_done, 1)

            def norm_out(n, lane):
                wait = waiter(dve, n)
                wait(rstd_done)
                for q in range(NCH):
                    for j, dst in ((0, xln[:, lane]), (1, xn)):
                        last = V.tensor_scalar(dst[:, q, :], hh[:, lane, q, :], mv[:, 0, q, 0:1],
                                               rs[:, 0, j * NCH + q:j * NCH + q + 1], ALU.subtract, ALU.mult)
                last.then_inc(xn_done, 1)

            FRONT, BACK = 29, 18

            class Front:

                def __init__(self, n, lane):
                    self.n, self.lane, self.k, self.wait = n, lane, 0, waiter(dve, n)

                def link(self, ins):
                    ins.then_inc(front_step, 1)
                    self.k += 1
                    dve.wait_ge(front_step, self.n * FRONT + self.k)

                def latent(self):
                    self.wait(lat_th)
                    V.scalar_tensor_tensor(lat[:, :], tl[:, :], 1.0, bank[7][:, 0:L], ALU.add, ALU.mult).then_inc(lat_done, 1)

                def out_gate(self):
                    for q in range(NCH):
                        self.wait(rest_a, q, NCH)
                        V.scalar_tensor_tensor(g2[:, self.lane, q, :], tg[:, q, NPAR:], 1.0,
                                               bank[REST[q]][0:CH, NPAR:NPAR + D], ALU.add, ALU.mult).then_inc(rest_d, 1)

                def head_norm(self):
                    self.wait(qk_sq, NCH - 1, NCH)
                    hd = lambda t: t[:, :].rearrange("p (h d) -> p h d", d=DH)
                    self.link(V.tensor_reduce(ss[:, :], hd(qb), AX.X, ALU.add))
                    self.link(V.tensor_scalar(ss[:, :], ss[:, :], 1.0 / DH, 1e-6, ALU.mult, ALU.add))
                    self.link(V.tensor_scalar(rq[:, :].bitcast(i32), ss[:, :].bitcast(i32), 1, None, ALU.arith_shift_right))
                    self.link(V.tensor_scalar(rq[:, :].bitcast(i32), rq[:, :].bitcast(i32), -1.0, float(0x5f3759df), ALU.mult, ALU.add))
                    for _ in range(3):
                        self.link(V.tensor_tensor(nt[:, :], rq[:, :], rq[:, :], ALU.mult))
                        self.link(V.scalar_tensor_tensor(nt[:, :], nt[:, :], -0.5, ss[:, :], ALU.mult, ALU.mult))
                        self.link(V.scalar_tensor_tensor(rq[:, :], nt[:, :], 1.5, rq[:, :], ALU.add, ALU.mult))
                    V.tensor_tensor(hd(qa), hd(qa), rq[:, :].unsqueeze(2).to_broadcast([CH, NCH * 2 * H, DH]),
                                    ALU.mult).then_inc(qk_n, 1)

                def rotate(self):
                    self.wait(qk_n)
                    for q in range(NCH):
                        for half in range(2):
                            a, o = [t[:, q * NQK:(q + 1) * NQK].rearrange("p (k h d) -> p k h d", k=2, d=DH) for t in (qa, qb)]
                            o1, o2 = slice(half * 8, half * 8 + 8), slice(8 - half * 8, 16 - half * 8)
                            last = V.tensor_tensor(o[:, :, :, o1], a[:, :, :, o2],
                                                   SIN[:, q, :, o1].unsqueeze(2).to_broadcast([CH, 2, H, 8]), ALU.mult)
                    self.link(last)

                def rotated(self):
                    self.wait(qk_cos)
                    V.tensor_tensor(qc[:, :], qc[:, :], qb[:, :], ALU.add).then_inc(qk_rot, 1)

                def gate_argument(self):
                    par = tg[:, :, 0:NPAR].rearrange("p c (h j) -> p c h j", j=4)
                    g = [gt[:, j, :] for j in range(6)]
                    g3 = lambda a: a.rearrange("p (c h) -> p c h", c=NCH)
                    V.tensor_tensor(g3(g[0]), par[:, :, :, 1], par[:, :, :, 3], ALU.subtract)
                    self.link(V.tensor_scalar(g3(g[3]), par[:, :, :, 2], 1.0, None, ALU.add))
                    V.tensor_tensor(g[1], g[0], g[0], ALU.mult)
                    self.link(V.scalar_tensor_tensor(g3(g[3]), par[:, :, :, 0], 1.0, g3(g[3]), ALU.add, ALU.mult))
                    self.link(V.tensor_scalar(g[2], g[1], COS_POLY[7], None, ALU.mult))
                    for p in range(6, 0, -1):
                        self.link(V.scalar_tensor_tensor(g[2], g[2], COS_POLY[p], g[1], ALU.add, ALU.mult))
                    V.scalar_tensor_tensor(g[2], g[2], COS_POLY[0], g[3], ALU.add, ALU.mult).then_inc(gate_arg, 1)

                def gate(self):
                    self.wait(gate_th)
                    self.link(V.tensor_scalar(gt[:, 4, :], gt[:, 4, :], 0.6, 0.5, ALU.mult, ALU.add))
                    self.link(V.tensor_scalar(gt[:, 4, :], gt[:, 4, :], 0.05, 0.95, ALU.max, ALU.min))
                    V.tensor_tensor(gt[:, 5, :], gt[:, 4, :], idf[:, :, :].rearrange("p c h -> p (c h)"),
                                    ALU.mult).then_inc(gate_w, 1)

                def features(self):
                    self.wait(qk_exp)
                    hd = lambda t: t[:, :].rearrange("p (h d) -> p h d", d=DH)
                    V.scalar_tensor_tensor(qf[:, :, 0:DH], hd(qb), 1.0, hd(qa), ALU.min, ALU.add).then_inc(qf_done, 1)

                def state(self):
                    for k in range(2):
                        self.wait(st_mm, k, 2)
                        V.tensor_tensor(states[:, k, :, :, 0:VE],
                                        bank[6 + k][:, 0:GR * 128].rearrange("p (g r e) -> p g r e", g=GR, r=4)[:, :, :, 0:VE],
                                        c("headblock").rearrange("p (r e) -> p r e", r=4).unsqueeze(1).to_broadcast([128, GR, 4, VE]),
                                        ALU.mult).then_inc(st_d, 1)

                def scores(self, q):
                    for r in range(4):
                        self.wait(sc_mm, 4 * q + r, 4 * NCH)
                        V.tensor_tensor(sm[:, q % 2, r, :].rearrange("p (g t) -> p g t", g=GR),
                                        bank[SC[r]][0:CH, 0:GR * CW].rearrange("p (g t) -> p g t", g=GR)[:, :, 0:CH],
                                        c("causal", CH).unsqueeze(1).to_broadcast([CH, GR, CH]), ALU.mult).then_inc(sc_d, 1)

                def attention(self):
                    for q, n, k in ((0, 2, 0), (2, 1, 6)):
                        self.wait(ot_mm, q // 2, 2)
                        o = mem.psum[0:CH, k:k + n, 0:H * 32].rearrange("p c (h e) -> p c h e", e=32)
                        d = dn[:, q:q + n, :]
                        self.link(V.tensor_tensor(d, o[:, :, :, DH], limit[:, q:q + n, :], ALU.max))
                        self.link(V.reciprocal(d, d))
                        last = V.tensor_tensor(att[:, self.lane, q:q + n].rearrange("p c (h d) -> p c h d", d=DH), o[:, :, :, 0:DH],
                                               d.unsqueeze(3).to_broadcast([CH, n, H, DH]), ALU.mult)
                    last.then_inc(att_done, 1)

                def end(self):
                    assert self.k == FRONT, self.k

            class Back:

                def __init__(self, n, lane):
                    self.n, self.lane, self.k, self.wait = n, lane, 0, waiter(dve, n)

                def link(self, ins):
                    ins.then_inc(back_step, 1)
                    self.k += 1
                    dve.wait_ge(back_step, self.n * BACK + self.k)

                def project(self):
                    self.wait(att_rs)
                    self.wait(pr_mm)
                    for q in range(NCH):
                        last = V.scalar_tensor_tensor(x1[:, q, :], bank[2 + q // 2][0:CH, (q % 2) * D:(q % 2 + 1) * D],
                                                      rr[:, 0, q:q + 1], g2[:, self.lane, q, :], ALU.mult, ALU.mult)
                    last.then_inc(pr_d, 1)
                    self.wait(pr_d)
                    V.tensor_tensor(x1[:, :, :], x1[:, :, :], xln[:, self.lane], ALU.add).then_inc(x1_done, 1)

                def hidden(self, m):
                    k = FB[m]
                    self.wait(f_th, m, 4)
                    self.link(V.scalar_tensor_tensor(hid[:, m, :], th[:, m, :], 1.0, bank[k][:, 0:L], ALU.add, ALU.mult))
                    V.tensor_tensor(hid[:, m, :], hid[:, m, :], bank[k + 1][:, 0:L], ALU.mult).then_inc(f_d, 1)

                def residual(self):
                    self.wait(h2_free)
                    self.wait(h_used)
                    self.wait(w3_mm)
                    V.tensor_tensor(h2[:, self.lane, 0:3:2, :], hx[:, 0:3:2, :], bank[2][0:CH, 0:2 * D].rearrange("p (c d) -> p c d", c=2), ALU.add)
                    V.tensor_tensor(h2[:, self.lane, 1, :], hx[:, 1, :], bank[3][0:CH, 0:D], ALU.add).then_inc(h2_done, 1)

                def norm_in(self):
                    self.wait(h2_done)
                    stats(h2[:, self.lane], 1, back_step, self.n * BACK + self.k + 1)
                    self.k += 2
                    V.tensor_scalar(ve2[:, 1, 0:NCH], mv[:, 1, :, 1], 1e-5, None, ALU.add).then_inc(var2_done, 1)

                def norm_out(self):
                    self.wait(rstd2_done)
                    self.wait(row_free)
                    for q in range(NCH):
                        last = V.tensor_scalar(row[:, self.lane, 0, q, 0:D], h2[:, self.lane, q, :], mv[:, 1, q, 0:1], rs[:, 1, q:q + 1],
                                               ALU.subtract, ALU.mult)
                    last.then_inc(flat_done, 1)

                def top(self):
                    self.wait(lg_mm)
                    self.link(V.tensor_copy(lg[:, :, :], bank[2][0:CH, 0:NCH * E].rearrange("p (c e) -> p c e", c=NCH)))
                    apart(dve)
                    for q in range(NCH):
                        last = V.max(mx[:, q, :], lg[:, q, :])
                    self.link(last)
                    apart(dve)
                    for q in range(NCH):
                        last = V.max_index(mi[:, q, :], mx[:, q, :], lg[:, q, :])
                    self.link(last)
                    V.tensor_tensor(ew[:, 0, :], mx[:, :, 1], mx[:, :, 0], ALU.subtract).then_inc(top_done, 1)
                    self.link(V.tensor_copy(tf[:, :, :], mi[:, :, 0:2]))
                    self.link(V.tensor_tensor(oh[:, :, :, :], c("expert", CH).unsqueeze(1).unsqueeze(1).to_broadcast([CH, NCH, 2, E]),
                                              tf[:, :, :].unsqueeze(3).to_broadcast([CH, NCH, 2, E]), ALU.is_equal))
                    V.tensor_tensor(ohs[:, :, :], oh[:, :, 0, :], oh[:, :, 1, :], ALU.add).then_inc(oh_done, 1)

                def places(self):
                    self.wait(rk_mm)
                    before = bank[3][0:CH, 0:NCH * E].rearrange("p (c e) -> p c e", c=NCH)
                    total = bank[3][0:CH, 32:32 + NCH * E].rearrange("p (c e) -> p c e", c=NCH)
                    self.link(V.tensor_tensor(base[:, 1, :], base[:, 0, :], total[:, 0, :], ALU.add))
                    self.link(V.tensor_tensor(base[:, 2, :], base[:, 1, :], total[:, 1, :], ALU.add))
                    self.link(V.tensor_tensor(rk[:, :, :], before, base[:, :, :], ALU.add))
                    V.tensor_tensor(base[:, 0, :], base[:, 2, :], total[:, 2, :], ALU.add).then_inc(rk_read, 1)
                    self.link(V.tensor_tensor(rp[:, :, :, :], oh[:, :, :, :], rk[:, :, :].unsqueeze(2).to_broadcast([CH, NCH, 2, E]), ALU.mult))
                    self.link(V.tensor_reduce(de[:, :, :], rp[:, :, :, :], AX.X, ALU.add))
                    V.tensor_copy(di[:, self.lane], de[:, :, :])
                    self.wait(ew_exp)
                    self.link(V.tensor_scalar(ew[:, 0, :], ew[:, 1, :], 1.0, None, ALU.add))
                    self.link(V.reciprocal(row[:, self.lane, 0, :, D + 1], ew[:, 0, :]))
                    V.tensor_tensor(row[:, self.lane, 1, :, D + 1], ew[:, 1, :], row[:, self.lane, 0, :, D + 1], ALU.mult).then_inc(dest_done, 1)

                def end(self):
                    assert self.k == BACK, self.k

            norm_in(0, 0, 16)
            norm_out(0, 0)
            f = Front(0, 0)
            f.latent(); f.out_gate(); f.head_norm(); f.gate_argument(); f.rotate(); f.rotated(); f.gate(); f.features()
            f.state()
            for q in range(NCH):
                f.scores(q)
            norm_in(1, 1, 16)
            norm_out(1, 1)
            f.attention(); f.end()
            Front(1, 1).latent()
            with dve.Fori(0, NP) as i:
                for b in range(2):
                    f, k = Front(i * 2 + (b + 1), 1 - b), Back(i * 2 + b, b)
                    f.out_gate()
                    k.project()
                    f.head_norm()
                    f.gate_argument()
                    f.rotate()
                    k.hidden(0)
                    f.rotated()
                    f.gate()
                    k.hidden(1)
                    k.hidden(2)
                    k.hidden(3)
                    f.features()
                    k.residual()
                    k.norm_in()
                    f.state()
                    k.norm_out()
                    f.scores(0)
                    f.scores(1)
                    k.top()
                    f.scores(2)
                    norm_in(i * 2 + (b + 2), b, i * 16 + 32)
                    norm_out(i * 2 + (b + 2), b)
                    k.places()
                    f.attention()
                    Front(i * 2 + (b + 2), b).latent()
                    f.end()
                    k.end()

        @block.scalar
        def _(act):
            A = nc.scalar.activation
            act.wait_ge(ld, 16 * 18)
            A(decay[:, :], decay[:, :], ACT.Tanh, scale=0.5).then_inc(act_tables, 1)
            act.wait_ge(tables, 1)
            A(logd[:, :], decay[:, :], ACT.Ln).then_inc(act_tables, 1)
            act.wait_ge(act_tables, 2)
            for q in range(NCH):
                A(df[:, q, :], logd[:, :], ACT.Exp, scale=c("pos1", CH)[:, q:q + 1]).then_inc(act_tables, 1)

            class Front:
                def __init__(self, n):
                    self.wait = waiter(act, n)

                def x_t(self):
                    self.wait(xn_t)
                    A(xt[:, :, :], two(4, L), ACT.Copy).then_inc(xt_done, 1)

                def latent(self):
                    self.wait(lat_mm)
                    A(tl[:, :], bank[7][:, 0:L], ACT.Tanh, scale=0.5).then_inc(lat_th, 1)

                def rest(self):
                    for q in range(NCH):
                        self.wait(rest_mm, q, NCH)
                        src = bank[REST[q]][0:CH, 0:NREST]
                        A(tg[:, q, :], src[:, 0:NPAR + D], ACT.Tanh, scale=0.5)
                        A(v[:, q, :], src[:, NPAR + D:], ACT.Copy).then_inc(rest_a, 1)

                def qk(self):
                    for q in range(NCH):
                        self.wait(qk_mm, q, NCH)
                        src = bank[QK[q]][0:CH, 0:NQK]
                        A(qb[:, q * NQK:(q + 1) * NQK], src, ACT.Square)
                        A(qa[:, q * NQK:(q + 1) * NQK], src, ACT.Copy).then_inc(qk_sq, 1)

                def gate(self):
                    self.wait(gate_arg)
                    A(gt[:, 4, :], gt[:, 2, :], ACT.Tanh, scale=temp[:, :]).then_inc(gate_th, 1)

                def features(self):
                    self.wait(qk_rot)
                    A(qb[:, :], qc[:, :], ACT.Exp)
                    A(qa[:, :], qc[:, :], ACT.Relu).then_inc(qk_exp, 1)

                def qk_t(self):
                    for q in range(NCH):
                        self.wait(tq_mm, q, NCH)
                        src = mem.psum[:, (4, 6, 4)[q]:(4, 6, 4)[q] + 2, 0:GR * CH].rearrange("p k (g t) -> p k g t", g=GR)
                        A(qt[:, :, :, q * CH:(q + 1) * CH], src, ACT.Copy).then_inc(tq_a, 1)

                def sums(self, q):
                    self.wait(pv_mm, q, NCH)
                    A(ot[:, q, :], bank[(7, 6, 7)[q]][:, 0:GR * CH], ACT.Copy).then_inc(ot_a, 1)

            class Back:
                def __init__(self, n, lane):
                    self.lane, self.wait = lane, waiter(act, n)

                def sumsq(self, j, src, ready, done):
                    self.wait(ready)
                    for q in range(NCH):
                        last = A(junk[:, j, q, :], src[:, q, :], ACT.Square, scale=SCALE_MEAN, accum_out=sa[:, j, q:q + 1])
                    last.then_inc(done, 1)

                def copy_t(self, k, ready, done):
                    self.wait(ready)
                    A(xb[:, :, :], two(k, L), ACT.Copy).then_inc(done, 1)

                def norm2(self):
                    self.wait(x1_rs)
                    for q in range(NCH):
                        last = A(xn2[:, q, :], x1[:, q, :], ACT.Copy, scale=rr[:, 1, q:q + 1])
                    last.then_inc(xn2_done, 1)

                def tanh(self, m):
                    self.wait(f_mm, m, 4)
                    A(th[:, m, :], bank[FB[m]][:, 0:L], ACT.Tanh, scale=0.5).then_inc(f_th, 1)

                def row(self):
                    self.wait(flat_done)
                    A(row[:, self.lane, 1, :, 0:D], row[:, self.lane, 0, :, 0:D], ACT.Copy).then_inc(row_copied, 1)

                def top(self):
                    self.wait(top_done)
                    A(ew[:, 1, :], ew[:, 0, :], ACT.Exp).then_inc(ew_exp, 1)

            f = Front(0)
            f.x_t(); f.latent(); f.rest(); f.qk(); f.gate(); f.features(); f.qk_t()
            f.sums(0); f.sums(1); f.sums(2)
            Front(1).x_t(); Front(1).latent()
            with act.Fori(0, NP) as i:
                for b in range(2):
                    f, k = Front(i * 2 + (b + 1)), Back(i * 2 + b, b)
                    k.copy_t(0, at_t, at_a)
                    k.sumsq(0, att[:, b], att_done, att_ss)
                    f.rest()
                    f.qk()
                    k.sumsq(1, x1, x1_done, x1_ss)
                    k.norm2()
                    k.copy_t(0, x2_t, x2_a)
                    f.gate()
                    k.tanh(0)
                    k.tanh(1)
                    k.tanh(2)
                    k.tanh(3)
                    f.features()
                    f.qk_t()
                    k.row()
                    k.copy_t(2, fl_t, fl_a)
                    f.sums(0)
                    f.sums(1)
                    k.top()
                    f.sums(2)
                    Front(i * 2 + (b + 2)).x_t()
                    Front(i * 2 + (b + 2)).latent()

        @block.gpsimd
        def _(pool):
            PO = nc.gpsimd
            pool.sem_inc(row_free, 2)
            pool.sem_inc(h2_free, 2)
            pool.wait_ge(tables, 2)

            def norm(n):
                waiter(pool, n)(var_done)
                PO.tensor_tensor(rs[:, 0, :], ve2[:, 0, :], mhalf[:, 0:2 * NCH], ALU.pow).then_inc(rstd_done, 1)

            def cos(n):
                waiter(pool, n)(qk_n)
                for q in range(NCH):
                    a, o = [t[:, q * NQK:(q + 1) * NQK].rearrange("p (k h d) -> p k h d", k=2, d=DH) for t in (qa, qc)]
                    last = PO.tensor_tensor(o, a, COS[:, q, :, :].unsqueeze(2).to_broadcast([CH, 2, H, DH]), ALU.mult)
                last.then_inc(qk_cos, 1)

            def values(n):
                wait = waiter(pool, n)
                wait(gate_w)
                wait(rest_a, NCH - 1, NCH)
                PO.tensor_tensor(ve[:, :, :, 0:DH], v[:, :, :].rearrange("p c (h d) -> p c h d", d=DH),
                                 gt[:, 5, :].rearrange("p (c h) -> p c h", c=NCH).unsqueeze(3).to_broadcast([CH, NCH, H, DH]),
                                 ALU.mult).then_inc(ve_done, 1)

            def root(n, j, ready, step, done):
                wait = waiter(pool, n)
                wait(ready)
                apart(pool)
                PO.tensor_scalar(sae[:, j, :], sa[:, j, :], 1e-6, None, ALU.add).then_inc(step, 1)
                wait(step)
                PO.tensor_tensor(rr[:, j, :], sae[:, j, :], mhalf[:, 0:NCH], ALU.pow).then_inc(done, 1)

            norm(0)
            cos(0)
            values(0)
            norm(1)

            def scatter(n, lane, sent_before):
                wait = waiter(pool, n)
                wait(dest_done)
                wait(rows_numbered)
                wait(row_copied)
                apart(pool)
                for q in range(NCH):
                    for j in range(2):
                        PO.indirect_dma_start(out=mem.xs, out_offset=bass.IndirectOffsetOnAxis(ap=di[:, lane, q, j:j + 1], axis=0),
                                              in_=row[:, lane, j, q, :], in_offset=None).then_inc(sent[lane], 16)
                return sent_before + 16 * 2 * NCH

            def pair(i, first=False):
                for b in range(2):
                    n = i * 2 + b
                    wait = waiter(pool, n)
                    root(n, 0, att_ss, att_step, att_rs)
                    root(n, 1, x1_ss, x1_step, x1_rs)
                    if b or not first:
                        arrived = scatter(i * 2 + (b - 1), 1 - b, i * (16 * 2 * NCH) - (0 if b else 16 * 2 * NCH))
                    cos(i * 2 + (b + 1))
                    PO.tensor_tensor(hx[:, :, :], hh[:, b], x1[:, :, :], ALU.add).then_inc(h_used, 1)
                    values(i * 2 + (b + 1))
                    if b or not first:
                        pool.wait_ge(sent[1 - b], arrived)
                        pool.sem_inc(row_free, 1)
                    wait(var2_done)
                    PO.tensor_tensor(rs[:, 1, 0:NCH], ve2[:, 1, 0:NCH], mhalf[:, 0:NCH], ALU.pow).then_inc(rstd2_done, 1)
                    PO.tensor_scalar(tokno[:, :], tokno[:, :], float(L), None, ALU.add).then_inc(tok_step, 1)
                    wait(flat_done)
                    wait(tok_step)
                    apart(pool)
                    for j in range(2):
                        last = PO.tensor_copy(row[:, b, j, :, D], tokno[:, :])
                    last.then_inc(rows_numbered, 1)
                    norm(i * 2 + (b + 2))

            pair(0, first=True)
            with pool.Fori(1, NP) as i:
                pair(i)
            pool.wait_ge(sent[1], scatter(2 * NP - 1, 1, (NP - 1) * 16 * 2 * NCH))

        @block.tensor
        def _(pe):
            MM, TR = nc.tensor.matmul, nc.tensor.transpose
            ident = c("ident", CH)[:, 0:CH]
            pe.wait_ge(tables, 2)

            def transpose_rows(src, k, done):
                for kk in range(2):
                    for q in range(NCH):
                        last = TR(bank[k + kk][0:KD, q * CH:(q + 1) * CH], src[:, q, kk * KD:(kk + 1) * KD], ident)
                last.then_inc(done, 1)

            def rows_out(w, ks, src, done):
                for q in range(NCH):
                    for kk in range(ks):
                        last = MM(bank[2 + q // 2][0:CH, (q % 2) * D:(q % 2 + 1) * D], src[:, kk, q * CH:(q + 1) * CH],
                                  w[:, kk, :], start=(kk == 0), stop=(kk == ks - 1))
                last.then_inc(done, 1)

            class Front:
                def __init__(self, n):
                    self.wait = waiter(pe, n)

                def x_t(self):
                    self.wait(xn_done)
                    transpose_rows(xn, 4, xn_t)

                def latent(self):
                    self.wait(xt_done)
                    for kk in range(2):
                        last = MM(bank[7][:, 0:L], wcomp[:, kk, :], xt[:, kk, :], start=(kk == 0), stop=(kk == 1))
                    last.then_inc(lat_mm, 1)

                def rest(self, *chunks):
                    self.wait(lat_done)
                    for q in chunks:
                        MM(bank[REST[q]][0:CH, 0:NREST], lat[:, q * CH:(q + 1) * CH], wlat[:, NQK:],
                           start=True, stop=True).then_inc(rest_mm, 1)

                def qk(self):
                    for q in range(NCH):
                        if q:
                            self.wait(rest_d, q - 1, NCH)
                        MM(bank[QK[q]][0:CH, 0:NQK], lat[:, q * CH:(q + 1) * CH], wlat[:, 0:NQK],
                           start=True, stop=True).then_inc(qk_mm, 1)

                def qk_t(self):
                    self.wait(qf_done)
                    for q in range(NCH):
                        if q == 2:
                            self.wait(tq_a, 0, NCH)
                        for kk in range(2):
                            for g in range(GR):
                                h0 = (q * 2 + kk) * H + 4 * g
                                last = TR(bank[(4, 6, 4)[q] + kk][:, g * CH:(g + 1) * CH],
                                          qf[:, h0:h0 + 4, :].rearrange("p h d -> p (h d)"), ident)
                        last.then_inc(tq_mm, 1)

                def state(self):
                    self.wait(ve_done)
                    self.wait(tq_a, 1, NCH)
                    for s_ in range(2):
                        for g in range(GR):
                            for q in range(s_ + 1):
                                h0 = (q * 2 + 1) * H + 4 * g
                                last = MM(bank[6 + s_][:, g * 128:(g + 1) * 128],
                                          qf[:, h0:h0 + 4, :].rearrange("p h d -> p (h d)"),
                                          ve[:, q, 4 * g:4 * g + 4, :].rearrange("p h e -> p (h e)"),
                                          start=(q == 0), stop=(q == s_))
                        last.then_inc(st_mm, 1)

                def scores(self, q):
                    if q == 0:
                        self.wait(tq_a, 2, NCH)
                    for r in range(4):
                        if q:
                            self.wait(sc_d, 4 * (q - 1) + r, 4 * NCH)
                        for g in range(GR):
                            last = MM(bank[SC[r]][0:CH, g * CW:(g + 1) * CW], qt[32 * r:32 * r + DH, 1, g, q * CH:(q + 1) * CH],
                                      qt[32 * r:32 * r + DH, 0, g, q * CH:q * CH + CW], start=True, stop=True)
                        last.then_inc(sc_mm, 1)

                def values(self, q):
                    self.wait(sc_d, 4 * q + 3, 4 * NCH)
                    if q < 2:
                        self.wait(st_d, 1, 2)
                    else:
                        self.wait(ot_a, 0, NCH)
                    to = bank[(7, 6, 7)[q]]
                    for g in range(GR):
                        t = slice(g * CH, (g + 1) * CH)
                        if q:
                            MM(to[:, t], states[:, q - 1, g].rearrange("p r e -> p (r e)"), qt[:, 0, g, q * CH:(q + 1) * CH],
                               start=True, stop=False)
                        for r in range(4):
                            last = MM(to[32 * r:32 * r + 32, t], ve[:, q, 4 * g + r, :], sm[:, q % 2, r, t],
                                      start=(q == 0), stop=True)
                    last.then_inc(pv_mm, 1)

                def sums_t(self, q):
                    self.wait(ot_a, q, NCH)
                    for g in range(GR):
                        last = TR(bank[(0, 1, 6)[q]][0:CH, g * 128:(g + 1) * 128], ot[:, q, g * CH:(g + 1) * CH], mem.c("ident"))
                    if q:
                        last.then_inc(ot_mm, 1)

            class Back:
                def __init__(self, n, lane):
                    self.lane, self.wait = lane, waiter(pe, n)

                def att_t(self):
                    self.wait(att_done)
                    transpose_rows(att[:, self.lane], 0, at_t)

                def project(self):
                    self.wait(rk_read)
                    self.wait(at_a)
                    rows_out(wproj, 2, xb, pr_mm)

                def norm2_t(self):
                    self.wait(xn2_done)
                    transpose_rows(xn2, 0, x2_t)

                def up(self, m):
                    if m == 0:
                        self.wait(x2_a)
                    if m == 3:
                        self.wait(f_d, 0, 4)
                    for j in range(2):
                        for kk in range(2):
                            last = MM(bank[FB[m] + j][:, 0:L], w12[:, kk, j, m * 128:(m + 1) * 128], xb[:, kk, :],
                                      start=(kk == 0), stop=(kk == 1))
                    last.then_inc(f_mm, 1)

                def down(self, m):
                    self.wait(f_d, m, 4)
                    for q in range(2):
                        MM(bank[2 + q][0:CH, 0:D], hid[:, m, q * CH:(q + 1) * CH], w3[:, m, :], start=(m == 0), stop=(m == 3))

                def down_last(self):
                    for m in range(4):
                        last = MM(bank[2][0:CH, D:2 * D], hid[:, m, 2 * CH:3 * CH], w3[:, m, :], start=(m == 0), stop=(m == 3))
                    last.then_inc(w3_mm, 1)

                def flat_t(self):
                    self.wait(flat_done)
                    transpose_rows(row[:, self.lane, 0], 2, fl_t)

                def logits(self):
                    self.wait(fl_a)
                    for q in range(NCH):
                        for kk in range(2):
                            last = MM(bank[2][0:CH, q * E:(q + 1) * E], xb[:, kk, q * CH:(q + 1) * CH], wr[:, kk, :],
                                      start=(kk == 0), stop=(kk == 1))
                    last.then_inc(lg_mm, 1)

                def ranks(self):
                    self.wait(oh_done)
                    src = ohs[:, :, :].rearrange("p c e -> p (c e)")
                    MM(bank[3][0:CH, 0:NCH * E], c("before", CH), src, start=True, stop=True)
                    MM(bank[3][0:CH, 32:32 + NCH * E], c("ones", CH), src, start=True, stop=True).then_inc(rk_mm, 1)

            f = Front(0)
            f.x_t(); f.latent(); f.rest(0, 1, 2); f.qk(); f.qk_t(); f.state(); f.scores(0)
            f.scores(1); f.values(0); f.scores(2); f.values(1); f.values(2)
            Front(1).x_t()
            f.sums_t(0); f.sums_t(1); f.sums_t(2)
            Front(1).latent()
            with pe.Fori(0, NP) as i:
                for b in range(2):
                    f, k = Front(i * 2 + (b + 1)), Back(i * 2 + b, b)
                    k.att_t()
                    f.rest(0)
                    k.project()
                    f.rest(1, 2)
                    f.qk()
                    k.norm2_t()
                    for m in range(4):
                        k.up(m)
                        if m > 1:
                            k.down(m - 2)
                    k.down(2)
                    k.down(3)
                    k.down_last()
                    f.qk_t()
                    f.state()
                    f.scores(0)
                    k.flat_t()
                    f.scores(1)
                    f.values(0)
                    k.logits()
                    f.scores(2)
                    f.values(1)
                    f.values(2)
                    k.ranks()
                    Front(i * 2 + (b + 2)).x_t()
                    f.sums_t(0)
                    f.sums_t(1)
                    f.sums_t(2)
                    Front(i * 2 + (b + 2)).latent()


def experts(nc, mem, I, out):
    NM = F // 128
    NPAIR, LAST = NTASK // 2, NTASK % 2
    assert LAST == 1
    with ExitStack() as ctx:
        mem.ctx = ctx
        sb, sem, X, Y, c = mem.sb, mem.sem, mem.X, mem.Y, mem.c
        xr = sb("task_rows", [128, 2, TC, ROW])
        w1, w2 = sb("task_w1", [KD, 2, 2, F]), sb("task_w2", [128, 2, NM, D])
        b1, b2 = sb("task_b1", [128, 2, NM]), sb("task_b2", [128, 2, D])
        xt = sb("task_x_t", [KD, 2, 2, T])
        hid = sb("task_hidden", [128, 2, NM, T])
        wt, ids = sb("task_weight", [128, 2, TC]), sb("task_ids", [128, 2, TC], i32)
        ys = sb("task_out", [128, 2, TC, D])
        cnt, tiles, cum = sb("count", [1, E]), sb("tiles", [1, E]), sb("tiles_upto", [1, E])
        cmp_, mix = sb("over_steps", [1, E, RSTEPS]), sb("mix", [1, E, E])
        ind, indt = sb("expert_past", [1, NTASK, E]), sb("expert_past_tiles", [1, NTASK, E])
        ej, bef, off = sb("task_expert_f", [1, NTASK]), sb("task_before", [1, NTASK]), sb("task_row_f", [1, NTASK])
        table, tail = sb("task_table", [1, 2, NTASK], i32), sb("tail_row", [1, E], i32)
        step, table_ready, tails = sem("table_step"), sem("table_ready"), sem("tails_stored")
        ld_x, ld_w = ([sem(f"{n}{p}") for p in range(2)] for n in ("task_rows_loaded", "task_weights_loaded"))
        x_free, w1_free, w2_free, y_free = sem("task_rows_free"), sem("w1_free"), sem("w2_free"), sem("task_out_free")
        tr, xt_a, xt_d = sem("task_transposed"), sem("task_xt_act"), sem("task_xt_dve")
        l1, gelu, l2, y_add, y_done = sem("up_mm"), sem("gelu_done"), sem("down_mm"), sem("bias_added"), sem("task_out_done")
        waited = sem("task_waits_apart")
        added = [sem(f"out_added{p}") for p in range(2)]
        block = ctx.enter_context(nc.Block())
        UP = [X[2], X[3], Y[0][0], Y[0][1]]
        DOWN = Y[1]

        @block.sync
        def _(sp):
            sp.wait_ge(table_ready, 1)
            for e in range(E):
                r = sp.value_load(tail[0:1, e:e + 1], min_val=0, max_val=E * CAP - T)
                sp.dma_start(mem.xs[bass.ds(r, T), :].rearrange("(c p) d -> p c d", c=TC), mem.pad[:, :, :]).then_inc(tails, 16)
            sp.wait_ge(tails, 16 * E)

            def load(j, p):
                row0 = sp.value_load(table[0:1, 0, bass.ds(j, 1)], min_val=0, max_val=E * CAP + IDLE * T)
                e = sp.value_load(table[0:1, 1, bass.ds(j, 1)], min_val=0, max_val=E - 1)
                sp.wait_ge(x_free, j + 1)
                sp.dma_start(xr[:, p], mem.xs[bass.ds(row0, T), :].rearrange("(c p) d -> p c d", c=TC)).then_inc(ld_x[p], 16)
                sp.wait_ge(w1_free, j + 1)
                sp.dma_start(w1[:, p], I["ffn_w1"][bass.ds(e, 1), :, :].rearrange("o (k p) n -> p (o k) n", k=2)).then_inc(ld_w[p], 16)
                sp.wait_ge(w2_free, j + 1)
                sp.dma_start(b1[:, p], I["ffn_b1"][bass.ds(e, 1), :].rearrange("o (p m) -> p (o m)", m=NM)).then_inc(ld_w[p], 16)
                sp.dma_start(w2[:, p], I["ffn_w2"][bass.ds(e, 1), :, :].rearrange("o (p m) n -> p (o m) n", m=NM)).then_inc(ld_w[p], 16)
                sp.dma_start(b2[:, p, :], I["ffn_b2"][bass.ds(e, 1), :].rearrange("o n -> (o n)").partition_broadcast(128)).then_inc(ld_w[p], 16)
            with sp.Fori(0, NPAIR) as i:
                for p in range(2):
                    load(i * 2 + p, p)
            load(NTASK - 1, 0)

        @block.vector
        def _(dve):
            V = nc.vector
            n = [0]

            def s(ins):
                ins.then_inc(step, 1)
                n[0] += 1
                dve.wait_ge(step, n[0])
            first = lambda name, m=None: c(name, 1)[:, 0:m]
            s(V.tensor_tensor(cnt[:, :], mem.base[0:1, 0, :], first("base", E), ALU.subtract))
            s(V.tensor_copy(tail[:, :], mem.base[0:1, 0, :]))
            s(V.tensor_tensor(cmp_[:, :, :], cnt[:, :].unsqueeze(2).to_broadcast([1, E, RSTEPS]),
                              first("steps", RSTEPS).unsqueeze(1).to_broadcast([1, E, RSTEPS]), ALU.is_gt))
            s(V.tensor_reduce(tiles[:, :], cmp_[:, :, :], AX.X, ALU.add))
            s(V.tensor_tensor(mix[:, :, :], tiles[:, :].unsqueeze(1).to_broadcast([1, E, E]),
                              first("upto", E * E).rearrange("o (a b) -> o a b", a=E), ALU.mult))
            s(V.tensor_reduce(cum[:, :], mix[:, :, :], AX.X, ALU.add))
            task = first("task", NTASK)
            s(V.tensor_tensor(ind[:, :, :], cum[:, :].unsqueeze(1).to_broadcast([1, NTASK, E]),
                              task.unsqueeze(2).to_broadcast([1, NTASK, E]), ALU.is_le))
            s(V.tensor_reduce(ej[:, :], ind[:, :, :], AX.X, ALU.add))
            s(V.tensor_tensor(indt[:, :, :], ind[:, :, :], tiles[:, :].unsqueeze(1).to_broadcast([1, NTASK, E]), ALU.mult))
            s(V.tensor_reduce(bef[:, :], indt[:, :, :], AX.X, ALU.add))
            s(V.tensor_tensor(bef[:, :], task, bef[:, :], ALU.subtract))
            s(V.tensor_scalar(bef[:, :], bef[:, :], float(T), None, ALU.mult))
            s(V.scalar_tensor_tensor(off[:, :], ej[:, :], float(CAP), bef[:, :], ALU.mult, ALU.add))
            s(V.tensor_copy(table[:, 0, :], off[:, :]))
            s(V.tensor_scalar(ej[:, :], ej[:, :], float(E - 1), None, ALU.min))
            s(V.tensor_copy(table[:, 1, :], ej[:, :]))
            dve.sem_inc(table_ready, 1)

            def rows_in(j, p):
                dve.wait_ge(tr, j + 1)
                V.tensor_copy(xt[:, p, 1, :], X[1][0:KD, 0:T]).then_inc(xt_d, 1)
                V.tensor_copy(wt[:, p, :], xr[:, p, :, D + 1])
                dve.wait_ge(y_free, j + 1)
                V.tensor_copy(ids[:, p, :], xr[:, p, :, D]).then_inc(x_free, 1)

            def rows_out(j, p):
                for q in range(TC):
                    dve.wait_ge(l2, j * TC + q + 1)
                    V.tensor_tensor(ys[:, p, q, :], DOWN[q % 2][:, 0:D], b2[:, p, :], ALU.add).then_inc(y_add, 1)
                    dve.wait_ge(y_add, j * TC + q + 1)
                    V.tensor_scalar(ys[:, p, q, :], ys[:, p, q, :], wt[:, p, q:q + 1], None, ALU.mult).then_inc(y_done, 1)
                dve.wait_ge(y_done, j * TC + TC)
            rows_in(0, 0)
            with dve.Fori(0, NPAIR) as i:
                for p in range(2):
                    rows_in(i * 2 + (p + 1), 1 - p)
                    rows_out(i * 2 + p, p)
            rows_out(NTASK - 1, 0)

        @block.scalar
        def _(act):
            def rows_in(j, p):
                act.wait_ge(tr, j + 1)
                nc.scalar.activation(xt[:, p, 0, :], X[0][0:KD, 0:T], ACT.Copy).then_inc(xt_a, 1)

            def up(j, p, loads):
                act.wait_ge(ld_w[p], loads)
                for m in range(NM):
                    act.wait_ge(l1, j * NM + m + 1)
                    nc.scalar.activation(hid[:, p, m, :], UP[m % 4][:, 0:T], ACT.Gelu, bias=b1[:, p, m:m + 1]).then_inc(gelu, 1)
            rows_in(0, 0)
            with act.Fori(0, NPAIR) as i:
                for p in range(2):
                    up(i * 2 + p, p, i * 64 + 64)
                    rows_in(i * 2 + (p + 1), 1 - p)
            up(NTASK - 1, 0, (NPAIR + 1) * 64)

        @block.gpsimd
        def _(pool):
            pool.sem_inc(x_free, 2)
            pool.sem_inc(w1_free, 2)
            pool.sem_inc(w2_free, 2)
            pool.sem_inc(y_free, 2)

            def add(j, p, sent):
                for q in range(TC):
                    pool.wait_ge(y_done, j * TC + q + 1)
                    pool.sem_inc(waited, 1)
                    nc.gpsimd.indirect_dma_start(out=out, out_offset=bass.IndirectOffsetOnAxis(ap=ids[:, p, q:q + 1], axis=0),
                                                 in_=ys[:, p, q, :], in_offset=None, compute_op=ALU.add).then_inc(added[p], 16)
                pool.wait_ge(added[p], sent)
                pool.sem_inc(y_free, 1)
            with pool.Fori(0, NPAIR) as i:
                for p in range(2):
                    add(i * 2 + p, p, i * (16 * TC) + 16 * TC)
            add(NTASK - 1, 0, (NPAIR + 1) * 16 * TC)

        @block.tensor
        def _(pe):
            MM, TR = nc.tensor.matmul, nc.tensor.transpose
            ident = c("ident")

            def rows_in(p, loads):
                pe.wait_ge(ld_x[p], loads)
                for kk in range(2):
                    for q in range(TC):
                        last = TR(X[kk][0:KD, q * 128:(q + 1) * 128], xr[:, p, q, kk * KD:(kk + 1) * KD], ident)
                last.then_inc(tr, 1)

            def up(j, p, loads):
                pe.wait_ge(xt_a, j + 1)
                pe.wait_ge(xt_d, j + 1)
                pe.wait_ge(ld_w[p], loads)
                for m in range(NM):
                    if m >= 4:
                        pe.wait_ge(gelu, j * NM + (m - 3))
                    for kk in range(2):
                        last = MM(UP[m % 4][:, 0:T], w1[:, p, kk, m::NM], xt[:, p, kk, :], start=(kk == 0), stop=(kk == 1))
                    last.then_inc(l1, 1)
                pe.wait_ge(l1, j * NM + NM)
                pe.sem_inc(w1_free, 1)

            def down(j, p):
                pe.wait_ge(gelu, j * NM + NM)
                for q in range(TC):
                    if q >= 2:
                        pe.wait_ge(y_add, j * TC + (q - 1))
                    for m in range(NM):
                        last = MM(DOWN[q % 2][:, 0:D], hid[:, p, m, q * 128:(q + 1) * 128], w2[:, p, m, :],
                                  start=(m == 0), stop=(m == NM - 1))
                    last.then_inc(l2, 1)
                pe.wait_ge(y_add, j * TC + TC)
                pe.sem_inc(w2_free, 1)
            rows_in(0, 16)
            with pe.Fori(0, NPAIR) as i:
                for p in range(2):
                    up(i * 2 + p, p, i * 64 + 64)
                    rows_in(1 - p, i * 16 + 16 * (p + 1))
                    down(i * 2 + p, p)
            up(NTASK - 1, 0, (NPAIR + 1) * 64)
            down(NTASK - 1, 0)


def program(nc, I, out):
    with ExitStack() as ctx:
        mem = Memory(nc, ctx)
        patches(nc, mem, I)
        sequences(nc, mem, I, out)
        experts(nc, mem, I, out)


_INS = {"x": "x", "txt": "txt"}
_INS |= {"L0_" + n: n for n in ["tok_W", "tok_b"] + ["attn_" + n for n in (
    "ln_w", "w_comp", "w_qkv", "w_reso", "qn_w", "kn_w", "w_outgate", "head_decay", "temperature", "w_proj", "memn_w",
    "ffn_ln_w", "w1", "w2", "w3")] + ["ffn_" + n for n in ("router_w", "w1", "b1", "w2", "b2")]}


def kernel(**inputs):
    import numpy as _np
    import concourse.bacc as _bacc
    from concourse import mybir as _mybir
    from concourse.bass_utils import run_bass_kernel_spmd as _run

    nc = _bacc.Bacc("TRN2", target_bir_lowering=False, num_devices=1)
    arrays = {f"in_{short}": _np.ascontiguousarray(inputs[name]) for name, short in _INS.items()}
    arrays["in_const"] = CONST
    aps = {k[3:]: nc.dram_tensor(k, a.shape, _mybir.dt.from_np(a.dtype), kind="ExternalInput").ap() for k, a in arrays.items()}
    out = nc.dram_tensor("out", (NTOK + T, D), _mybir.dt.float32, kind="ExternalOutput").ap()
    program(nc, aps, out)
    r = _run(nc, [arrays], core_ids=[0])
    return r.results[0]["out"][:NTOK].reshape(B, L, D)
```

```python
import concourse.bass as bass
from concourse import mybir
from contextlib import ExitStack
import numpy as np

B, IMG, P16, CIN, D = 32, 224, 16, 3, 192
G = IMG // P16
NPATCH, NTXT = G * G, 77
L = NPATCH + NTXT
CH = 91
NCH = L // CH
H, DH = 12, 16
GR = 3
KD = 96
LAT, HID = 128, 512
E, F = 8, 768
NTOK = B * L
T = 384
TC = T // 128
CAP = NTOK + T
NTASK = (2 * NTOK + E * (T - 1)) // T
IDLE = NTASK - (2 * NTOK + T - 1) // T
ROW = D + 2
VE = DH + 1
NQK, NPAR = 2 * D, 4 * H
NREST = NPAR + 2 * D
CW = 96
RSTEPS = (NTOK + T - 1) // T
assert L == CH * NCH and H == 4 * GR and D == 2 * KD and 128 % P16 == 0

f32, i32, u32, f32r = mybir.dt.float32, mybir.dt.int32, mybir.dt.uint32, mybir.dt.float32r
ALU, ACT, AX = mybir.AluOpType, mybir.ActivationFunctionType, mybir.AxisListType

_nodes = 2 + 2 * np.cos(np.pi * (np.arange(400) + 0.5) / 400)
COS_POLY = [float(c) for c in np.polynomial.chebyshev.Chebyshev.fit(
    _nodes, np.cos(np.pi / 2 * np.sqrt(_nodes)), 7, domain=[0, 4]).convert(kind=np.polynomial.Polynomial).coef]


def constants():
    parts = {}
    s, t = np.arange(CH)[:, None], np.arange(CH)[None, :]
    parts["ident"] = np.eye(128)
    parts["causal"] = (s <= t)
    parts["before"] = (s < t)
    parts["ones"] = np.ones((CH, CH))
    slot = np.arange(128)[:, None] // 32
    parts["headblock"] = slot == (np.arange(4 * VE)[None, :] // VE)
    inv = 1.0 / 10000.0 ** (np.arange(0, DH, 2, dtype=np.float32) / np.float32(DH))
    pos = np.arange(L, dtype=np.float32)
    ang = np.outer(pos, inv.astype(np.float32)).astype(np.float32)
    cos, sin = np.cos(ang), np.sin(ang)
    tok = lambda a: a.reshape(NCH, CH, -1).transpose(1, 0, 2).reshape(CH, -1)
    parts["cos"] = tok(np.concatenate([cos, cos], 1))
    parts["sin"] = tok(np.concatenate([-sin, sin], 1))
    parts["pos1"] = tok((pos + 1)[:, None])
    parts["tokno"] = tok(pos[:, None])
    px = np.arange(128) % P16
    parts["right_half"] = (px >= P16 // 2)[:, None]
    parts["left_half"] = (px < P16 // 2)[:, None]
    parts["expert"] = np.tile(np.arange(E), (128, 1))
    parts["base"] = np.tile(np.arange(E) * CAP, (128, NCH))
    parts["steps"] = np.tile(np.arange(RSTEPS) * T, (1, 1))
    parts["upto"] = np.tril(np.ones((E, E))).reshape(1, -1)
    parts["task"] = np.arange(NTASK)[None, :]
    parts["padid"] = NTOK + np.arange(128)[:, None] + 128 * np.arange(TC)[None, :]
    at, cols = {}, []
    n = 0
    for k, a in parts.items():
        a = np.asarray(a, np.float32)
        full = np.zeros((128, a.shape[1]), np.float32)
        full[:a.shape[0]] = a
        at[k] = (n, n + a.shape[1])
        n += a.shape[1]
        cols.append(full)
    return np.concatenate(cols, 1), at


CONST, CONST_AT = constants()


class Memory:

    def __init__(self, nc, ctx):
        self.nc, self.ctx = nc, ctx
        self.psum = ctx.enter_context(nc.psum_tensor("psum", [128, 8, 512], f32))
        self.ps = [self.psum[:, k, :] for k in range(8)]
        self.X, self.Y = self.ps[:4], [self.ps[4:6], self.ps[6:8]]
        self.cst = self.sb("cst", [128, CONST.shape[1]])
        self.pad = self.sb("idle_rows", [128, TC, ROW])
        self.base = self.sb("expert_fill", [CH, NCH, E])
        self.table = self.sb("task_table", [1, 2, NTASK], i32)
        self.ld = self.sem("block_weights_loaded")
        self.wcomp, self.wproj = self.sb("w_comp", [KD, 2, LAT]), self.sb("w_proj", [KD, 2, D])
        self.wlat = self.sb("w_latent", [LAT, NQK + NREST])
        self.w12, self.w3 = self.sb("w_12", [KD, 2, 2, HID]), self.sb("w_3", [128, HID // 128, D])
        self.wr = self.sb("w_router", [KD, 2, CW])
        self.lnw = self.sb("norm_weights", [KD, 3, 2])
        self.qkw = self.sb("qk_norm_w", [CH, 2, DH])
        self.temp, self.decay = self.sb("temperature", [CH, 1]), self.sb("decay", [CH, H])
        self.h0 = nc.dram_tensor("tokens", (B + 2, L, D), f32, kind="Internal").ap()
        self.xs = nc.dram_tensor("dispatched", (E * CAP + T * (IDLE + 1), ROW), f32, kind="Internal").ap()

    def sb(self, name, shape, dt=f32):
        return self.ctx.enter_context(self.nc.sbuf_tensor(name, shape, dt))

    def sem(self, name):
        return self.ctx.enter_context(self.nc.semaphore(name))

    def c(self, name, p=128):
        a, b = CONST_AT[name]
        return self.cst[0:p, a:b]


def patches(nc, mem, I):
    NG, HALF, WH = 4, G // 2, IMG * CIN // 2
    with ExitStack() as ctx:
        mem.ctx = ctx
        sb, sem, X, Y = mem.sb, mem.sem, mem.X, mem.Y
        xi = [sb(f"pixels{i}", [128, P16, WH]) for i in range(2)]
        wr = sb("w_raw", [128, 2, 5, CIN * D])
        wv = sb("w_class", [128, 2, 2, 3, CIN * D])
        tmp, tmp_e = sb("w_tmp", [128, 4, CIN * D]), sb("w_tmp_edge", [128, 2, CIN * D])
        xt = sb("pixels_t", [128, 2, 2, CIN * 128])
        xp = sb("pixels_packed", [128, 2, CIN * P16 * P16])
        os_ = [sb(f"emb{i}", [128, HALF * D]) for i in range(2)]
        bias = sb("tok_bias", [128, D])
        ld_w, ld_c = sem("tok_w_loaded"), sem("const_loaded")
        ld_x = [sem(f"pixels_loaded{i}") for i in range(2)]
        xi_free, w_ready, wstep = sem("pixels_free"), sem("w_class_ready"), sem("w_step")
        tp, ev_a, ev_d, mm, ob = (sem("pix_transposed"), sem("pix_copied_act"), sem("pix_copied_dve"),
                                  sem("emb_done"), sem("emb_copied"))
        packed, edge_step, w_step = sem("pix_packed"), sem("w_edge_step"), sem("block_weight_step")
        os_free, st = sem("emb_free"), [sem(f"emb_stored{i}") for i in range(2)]
        st_txt = sem("txt_copied")
        NT, U = 3, G
        xr = I["x"].rearrange("b (gy py) w c -> b gy py (w c)", py=P16)
        h0 = mem.h0
        block = ctx.enter_context(nc.Block())

        @block.sync
        def _(sp):
            sp.dma_start(mem.cst[:, :], I["const"]).then_inc(ld_c, 16)
            for hh in range(2):
                for k in range(5):
                    src = I["tok_W"].rearrange("(h p k c) d -> h k p c d", h=2, k=5, c=CIN)[hh, k]
                    sp.dma_start(wr[:, hh, k, :].rearrange("p (c d) -> p c d", c=CIN), src).then_inc(ld_w, 16)
            sp.dma_start(bias[:, :], I["tok_b"].partition_broadcast(128)).then_inc(ld_w, 16)

            def load(half, rows):
                for g, gy in enumerate(rows):
                    sp.dma_start(xi[half][32 * g:32 * g + 32, :, :],
                                 xr[:, gy, :, half * WH:(half + 1) * WH]).then_inc(ld_x[half], 16)

            def store(half, rows):
                for g, gy in enumerate(rows):
                    dst = h0[0:B, bass.ds(gy * G + half * HALF, HALF), :].rearrange("b l d -> b (l d)")
                    sp.dma_start(dst, os_[half][32 * g:32 * g + 32, :]).then_inc(st[half], 16)

            for half in range(2):
                load(half, [1 + g for g in range(NG)])
            sp.dma_start(h0[0:B, NPATCH:L, :], I["txt"]).then_inc(st_txt, 16)
            sp.dma_start(h0[B:B + 2, :, :].rearrange("b l d -> (b l d)"),
                         I["txt"].rearrange("b l d -> (b l d)")[0:2 * L * D]).then_inc(st_txt, 16)
            def w(dst, src, **how):
                sp.dma_start(dst, src, **how).then_inc(mem.ld, 16)
            w(mem.wcomp[:, :, :], I["attn_w_comp"].rearrange("(k p) n -> p k n", k=2))
            w(mem.wproj[:, :, :], I["attn_w_proj"].rearrange("(k p) n -> p k n", k=2))
            w(mem.wlat[:, 0:NQK], I["attn_w_qkv"][:, 0:NQK])
            w(mem.wlat[:, NQK:NQK + NPAR], I["attn_w_reso"])
            w(mem.wlat[:, NQK + NPAR:NQK + NPAR + D], I["attn_w_outgate"])
            w(mem.wlat[:, NQK + NPAR + D:], I["attn_w_qkv"][:, NQK:])
            w(mem.w12[:, :, 0, :], I["attn_w1"].rearrange("(k p) n -> p k n", k=2))
            w(mem.w12[:, :, 1, :], I["attn_w2"].rearrange("(k p) n -> p k n", k=2))
            w(mem.w3[:, :, :], I["attn_w3"].rearrange("(k p) n -> p k n", p=128))
            for k in range(2):
                w(mem.wr[:, k, 0:E], I["ffn_router_w"].rearrange("e (k p) -> k p e", k=2)[k], allow_slow_non_contiguous=True)
            for j, n in enumerate(("attn_ln_w", "attn_memn_w", "attn_ffn_ln_w")):
                w(mem.lnw[:, j, :], I[n].rearrange("(k p) -> p k", k=2), allow_slow_non_contiguous=True)
            w(mem.qkw[:, 0, :], I["attn_qn_w"].partition_broadcast(CH))
            w(mem.qkw[:, 1, :], I["attn_kn_w"].partition_broadcast(CH))
            w(mem.temp[:, :], I["attn_temperature"].partition_broadcast(CH))
            w(mem.decay[:, :], I["attn_head_decay"].partition_broadcast(CH))
            with sp.Fori(0, NT - 1) as t:
                for half in range(2):
                    sp.wait_ge(xi_free, t * 2 + half + 1)
                    load(half, [t * NG + 5 + g for g in range(NG)])
                for half in range(2):
                    sp.wait_ge(ob, t * U + (half + 1) * HALF)
                    store(half, [t * NG + 1 + g for g in range(NG)])
                    sp.wait_ge(st[half], (t + 1) * NG * 16)
                    sp.sem_inc(os_free, 1)
            edges = [0, G - 1]
            for half in range(2):
                sp.wait_ge(xi_free, 2 * (NT - 1) + half + 1)
                load(half, edges)
            for half in range(2):
                sp.wait_ge(ob, (NT - 1) * U + (half + 1) * HALF)
                store(half, [(NT - 1) * NG + 1 + g for g in range(NG)])
                sp.wait_ge(st[half], NT * NG * 16)
                sp.sem_inc(os_free, 1)
            for half in range(2):
                sp.wait_ge(ob, NT * U + (half + 1) * HALF)
                store(half, edges)
            for half in range(2):
                sp.wait_ge(st[half], (NT * NG + 2) * 16)
            sp.wait_ge(st_txt, 32)

        @block.vector
        def _(dve):
            dve.wait_ge(ld_c, 16)
            dve.wait_ge(ld_w, 16 * 11)
            n = 0

            def step(ins):
                ins.then_inc(wstep, 1)
                dve.wait_ge(wstep, n + 1)
                return n + 1

            add = lambda o, a, b: nc.vector.tensor_tensor(o, a, b, ALU.add)
            mask_add = lambda o, a, m, b: nc.vector.scalar_tensor_tensor(o, a, mem.c(m), b, ALU.mult, ALU.add)
            for hh in range(2):
                w0, w00, w80, w08, w88 = [wr[:, hh, k, :] for k in range(5)]
                o, a0, a8 = wv[:, hh, 0], tmp[:, 0, :], tmp[:, 1, :]
                n = step(add(a0, w00, w80))
                n = step(add(a8, w08, w88))
                n = step(add(tmp[:, 2, :], w0, a0))
                n = step(add(tmp[:, 3, :], w0, a8))
                n = step(add(o[:, 1, :], tmp[:, 2, :], a8))
                n = step(mask_add(o[:, 0, :], a8, "right_half", tmp[:, 2, :]))
                n = step(mask_add(o[:, 2, :], a0, "left_half", tmp[:, 3, :]))
            dve.sem_inc(w_ready, 1)

            def tile(base, rows, edge, os_wait):
                def copy_out(u):
                    half, at = u // HALF, u % HALF
                    if at == 0 and os_wait is not None:
                        dve.wait_ge(os_free, os_wait + half)
                    dve.wait_ge(mm, base + u + 1)
                    nc.vector.tensor_tensor(os_[half][0:rows, at * D:(at + 1) * D],
                                            Y[(u // 2) % 2][u % 2][0:rows, 0:D],
                                            bias[0:rows, :], ALU.add).then_inc(ob, 1)
                for u in range(U):
                    dve.wait_ge(tp, base + u + 1)
                    nc.vector.tensor_copy(xt[:, u % 2, 1, :].rearrange("p (c r) -> p c r", c=CIN)[:, :, 0:rows],
                                          X[2 * (u % 2) + 1][:, 0:CIN * 128].rearrange("p (c r) -> p c r", c=CIN)[:, :, 0:rows]
                                          ).then_inc(ev_d, 1)
                    if u:
                        copy_out(u - 1)
                copy_out(U - 1)
            dve.sem_inc(os_free, 2)
            with dve.Fori(0, NT) as t:
                tile(t * U, 128, False, t * 2 + 1)
            tile(NT * U, 64, True, NT * 2 + 1)

        @block.scalar
        def _(act):
            def tile(base, loads, rows):
                def pack(u):
                    half, at = u // HALF, u % HALF
                    if at == 0:
                        act.wait_ge(ld_x[half], loads)
                    src = xi[half][0:rows, :, at * 48:(at + 1) * 48].rearrange("p y (x c) -> p c y x", c=CIN)
                    nc.scalar.activation(xp[0:rows, u % 2, :].rearrange("p (c y x) -> p c y x", c=CIN, y=P16),
                                         src, ACT.Copy).then_inc(packed, 1)
                    if at == HALF - 1:
                        act.wait_ge(packed, base + u + 1)
                        act.sem_inc(xi_free, 1)
                pack(0)
                pack(1)
                for u in range(U):
                    act.wait_ge(tp, base + u + 1)
                    nc.scalar.activation(xt[:, u % 2, 0, :].rearrange("p (c r) -> p c r", c=CIN)[:, :, 0:rows],
                                         X[2 * (u % 2)][:, 0:CIN * 128].rearrange("p (c r) -> p c r", c=CIN)[:, :, 0:rows],
                                         ACT.Copy).then_inc(ev_a, 1)
                    if u + 2 < U:
                        pack(u + 2)
            with act.Fori(0, NT) as t:
                tile(t * U, t * (16 * NG) + 16 * NG, 128)
            tile(NT * U, 16 * (NT * NG + 2), 64)

        @block.gpsimd
        def _(pool):
            PO = nc.gpsimd
            n = [0, 0]

            def step(ins, of=0):
                which = (edge_step, w_step)[of]
                ins.then_inc(which, 1)
                n[of] += 1
                pool.wait_ge(which, n[of])
            pool.wait_ge(ld_c, 16)
            pool.wait_ge(ld_w, 16 * 11)
            for hh in range(2):
                w0 = wr[:, hh, 0, :]
                a0, a8 = [wr[:, hh, k, :] for k in ((1, 3) if hh == 0 else (2, 4))]
                o = wv[:, hh, 1]
                step(PO.tensor_tensor(tmp_e[:, 0, :], w0, a0, ALU.add))
                step(PO.tensor_tensor(o[:, 1, :], tmp_e[:, 0, :], a8, ALU.add))
                step(PO.tensor_scalar(tmp_e[:, 1, :], a8, mem.c("right_half"), None, ALU.mult))
                step(PO.tensor_tensor(o[:, 0, :], tmp_e[:, 0, :], tmp_e[:, 1, :], ALU.add))
                step(PO.tensor_tensor(tmp_e[:, 0, :], w0, a8, ALU.add))
                step(PO.tensor_scalar(tmp_e[:, 1, :], a0, mem.c("left_half"), None, ALU.mult))
                step(PO.tensor_tensor(o[:, 2, :], tmp_e[:, 0, :], tmp_e[:, 1, :], ALU.add))
            pool.wait_ge(mem.ld, 16 * 18)
            wcomp, wproj, wlat, w12, w3, lnw = mem.wcomp, mem.wproj, mem.wlat, mem.w12, mem.w3, mem.lnw
            scale = lambda t, by: step(PO.tensor_scalar(t, t, by, None, ALU.mult), 1)
            for k in range(2):
                scale(wcomp[:, k, :], lnw[:, 0, k:k + 1])
                scale(wproj[:, k, :], lnw[:, 1, k:k + 1])
                for j in range(2):
                    scale(w12[:, k, j, :], lnw[:, 2, k:k + 1])
            scale(wproj[:, :, :], 0.5)
            scale(wlat[:, :], 0.5)
            scale(w3[:, :, :], 0.5)
            scale(mem.temp[:, :], 0.125)
            step(PO.memset(mem.wr[:, :, E:], 0.0), 1)

        @block.tensor
        def _(pe):
            pe.wait_ge(ld_c, 16)
            ident = mem.c("ident")

            def transposes(u, base, rows):
                pe.wait_ge(packed, base + u + 1)
                for hh in range(2):
                    for c in range(CIN):
                        src = xp[0:rows, u % 2, (2 * c + hh) * 128:(2 * c + hh + 1) * 128]
                        last = nc.tensor.transpose(X[2 * (u % 2) + hh][:, c * 128:c * 128 + rows], src,
                                                   ident[0:rows, 0:rows])
                last.then_inc(tp, 1)

            def products(u, base, rows, edge):
                pe.wait_ge(ev_a, base + u + 1)
                pe.wait_ge(ev_d, base + u + 1)
                col = 0 if u == 0 else 2 if u == G - 1 else 1
                bank = Y[(u // 2) % 2][u % 2]
                parts = [(0, 32, (1, 0)), (32, 64, (0, 1))] if edge else [(0, rows, (0, 0))]
                for r0, r1, rowclass in parts:
                    for k in range(2 * CIN):
                        hh, c = k // CIN, k % CIN
                        last = nc.tensor.matmul(bank[r0:r1, 0:D],
                                                xt[:, u % 2, hh, c * 128 + r0:c * 128 + r1],
                                                wv[:, hh, rowclass[hh], col, c * D:(c + 1) * D],
                                                start=(k == 0), stop=(k == 2 * CIN - 1))
                last.then_inc(mm, 1)

            def tile(base, rows, edge):
                transposes(0, base, rows)
                for u in range(U):
                    if u + 1 < U:
                        transposes(u + 1, base, rows)
                    products(u, base, rows, edge)
            pe.wait_ge(w_ready, 1)
            with pe.Fori(0, NT) as t:
                tile(t * U, 128, False)
            pe.wait_ge(edge_step, 14)
            tile(NT * U, 64, True)



def sequences(nc, mem, I, out):
    NP = B // 2
    SCALE_MEAN = float(D) ** -0.5
    LP = L + CW - CH
    SC, REST, QK, FB = (0, 1, 4, 5), (4, 5, 6), (7, 4, 5), (0, 4, 6, 0)
    with ExitStack() as ctx:
        mem.ctx = ctx
        sb, sem, X, Y, c = mem.sb, mem.sem, mem.X, mem.Y, mem.c
        wcomp, wproj, wlat, w12, w3, wr = mem.wcomp, mem.wproj, mem.wlat, mem.w12, mem.w3, mem.wr
        qkw, temp, decay, logd = mem.qkw, mem.temp, mem.decay, sb("log_decay", [CH, H])
        COS, SIN = sb("cos_w", [CH, NCH, 2, DH]), sb("sin_w", [CH, NCH, 2, DH])
        df, idf = sb("decay_to", [CH, NCH, H]), sb("decay_from", [CH, NCH, H])
        mhalf = sb("minus_half", [CH, NCH * 2 * H])
        tokno, base, pad_x = sb("token_number", [CH, NCH]), mem.base, mem.pad
        hh, xln, g2, h2 = [sb(n, [CH, 2, NCH, D]) for n in ("h", "x_ln", "out_gate", "h2")]
        xn, xn2, v, hx = [sb(n, [CH, NCH, D]) for n in ("x_n", "x_n2", "v", "h_plus_x1")]
        att, x1 = sb("att", [CH, 2, NCH, D + 1]), sb("x1", [CH, NCH, D + 1])
        xt, xb = sb("x_t", [KD, 2, L]), sb("back_t", [KD, 2, L])
        stat, mv = sb("bn", [CH, 2, NCH, 6]), sb("mean_var", [CH, 2, NCH, 2])
        nm, nb = sb("minus_mean", [CH, 2, NCH]), sb("norm_bias", [CH, 2, NCH])
        ve2, rs = sb("var_eps", [CH, 2, 2 * NCH]), sb("rstd", [CH, 2, 2 * NCH])
        tl, lat = sb("tanh_latent", [LAT, L]), sb("latent", [LAT, L])
        tg = sb("tanh_rest", [CH, NCH, NPAR + D])
        gt = sb("gate_tmp", [CH, 6, NCH * H])
        ve = sb("v_ext", [CH, NCH, H, 32])
        qa, qb, qc, qd = [sb(n, [CH, NCH * NQK]) for n in ("qk", "qk_sq", "qk_rot", "qk_partner_sin")]
        ss, rq, nt = sb("qk_ss", [CH, NCH * 2 * H]), sb("qk_rstd", [CH, NCH * 2 * H]), sb("newton", [CH, NCH * 2 * H])
        qf = sb("qk_feat", [CH, NCH * 2 * H, 32])
        qt = sb("qk_feat_t", [128, 2, GR, LP])
        states = sb("states", [128, 2, GR, 4, 32])
        sm = sb("scores", [CH, 2, 4, GR * CH])
        ot = sb("att_sum_t", [128, NCH, GR * CH])
        dn, limit = sb("den", [CH, NCH, H]), sb("den_limit", [CH, NCH, H])
        sa, rr = sb("mean_square", [CH, 2, NCH]), sb("rstd2", [CH, 2, NCH])
        junk = sb("squares", [CH, 2, NCH, D + 1])
        th, hid = sb("tanh_h1", [128, HID // 128, L]), sb("ffn_hidden", [128, HID // 128, L])
        row = sb("rows", [CH, 2, 2, NCH, ROW])
        lg = sb("logits", [CH, NCH, E])
        mx, mi = sb("top_logits", [CH, NCH, 8]), sb("top_experts", [CH, NCH, 8], u32)
        tf, oh = sb("top_f", [CH, NCH, 2]), sb("one_hot", [CH, NCH, 2, E])
        ohs, rk = sb("picked", [CH, NCH, E]), sb("rank", [CH, NCH, E])
        rp, de = sb("rank_picked", [CH, NCH, 2, E]), sb("dest_f", [CH, NCH, 2])
        di = sb("dest", [CH, 2, NCH, 2], i32)
        ew = sb("top_w", [CH, 2, NCH])
        zeros = sb("zeros", [128, 512], mybir.dt.bfloat16)

        cnt, tiles, cum = sb("count", [1, E]), sb("tiles", [1, E]), sb("tiles_upto", [1, E])
        cmp_, mix = sb("over_steps", [1, E, RSTEPS]), sb("mix", [1, E, E])
        ind, indt = sb("expert_past", [1, NTASK, E]), sb("expert_past_tiles", [1, NTASK, E])
        ej, bef, off = sb("task_expert_f", [1, NTASK]), sb("task_before", [1, NTASK]), sb("task_row_f", [1, NTASK])
        table, tail = mem.table, sb("tail_row", [1, E], i32)
        table_ready, tails = sem("table_ready"), sem("tails_stored")
        cleared, setup, tables, act_tables = sem("buffers_cleared"), sem("setup_step"), sem("tables_ready"), sem("act_tables")
        ld_h, st_h, sent = ([sem(f"{n}{b}") for b in range(2)] for n in ("h_loaded", "h2_stored", "rows_sent"))
        st_pad, pad_ready = sem("idle_rows_stored"), sem("idle_rows_ready")
        h_used, h2_free, row_free = sem("h_used"), sem("h2_free"), sem("rows_free")
        var_done, rstd_step, rstd_done, xln_done, xn_done = (
            sem(n) for n in ("var", "rstd_step", "rstd_done", "xln_done", "xn_done"))
        xn_t, xt_done = sem("xn_transposed"), sem("xt_copied")
        lat_mm, lat_th, lat_done = sem("latent_mm"), sem("latent_tanh"), sem("latent_done")
        rest_mm, rest_a, rest_d = sem("rest_mm"), sem("rest_act"), sem("rest_dve")
        qk_mm, qk_sq = sem("qk_mm"), sem("qk_squared")
        qk_sin, qk_cos, qk_sum, qk_rot, qk_exp, qf_done = sem("qk_partner_sin_done"), sem("qk_times_cos"), sem("qk_cos_plus_sin"), sem("qk_rotated"), sem("qk_exp"), sem("qk_features")
        gate_arg, gate_th, gate_w, ve_done = sem("gate_arg"), sem("gate_tanh"), sem("gate_weights"), sem("v_weighted")
        tq_mm, tq_a = sem("qk_transposed"), sem("qkt_copied")
        st_mm, st_d, sc_mm, sc_d, pv_mm = sem("state_mm"), sem("state_masked"), sem("score_mm"), sem("score_masked"), sem("pv_mm")
        ot_a, ot_mm = sem("att_sum_copied"), sem("att_sum_transposed")
        att_done, att_ss, att_rs = sem("att_done"), sem("att_sumsq"), sem("att_rstd")
        at_t, at_a, pr_mm, pr_d = sem("att_transposed"), sem("att_t_copied"), sem("proj_mm"), sem("proj_gated")
        x1_done, x1_ss, x1_rs, xn2_done = sem("x1_done"), sem("x1_sumsq"), sem("x1_rstd"), sem("xn2_done")
        x2_t, x2_a = sem("xn2_transposed"), sem("xn2_t_copied")
        f_mm, f_th, f_d, w3_mm, h2_done = sem("ffn_mm"), sem("ffn_tanh"), sem("ffn_hidden_done"), sem("ffn_out_mm"), sem("h2_done")
        var2_done, rstd2_done, flat_done = sem("var2"), sem("rstd2_done"), sem("flat_done")
        fl_t, fl_a, lg_mm = sem("flat_transposed"), sem("flat_t_copied"), sem("logits_mm")
        top_done, ew_exp, oh_done, rk_mm, rk_read, dest_done = (sem("top_done"), sem("top_exp"), sem("one_hot_done"), sem("rank_mm"),
                                                                sem("rank_read"), sem("dest_done"))
        waited = sem("waits_apart")
        ln_step, front_step, back_step = sem("norm_step"), sem("front_step"), sem("back_step")
        row_copied = sem("row_copied")
        tok_step, rows_numbered = sem("token_step"), sem("rows_numbered")
        block = ctx.enter_context(nc.Block())
        bank = mem.ps
        two = lambda k, n: mem.psum[0:KD, k:k + 2, 0:n]

        def apart(eng):
            eng.sem_inc(waited, 1)

        def waiter(eng, n):
            return lambda s, k=0, per=1: eng.wait_ge(s, n * per + (k + 1))

        @block.sync
        def _(sp):
            def load(b, n):
                sp.dma_start(hh[:, b], mem.h0[n].rearrange("(c p) d -> p c d", c=NCH)).then_inc(ld_h[b], 16)
            load(0, 0)
            load(1, 1)
            sp.wait_ge(pad_ready, 1)
            for k in range(IDLE + 1):
                sp.dma_start(mem.xs[E * CAP + k * T:E * CAP + (k + 1) * T, :].rearrange("(c p) d -> p c d", c=TC),
                             pad_x[:, :, :]).then_inc(st_pad, 16)
            sp.dma_start(out[NTOK:NTOK + T, :].rearrange("(c p) d -> p c d", c=TC), pad_x[:, :, 0:D]).then_inc(st_pad, 16)
            with sp.Fori(0, NP) as i:
                for b in range(2):
                    n = i * 2 + b
                    wait = waiter(sp, n)
                    wait(h_used)
                    sp.dma_start(hh[:, b], mem.h0[bass.ds(i * 2 + (b + 2), 1), :, :].rearrange(
                        "o (c p) d -> p (o c) d", c=NCH)).then_inc(ld_h[b], 16)
                    wait(h2_done)
                    sp.dma_start(out[bass.ds(i * (2 * L) + b * L, L), :].rearrange("(c p) d -> p c d", c=NCH),
                                 h2[:, b]).then_inc(st_h[b], 16)
                    sp.wait_ge(st_h[b], i * 16 + 16)
                    sp.sem_inc(h2_free, 1)
            sp.wait_ge(table_ready, 1)
            for e in range(E):
                r = sp.value_load(tail[0:1, e:e + 1], min_val=0, max_val=E * CAP - T)
                sp.dma_start(mem.xs[bass.ds(r, T), :].rearrange("(c p) d -> p c d", c=TC), mem.pad[:, :, :]).then_inc(tails, 16)
            for b in range(2):
                sp.wait_ge(ld_h[b], 16 * (NP + 1))
            sp.wait_ge(st_pad, 16 * (IDLE + 2))
            sp.wait_ge(tails, 16 * E)

        @block.vector
        def _(dve):
            V = nc.vector
            n = [0]

            def s(ins):
                ins.then_inc(setup, 1)
                n[0] += 1
                dve.wait_ge(setup, n[0])
            s(V.memset(ve[:, :, :, :], 0.0))
            s(V.memset(qt[:, :, :, L:], 0.0))
            s(V.memset(att[:, :, :, D], (1e-6 * D) ** 0.5))
            s(V.memset(x1[:, :, D], (1e-6 * D) ** 0.5))
            s(V.tensor_scalar(tokno[:, :], c("tokno", CH), float(-L), None, ALU.add))
            s(V.tensor_copy(base[:, :, :].rearrange("p c e -> p (c e)"), c("base", CH)))
            dve.sem_inc(rk_read, 1)
            def stats(src, j, s_, count):
                for q in range(NCH):
                    last = V.bn_stats(stat[:, j, q, :], src[:, q, :])
                last.then_inc(s_, 1)
                dve.wait_ge(s_, count)
                apart(dve)
                for q in range(NCH):
                    last = V.bn_aggr(mv[:, j, q, :], stat[:, j, q, :])
                last.then_inc(s_, 1)
                dve.wait_ge(s_, count + 1)

            def norm_in(n, lane, loads):
                dve.wait_ge(ld_h[lane], loads)
                stats(hh[:, lane], 0, ln_step, n * 2 + 1)
                V.tensor_scalar(ve2[:, 0, 0:NCH], mv[:, 0, :, 1], 1e-5, None, ALU.add)
                V.tensor_scalar(ve2[:, 0, NCH:], mv[:, 0, :, 1], 1.0 + 1e-6, 1e-11, ALU.mult, ALU.add)
                V.tensor_scalar(nm[:, :, :], mv[:, 0, :, 0].unsqueeze(1).to_broadcast([CH, 2, NCH]), -1.0, None, ALU.mult).then_inc(var_done, 1)
            norm_in(0, 0, 16)

            s(V.memset(pad_x[:, :, :], 0.0))
            V.tensor_copy(pad_x[:, :, D], c("padid")).then_inc(pad_ready, 1)
            cosc, sinc = [c(k, CH).rearrange("p (c d) -> p c d", c=NCH) for k in ("cos", "sin")]
            s(V.tensor_scalar(qkw[:, :, :], qkw[:, :, :], 9.0 / 64.0, None, ALU.mult))
            for k in range(2):
                wb = qkw[:, k, :].unsqueeze(1).to_broadcast([CH, NCH, DH])
                s(V.tensor_tensor(COS[:, :, k, :], cosc, wb, ALU.mult))
                for half in range(2):
                    o = slice(half * 8, half * 8 + 8)
                    wp = qkw[:, k, 8 - half * 8:16 - half * 8].unsqueeze(1).to_broadcast([CH, NCH, 8])
                    s(V.tensor_tensor(SIN[:, :, k, o], sinc[:, :, o], wp, ALU.mult))
            dve.wait_ge(act_tables, 1)
            s(V.tensor_scalar(decay[:, :], decay[:, :], 0.325, 0.625, ALU.mult, ALU.add))
            s(V.tensor_scalar(decay[:, :], decay[:, :], 1e-5, 0.999, ALU.max, ALU.min))
            dve.sem_inc(tables, 1)
            dve.wait_ge(act_tables, 2 + NCH)
            s(V.tensor_scalar(limit[:, :, :], df[:, :, :], 1e-35, None, ALU.max))
            s(V.reciprocal(limit[:, :, :], limit[:, :, :]))
            s(V.tensor_scalar(limit[:, :, :], limit[:, :, :], 1e-5, None, ALU.mult))
            s(V.tensor_scalar(idf[:, :, :], df[:, :, :], 1e-8, None, ALU.add))
            s(V.reciprocal(idf[:, :, :], idf[:, :, :]))
            s(V.tensor_scalar(decay[:, :], decay[:, :], -1.0, 1.0, ALU.mult, ALU.add))
            s(V.tensor_tensor(idf[:, :, :], idf[:, :, :], decay[:, :].unsqueeze(1).to_broadcast([CH, NCH, H]), ALU.mult))
            s(V.tensor_copy(ve[:, :, :, DH], idf[:, :, :]))
            dve.sem_inc(tables, 1)

            FRONT, BACK = 28, 18

            class Front:

                def __init__(self, n, lane):
                    self.n, self.lane, self.k, self.wait = n, lane, 0, waiter(dve, n)

                def link(self, *instructions, meanwhile=lambda: None):
                    for ins in instructions:
                        ins.then_inc(front_step, 1)
                        self.k += 1
                    meanwhile()
                    dve.wait_ge(front_step, self.n * FRONT + self.k)

                def latent(self):
                    self.wait(lat_th)
                    V.scalar_tensor_tensor(lat[:, :], tl[:, :], 1.0, bank[2][:, 0:L], ALU.add, ALU.mult).then_inc(lat_done, 1)

                def out_gate(self, *chunks):
                    for q in chunks:
                        self.wait(rest_a, q, NCH)
                        V.scalar_tensor_tensor(g2[:, self.lane, q, :], tg[:, q, NPAR:], 1.0,
                                               bank[REST[q]][0:CH, NPAR:NPAR + D], ALU.add, ALU.mult).then_inc(rest_d, 1)

                def gate_argument(self, k=None):
                    self.wait(rest_a, NCH - 1, NCH)
                    par = tg[:, :, 0:NPAR].rearrange("p c (h j) -> p c h j", j=4)
                    g = [gt[:, j, :] for j in range(6)]
                    g3 = lambda a: a.rearrange("p (c h) -> p c h", c=NCH)
                    self.link(V.tensor_tensor(g3(g[0]), par[:, :, :, 1], par[:, :, :, 3], ALU.subtract),
                              V.tensor_scalar(g3(g[3]), par[:, :, :, 2], 1.0, None, ALU.add))
                    self.link(V.tensor_tensor(g[1], g[0], g[0], ALU.mult),
                              V.scalar_tensor_tensor(g3(g[3]), par[:, :, :, 0], 1.0, g3(g[3]), ALU.add, ALU.mult))
                    self.link(V.tensor_scalar(g[2], g[1], COS_POLY[7], None, ALU.mult))
                    for p in range(6, 0, -1):
                        if p == 2 and k:
                            k.norm2()
                        self.link(V.scalar_tensor_tensor(g[2], g[2], COS_POLY[p], g[1], ALU.add, ALU.mult))
                    V.scalar_tensor_tensor(g[2], g[2], COS_POLY[0], g[3], ALU.add, ALU.mult).then_inc(gate_arg, 1)

                def rotate(self, q, half):
                    a, o = [t[:, q * NQK:(q + 1) * NQK].rearrange("p (k h d) -> p k h d", k=2, d=DH) for t in (qa, qd)]
                    o1, o2 = slice(half * 8, half * 8 + 8), slice(8 - half * 8, 16 - half * 8)
                    V.tensor_tensor(o[:, :, :, o1], a[:, :, :, o2],
                                    SIN[:, q, :, o1].unsqueeze(2).to_broadcast([CH, 2, H, 8]), ALU.mult).then_inc(qk_sin, 1)

                def head_norm(self):
                    self.wait(qk_sq, NCH - 1, NCH)
                    rotate = lambda n: lambda: self.rotate(n // 2, n % 2)
                    self.link(V.tensor_reduce(ss[:, :], qb[:, :].rearrange("p (h d) -> p h d", d=DH), AX.X, ALU.add),
                              meanwhile=rotate(0))
                    self.link(V.tensor_scalar(ss[:, :], ss[:, :], 1.0 / DH, 1e-6, ALU.mult, ALU.add), meanwhile=rotate(1))
                    self.link(V.tensor_scalar(rq[:, :].bitcast(i32), ss[:, :].bitcast(i32), -0.5, float(0x5f3759df), ALU.mult, ALU.add),
                              meanwhile=rotate(2))
                    self.link(V.tensor_tensor(nt[:, :], rq[:, :], rq[:, :], ALU.mult), meanwhile=rotate(3))
                    self.link(V.tensor_tensor(nt[:, :], nt[:, :], ss[:, :], ALU.mult), meanwhile=rotate(4))
                    quadratic = lambda: V.scalar_tensor_tensor(nt[:, :], nt[:, :], -10.0 / 3.0, nt[:, :], ALU.add, ALU.mult)
                    better = lambda: V.scalar_tensor_tensor(rq[:, :], nt[:, :], 5.0, rq[:, :], ALU.add, ALU.mult)
                    self.link(quadratic(), meanwhile=rotate(5))
                    self.link(better())
                    self.link(V.tensor_tensor(nt[:, :], rq[:, :], rq[:, :], ALU.mult))
                    self.link(V.scalar_tensor_tensor(nt[:, :], nt[:, :], 9.0 / 64.0, ss[:, :], ALU.mult, ALU.mult))
                    self.link(quadratic())
                    self.link(better())

                def rotated(self):
                    self.wait(qk_sum)
                    for q in range(NCH):
                        x = qc[:, q * NQK:(q + 1) * NQK].rearrange("p (h d) -> p h d", d=DH)
                        V.tensor_tensor(x, x, rq[:, q * 2 * H:(q + 1) * 2 * H].unsqueeze(2).to_broadcast([CH, 2 * H, DH]),
                                        ALU.mult).then_inc(qk_rot, 1)

                def gate(self):
                    self.wait(gate_th)
                    self.link(V.tensor_scalar(gt[:, 4, :], gt[:, 4, :], 0.6, 0.5, ALU.mult, ALU.add))
                    self.link(V.tensor_scalar(gt[:, 4, :], gt[:, 4, :], 0.05, 0.95, ALU.max, ALU.min))
                    V.tensor_tensor(gt[:, 5, :], gt[:, 4, :], idf[:, :, :].rearrange("p c h -> p (c h)"),
                                    ALU.mult).then_inc(gate_w, 1)

                def features(self, q):
                    self.wait(qk_exp, q, NCH)
                    hd = lambda t: t[:, q * NQK:(q + 1) * NQK].rearrange("p (h d) -> p h d", d=DH)
                    V.scalar_tensor_tensor(qf[:, q * 2 * H:(q + 1) * 2 * H, 0:DH], hd(qb), 1.0, hd(qa), ALU.min, ALU.add).then_inc(qf_done, 1)

                def state(self):
                    for k in range(2):
                        self.wait(st_mm, k, 2)
                        V.tensor_tensor(states[:, k, :, :, 0:VE],
                                        bank[6 + k][:, 0:GR * 128].rearrange("p (g r e) -> p g r e", g=GR, r=4)[:, :, :, 0:VE],
                                        c("headblock").rearrange("p (r e) -> p r e", r=4).unsqueeze(1).to_broadcast([128, GR, 4, VE]),
                                        ALU.mult).then_inc(st_d, 1)

                def scores(self, q):
                    for r in range(4):
                        self.wait(sc_mm, 4 * q + r, 4 * NCH)
                        V.tensor_tensor(sm[:, q % 2, r, :].rearrange("p (g t) -> p g t", g=GR),
                                        bank[SC[r]][0:CH, 0:GR * CW].rearrange("p (g t) -> p g t", g=GR)[:, :, 0:CH],
                                        c("causal", CH).unsqueeze(1).to_broadcast([CH, GR, CH]), ALU.mult).then_inc(sc_d, 1)

                def attention(self):
                    for q, n, k in ((0, 2, 0), (2, 1, 6)):
                        self.wait(ot_mm, q // 2, 2)
                        o = mem.psum[0:CH, k:k + n, 0:H * 32].rearrange("p c (h e) -> p c h e", e=32)
                        d = dn[:, q:q + n, :]
                        self.link(V.tensor_tensor(d, o[:, :, :, DH], limit[:, q:q + n, :], ALU.max))
                        self.link(V.reciprocal(d, d))
                        last = V.tensor_tensor(att[:, self.lane, q:q + n, 0:D].rearrange("p c (h d) -> p c h d", d=DH), o[:, :, :, 0:DH],
                                               d.unsqueeze(3).to_broadcast([CH, n, H, DH]), ALU.mult)
                    last.then_inc(att_done, 1)

                def end(self):
                    assert self.k == FRONT, self.k

            class Back:

                def __init__(self, n, lane):
                    self.n, self.lane, self.k, self.wait = n, lane, 0, waiter(dve, n)

                def link(self, ins):
                    ins.then_inc(back_step, 1)
                    self.k += 1
                    dve.wait_ge(back_step, self.n * BACK + self.k)

                def project(self):
                    self.wait(att_rs)
                    self.wait(pr_mm)
                    for q in range(NCH):
                        last = V.scalar_tensor_tensor(x1[:, q, 0:D], bank[2 + q // 2][0:CH, (q % 2) * D:(q % 2 + 1) * D],
                                                      rr[:, 0, q:q + 1], g2[:, self.lane, q, :], ALU.mult, ALU.mult)
                    last.then_inc(pr_d, 1)
                    self.wait(pr_d)
                    self.wait(xln_done)
                    V.tensor_tensor(x1[:, :, 0:D], x1[:, :, 0:D], xln[:, self.lane], ALU.add).then_inc(x1_done, 1)

                def norm2(self):
                    self.wait(x1_rs)
                    for q in range(NCH):
                        last = V.tensor_scalar(xn2[:, q, :], x1[:, q, 0:D], rr[:, 1, q:q + 1], None, ALU.mult)
                    last.then_inc(xn2_done, 1)

                def hidden(self, *tiles):
                    for m in tiles:
                        self.wait(f_th, m, 4)
                        V.scalar_tensor_tensor(hid[:, m, :], th[:, m, :], 1.0, bank[FB[m]][:, 0:L],
                                               ALU.add, ALU.mult).then_inc(back_step, 1)
                        self.k += 1
                    for m in tiles:
                        dve.wait_ge(back_step, self.n * BACK + self.k - (tiles[-1] - m))
                        V.tensor_tensor(hid[:, m, :], hid[:, m, :], bank[FB[m] + 1][:, 0:L], ALU.mult).then_inc(f_d, 1)

                def residual(self):
                    self.wait(h2_free)
                    self.wait(h_used)
                    self.wait(w3_mm)
                    V.tensor_tensor(h2[:, self.lane, 0:3:2, :], hx[:, 0:3:2, :], bank[2][0:CH, 0:2 * D].rearrange("p (c d) -> p c d", c=2), ALU.add)
                    V.tensor_tensor(h2[:, self.lane, 1, :], hx[:, 1, :], bank[3][0:CH, 0:D], ALU.add).then_inc(h2_done, 1)

                def norm_in(self):
                    self.wait(h2_done)
                    stats(h2[:, self.lane], 1, back_step, self.n * BACK + self.k + 1)
                    self.k += 2
                    V.tensor_scalar(ve2[:, 1, 0:NCH], mv[:, 1, :, 1], 1e-5, None, ALU.add).then_inc(var2_done, 1)

                def norm_out(self):
                    self.wait(rstd2_done)
                    self.wait(row_free)
                    for q in range(NCH):
                        last = V.tensor_scalar(row[:, self.lane, 0, q, 0:D], h2[:, self.lane, q, :], mv[:, 1, q, 0:1], rs[:, 1, q:q + 1],
                                               ALU.subtract, ALU.mult)
                    last.then_inc(flat_done, 1)

                def top(self):
                    self.wait(lg_mm)
                    self.link(V.tensor_copy(lg[:, :, :], bank[2][0:CH, 0:NCH * CW].rearrange("p (c e) -> p c e", c=NCH)[:, :, 0:E]))
                    apart(dve)
                    for q in range(NCH):
                        last = V.max(mx[:, q, :], lg[:, q, :])
                    self.link(last)
                    apart(dve)
                    for q in range(NCH):
                        last = V.max_index(mi[:, q, :], mx[:, q, :], lg[:, q, :])
                    self.link(last)
                    V.tensor_tensor(ew[:, 0, :], mx[:, :, 1], mx[:, :, 0], ALU.subtract).then_inc(top_done, 1)
                    self.link(V.tensor_copy(tf[:, :, :], mi[:, :, 0:2]))
                    self.link(V.tensor_tensor(oh[:, :, :, :], c("expert", CH).unsqueeze(1).unsqueeze(1).to_broadcast([CH, NCH, 2, E]),
                                              tf[:, :, :].unsqueeze(3).to_broadcast([CH, NCH, 2, E]), ALU.is_equal))
                    V.tensor_tensor(ohs[:, :, :], oh[:, :, 0, :], oh[:, :, 1, :], ALU.add).then_inc(oh_done, 1)

                def places(self):
                    self.wait(rk_mm)
                    before = bank[3][0:CH, 0:NCH * E].rearrange("p (c e) -> p c e", c=NCH)
                    total = bank[3][0:CH, 32:32 + NCH * E].rearrange("p (c e) -> p c e", c=NCH)
                    self.link(V.tensor_tensor(base[:, 1, :], base[:, 0, :], total[:, 0, :], ALU.add))
                    self.link(V.tensor_tensor(base[:, 2, :], base[:, 1, :], total[:, 1, :], ALU.add))
                    self.link(V.tensor_tensor(rk[:, :, :], before, base[:, :, :], ALU.add))
                    V.tensor_tensor(base[:, 0, :], base[:, 2, :], total[:, 2, :], ALU.add).then_inc(rk_read, 1)
                    self.link(V.tensor_tensor(rp[:, :, :, :], oh[:, :, :, :], rk[:, :, :].unsqueeze(2).to_broadcast([CH, NCH, 2, E]), ALU.mult))
                    self.link(V.tensor_reduce(de[:, :, :], rp[:, :, :, :], AX.X, ALU.add))
                    V.tensor_copy(di[:, self.lane], de[:, :, :])
                    self.wait(ew_exp)
                    self.link(V.tensor_scalar(ew[:, 0, :], ew[:, 1, :], 1.0, None, ALU.add))
                    self.link(V.reciprocal(row[:, self.lane, 0, :, D + 1], ew[:, 0, :]))
                    V.tensor_tensor(row[:, self.lane, 1, :, D + 1], ew[:, 1, :], row[:, self.lane, 0, :, D + 1], ALU.mult).then_inc(dest_done, 1)

                def end(self):
                    assert self.k == BACK, self.k

            f = Front(0, 0)
            dve.wait_ge(cleared, 4)
            f.latent(); f.out_gate(0, 1, 2); f.gate_argument(); f.head_norm(); f.gate(); f.rotated()
            for q in range(NCH):
                f.features(q)
            norm_in(1, 1, 16)
            f.state()
            f.scores(0)
            f.scores(1)
            Front(1, 1).latent()
            f.scores(2)
            f.attention(); f.end()
            with dve.Fori(0, NP) as i:
                for b in range(2):
                    f, k = Front(i * 2 + (b + 1), 1 - b), Back(i * 2 + b, b)
                    f.out_gate(0, 1)
                    k.project()
                    f.out_gate(2)
                    f.gate_argument(k)
                    f.head_norm()
                    k.hidden(0, 1)
                    f.rotated()
                    f.gate()
                    k.hidden(2)
                    for q in range(NCH):
                        f.features(q)
                    k.hidden(3)
                    norm_in(i * 2 + (b + 2), b, i * 16 + 32)
                    k.residual()
                    k.norm_in()
                    f.scores(0)
                    f.state()
                    k.norm_out()
                    f.scores(1)
                    Front(i * 2 + (b + 2), b).latent()
                    f.scores(2)
                    k.top()
                    f.attention()
                    k.places()
                    f.end()
                    k.end()

            dve.wait_ge(rk_read, B + 1)
            first = lambda name, m=None: c(name, 1)[:, 0:m]
            s(V.tensor_tensor(cnt[:, :], mem.base[0:1, 0, :], first("base", E), ALU.subtract))
            s(V.tensor_copy(tail[:, :], mem.base[0:1, 0, :]))
            s(V.tensor_tensor(cmp_[:, :, :], cnt[:, :].unsqueeze(2).to_broadcast([1, E, RSTEPS]),
                              first("steps", RSTEPS).unsqueeze(1).to_broadcast([1, E, RSTEPS]), ALU.is_gt))
            s(V.tensor_reduce(tiles[:, :], cmp_[:, :, :], AX.X, ALU.add))
            s(V.tensor_tensor(mix[:, :, :], tiles[:, :].unsqueeze(1).to_broadcast([1, E, E]),
                              first("upto", E * E).rearrange("o (a b) -> o a b", a=E), ALU.mult))
            s(V.tensor_reduce(cum[:, :], mix[:, :, :], AX.X, ALU.add))
            task = first("task", NTASK)
            s(V.tensor_tensor(ind[:, :, :], cum[:, :].unsqueeze(1).to_broadcast([1, NTASK, E]),
                              task.unsqueeze(2).to_broadcast([1, NTASK, E]), ALU.is_le))
            s(V.tensor_reduce(ej[:, :], ind[:, :, :], AX.X, ALU.add))
            s(V.tensor_tensor(indt[:, :, :], ind[:, :, :], tiles[:, :].unsqueeze(1).to_broadcast([1, NTASK, E]), ALU.mult))
            s(V.tensor_reduce(bef[:, :], indt[:, :, :], AX.X, ALU.add))
            s(V.tensor_tensor(bef[:, :], task, bef[:, :], ALU.subtract))
            s(V.tensor_scalar(bef[:, :], bef[:, :], float(T), None, ALU.mult))
            s(V.scalar_tensor_tensor(off[:, :], ej[:, :], float(CAP), bef[:, :], ALU.mult, ALU.add))
            s(V.tensor_copy(table[:, 0, :], off[:, :]))
            s(V.tensor_scalar(ej[:, :], ej[:, :], float(E - 1), None, ALU.min))
            s(V.tensor_copy(table[:, 1, :], ej[:, :]))
            dve.sem_inc(table_ready, 1)

        @block.scalar
        def _(act):
            A = nc.scalar.activation
            A(decay[:, :], decay[:, :], ACT.Tanh, scale=0.5).then_inc(act_tables, 1)
            act.wait_ge(tables, 1)
            A(logd[:, :], decay[:, :], ACT.Ln).then_inc(act_tables, 1)
            act.wait_ge(act_tables, 2)
            for q in range(NCH):
                A(df[:, q, :], logd[:, :], ACT.Exp, scale=c("pos1", CH)[:, q:q + 1]).then_inc(act_tables, 1)

            class Front:
                def __init__(self, n):
                    self.wait = waiter(act, n)

                def norm_out(self, lane, j, dst):
                    self.wait(rstd_done)
                    for q in range(NCH):
                        last = A(dst[:, q, :], hh[:, lane, q, :], ACT.Identity, bias=nb[:, j, q:q + 1],
                                 scale=rs[:, 0, j * NCH + q:j * NCH + q + 1])
                    last.then_inc((xln_done, xn_done)[j], 1)

                def x_t(self):
                    self.wait(xn_t)
                    A(xt[:, :, :], two(2, L), ACT.Copy).then_inc(xt_done, 1)

                def latent(self):
                    self.wait(lat_mm)
                    A(tl[:, :], bank[2][:, 0:L], ACT.Tanh, scale=0.5).then_inc(lat_th, 1)

                def rest(self, *chunks):
                    for q in chunks:
                        self.wait(rest_mm, q, NCH)
                        src = bank[REST[q]][0:CH, 0:NREST]
                        A(tg[:, q, :], src[:, 0:NPAR + D], ACT.Tanh, scale=0.5)
                        A(v[:, q, :], src[:, NPAR + D:], ACT.Copy).then_inc(rest_a, 1)

                def qk(self, *chunks):
                    for q in chunks:
                        self.wait(qk_mm, q, NCH)
                        src = bank[QK[q]][0:CH, 0:NQK]
                        A(qb[:, q * NQK:(q + 1) * NQK], src, ACT.Square)
                        A(qa[:, q * NQK:(q + 1) * NQK], src, ACT.Copy).then_inc(qk_sq, 1)

                def gate(self):
                    self.wait(gate_arg)
                    A(gt[:, 4, :], gt[:, 2, :], ACT.Tanh, scale=temp[:, :]).then_inc(gate_th, 1)

                def features(self):
                    for q in range(NCH):
                        self.wait(qk_rot, q, NCH)
                        A(qb[:, q * NQK:(q + 1) * NQK], qc[:, q * NQK:(q + 1) * NQK], ACT.Exp)
                        A(qa[:, q * NQK:(q + 1) * NQK], qc[:, q * NQK:(q + 1) * NQK], ACT.Relu).then_inc(qk_exp, 1)

                def qk_t(self):
                    for q in range(NCH):
                        self.wait(tq_mm, q, NCH)
                        src = mem.psum[:, (4, 6, 4)[q]:(4, 6, 4)[q] + 2, 0:GR * CH].rearrange("p k (g t) -> p k g t", g=GR)
                        A(qt[:, :, :, q * CH:(q + 1) * CH], src, ACT.Copy).then_inc(tq_a, 1)

                def sums(self, q):
                    self.wait(pv_mm, q, NCH)
                    A(ot[:, q, :], bank[(7, 6, 7)[q]][:, 0:GR * CH], ACT.Copy).then_inc(ot_a, 1)

            class Back:
                def __init__(self, n, lane):
                    self.lane, self.wait = lane, waiter(act, n)

                def sumsq(self, j, src, ready, done):
                    self.wait(ready)
                    for q in range(NCH):
                        last = A(junk[:, j, q, :], src[:, q, :], ACT.Square, scale=SCALE_MEAN, accum_out=sa[:, j, q:q + 1])
                    last.then_inc(done, 1)

                def copy_t(self, k, ready, done):
                    self.wait(ready)
                    A(xb[:, :, :], two(k, L), ACT.Copy).then_inc(done, 1)

                def tanh(self, m):
                    self.wait(f_mm, m, 4)
                    A(th[:, m, :], bank[FB[m]][:, 0:L], ACT.Tanh, scale=0.5).then_inc(f_th, 1)

                def row(self):
                    self.wait(flat_done)
                    A(row[:, self.lane, 1, :, 0:D], row[:, self.lane, 0, :, 0:D], ACT.Copy).then_inc(row_copied, 1)

                def top(self):
                    self.wait(top_done)
                    A(ew[:, 1, :], ew[:, 0, :], ACT.Exp).then_inc(ew_exp, 1)

            f = Front(0)
            f.norm_out(0, 1, xn); f.x_t(); f.norm_out(0, 0, xln[:, 0]); f.latent(); f.rest(0, 1, 2); f.qk(0, 1, 2); f.gate(); f.features(); f.qk_t()
            Front(1).norm_out(1, 1, xn)
            Front(1).x_t()
            Front(1).norm_out(1, 0, xln[:, 1])
            Front(1).latent()
            f.sums(0); f.sums(1); f.sums(2)
            with act.Fori(0, NP) as i:
                for b in range(2):
                    f, k, after = Front(i * 2 + (b + 1)), Back(i * 2 + b, b), Front(i * 2 + (b + 2))
                    f.rest(0, 1)
                    k.copy_t(0, at_t, at_a)
                    k.sumsq(0, att[:, b], att_done, att_ss)
                    f.rest(2)
                    f.qk(0)
                    k.sumsq(1, x1, x1_done, x1_ss)
                    f.qk(1, 2)
                    f.gate()
                    k.copy_t(0, x2_t, x2_a)
                    k.tanh(0)
                    k.tanh(1)
                    k.tanh(2)
                    f.features()
                    k.tanh(3)
                    f.qk_t()
                    after.norm_out(b, 1, xn)
                    after.x_t()
                    after.norm_out(b, 0, xln[:, b])
                    k.row()
                    after.latent()
                    f.sums(0)
                    k.copy_t(2, fl_t, fl_a)
                    f.sums(1)
                    k.top()
                    f.sums(2)

        @block.gpsimd
        def _(pool):
            PO = nc.gpsimd
            pool.sem_inc(row_free, 2)
            pool.sem_inc(h2_free, 2)
            PO.memset(mhalf[:, :], -0.5).then_inc(cleared, 1)
            PO.memset(zeros[:, :], 0.0).then_inc(cleared, 1)
            PO.memset(states[:, :, :, :, :], 0.0).then_inc(cleared, 1)
            PO.memset(qf[:, :, :], 0.0).then_inc(cleared, 1)
            pool.wait_ge(cleared, 4)

            def norm(n):
                waiter(pool, n)(var_done)
                PO.tensor_tensor(rs[:, 0, :], ve2[:, 0, :], mhalf[:, 0:2 * NCH], ALU.pow).then_inc(rstd_step, 1)
                waiter(pool, n)(rstd_step)
                PO.tensor_tensor(nb[:, :, :].rearrange("p j q -> p (j q)"), nm[:, :, :].rearrange("p j q -> p (j q)"), rs[:, 0, :],
                                 ALU.mult).then_inc(rstd_done, 1)

            def cos(n):
                waiter(pool, n)(qk_sq, NCH - 1, NCH)
                for q in range(NCH):
                    a, o = [t[:, q * NQK:(q + 1) * NQK].rearrange("p (k h d) -> p k h d", k=2, d=DH) for t in (qa, qc)]
                    last = PO.tensor_tensor(o, a, COS[:, q, :, :].unsqueeze(2).to_broadcast([CH, 2, H, DH]), ALU.mult)
                last.then_inc(qk_cos, 1)
                waiter(pool, n)(qk_cos)
                waiter(pool, n)(qk_sin, 5, 6)
                PO.tensor_tensor(qc[:, :], qc[:, :], qd[:, :], ALU.add).then_inc(qk_sum, 1)

            def values(n):
                wait = waiter(pool, n)
                wait(gate_w)
                wait(rest_a, NCH - 1, NCH)
                PO.tensor_tensor(ve[:, :, :, 0:DH], v[:, :, :].rearrange("p c (h d) -> p c h d", d=DH),
                                 gt[:, 5, :].rearrange("p (c h) -> p c h", c=NCH).unsqueeze(3).to_broadcast([CH, NCH, H, DH]),
                                 ALU.mult).then_inc(ve_done, 1)

            def root(n, j, ready, done):
                wait = waiter(pool, n)
                wait(ready)
                PO.tensor_tensor(rr[:, j, :], sa[:, j, :], mhalf[:, 0:NCH], ALU.pow).then_inc(done, 1)

            norm(0)
            pool.wait_ge(tables, 2)
            cos(0)
            values(0)
            norm(1)

            def scatter(n, lane, sent_before):
                wait = waiter(pool, n)
                wait(dest_done)
                wait(rows_numbered)
                wait(row_copied)
                apart(pool)
                for q in range(NCH):
                    for j in range(2):
                        PO.indirect_dma_start(out=mem.xs, out_offset=bass.IndirectOffsetOnAxis(ap=di[:, lane, q, j:j + 1], axis=0),
                                              in_=row[:, lane, j, q, :], in_offset=None).then_inc(sent[lane], 16)
                return sent_before + 16 * 2 * NCH

            def pair(i, first=False):
                for b in range(2):
                    n = i * 2 + b
                    wait = waiter(pool, n)
                    root(n, 0, att_ss, att_rs)
                    root(n, 1, x1_ss, x1_rs)
                    cos(i * 2 + (b + 1))
                    PO.tensor_tensor(hx[:, :, :], hh[:, b], x1[:, :, 0:D], ALU.add).then_inc(h_used, 1)
                    values(i * 2 + (b + 1))
                    if b or not first:
                        arrived = scatter(i * 2 + (b - 1), 1 - b, i * (16 * 2 * NCH) - (0 if b else 16 * 2 * NCH))
                    norm(i * 2 + (b + 2))
                    wait(var2_done)
                    PO.tensor_tensor(rs[:, 1, 0:NCH], ve2[:, 1, 0:NCH], mhalf[:, 0:NCH], ALU.pow).then_inc(rstd2_done, 1)
                    PO.tensor_scalar(tokno[:, :], tokno[:, :], float(L), None, ALU.add).then_inc(tok_step, 1)
                    wait(flat_done)
                    wait(tok_step)
                    apart(pool)
                    for j in range(2):
                        last = PO.tensor_copy(row[:, b, j, :, D], tokno[:, :])
                    last.then_inc(rows_numbered, 1)
                    if b or not first:
                        pool.wait_ge(sent[1 - b], arrived)
                        pool.sem_inc(row_free, 1)

            pair(0, first=True)
            with pool.Fori(1, NP) as i:
                pair(i)
            pool.wait_ge(sent[1], scatter(2 * NP - 1, 1, (NP - 1) * 16 * 2 * NCH))

        @block.tensor
        def _(pe):
            MM, TR = nc.tensor.matmul, nc.tensor.transpose
            ident = c("ident", CH)[:, 0:CH]
            pe.wait_ge(cleared, 4)

            def keep_clock(k, n):
                for _ in range(n):
                    MM(bank[k][0:32, 0:512], zeros[:, 0:32], zeros[:, :], start=True, stop=True)

            def transpose_rows(src, k, done):
                for kk in range(2):
                    for q in range(NCH):
                        last = TR(bank[k + kk][0:KD, q * CH:(q + 1) * CH], src[:, q, kk * KD:(kk + 1) * KD], ident)
                last.then_inc(done, 1)

            def rows_out(w, ks, src, done):
                for q in range(NCH):
                    for kk in range(ks):
                        last = MM(bank[2 + q // 2][0:CH, (q % 2) * D:(q % 2 + 1) * D], src[:, kk, q * CH:(q + 1) * CH],
                                  w[:, kk, :], start=(kk == 0), stop=(kk == ks - 1))
                last.then_inc(done, 1)

            class Front:
                def __init__(self, n):
                    self.wait = waiter(pe, n)

                def x_t(self):
                    self.wait(xn_done)
                    transpose_rows(xn, 2, xn_t)

                def latent(self):
                    self.wait(xt_done)
                    for kk in range(2):
                        last = MM(bank[2][:, 0:L], wcomp[:, kk, :], xt[:, kk, :], start=(kk == 0), stop=(kk == 1))
                    last.then_inc(lat_mm, 1)

                def rest(self, *chunks):
                    self.wait(lat_done)
                    for q in chunks:
                        MM(bank[REST[q]][0:CH, 0:NREST], lat[:, q * CH:(q + 1) * CH], wlat[:, NQK:],
                           start=True, stop=True).then_inc(rest_mm, 1)

                def qk(self):
                    for q in range(NCH):
                        if q:
                            self.wait(rest_d, q - 1, NCH)
                        MM(bank[QK[q]][0:CH, 0:NQK], lat[:, q * CH:(q + 1) * CH], wlat[:, 0:NQK],
                           start=True, stop=True).then_inc(qk_mm, 1)

                def qk_t(self, *chunks):
                    for q in chunks:
                        self.wait(qf_done, q, NCH)
                        if q == 2:
                            self.wait(tq_a, 0, NCH)
                        for kk in range(2):
                            for g in range(GR):
                                h0 = (q * 2 + kk) * H + 4 * g
                                last = TR(bank[(4, 6, 4)[q] + kk][:, g * CH:(g + 1) * CH],
                                          qf[:, h0:h0 + 4, :].rearrange("p h d -> p (h d)"), ident)
                        last.then_inc(tq_mm, 1)

                def state(self, s_):
                    self.wait(ve_done)
                    self.wait(tq_a, 1, NCH)
                    for g in range(GR):
                        for q in range(s_ + 1):
                            h0 = (q * 2 + 1) * H + 4 * g
                            last = MM(bank[6 + s_][:, g * 128:(g + 1) * 128],
                                      qf[:, h0:h0 + 4, :].rearrange("p h d -> p (h d)"),
                                      ve[:, q, 4 * g:4 * g + 4, :].rearrange("p h e -> p (h e)"),
                                      start=(q == 0), stop=(q == s_))
                    last.then_inc(st_mm, 1)

                def heads(self, after, k=None):
                    self.state(0)
                    self.state(1)
                    self.scores(0)
                    if k:
                        k.wait(h2_done)
                        keep_clock(3, 3)
                    after.x_t()
                    self.scores(1)
                    after.latent()
                    keep_clock(3, 2)
                    self.values(0)
                    if k:
                        after.wait(lat_done)
                        keep_clock(3, 2)
                        k.flat_t()
                    self.scores(2)
                    if k:
                        k.logits()
                    self.values(1)
                    self.values(2)

                def scores(self, q):
                    if q == 0:
                        self.wait(tq_a, 2, NCH)
                    for r in range(4):
                        if q:
                            self.wait(sc_d, 4 * (q - 1) + r, 4 * NCH)
                        for g in range(GR):
                            last = MM(bank[SC[r]][0:CH, g * CW:(g + 1) * CW], qt[32 * r:32 * r + 32, 1, g, q * CH:(q + 1) * CH],
                                      qt[32 * r:32 * r + 32, 0, g, q * CH:q * CH + CW], start=True, stop=True)
                        last.then_inc(sc_mm, 1)

                def values(self, q):
                    self.wait(sc_d, 4 * q + 3, 4 * NCH)
                    if q < 2:
                        self.wait(st_d, 1, 2)
                    else:
                        self.wait(ot_a, 0, NCH)
                    to = bank[(7, 6, 7)[q]]
                    for g in range(GR):
                        t = slice(g * CH, (g + 1) * CH)
                        if q:
                            MM(to[:, t], states[:, q - 1, g].rearrange("p r e -> p (r e)"), qt[:, 0, g, q * CH:(q + 1) * CH],
                               start=True, stop=False)
                        for r in range(4):
                            last = MM(to[32 * r:32 * r + 32, t], ve[:, q, 4 * g + r, :], sm[:, q % 2, r, t],
                                      start=(q == 0), stop=True)
                    last.then_inc(pv_mm, 1)

                def sums_t(self, q):
                    self.wait(ot_a, q, NCH)
                    for g in range(GR):
                        last = TR(bank[(0, 1, 6)[q]][0:CH, g * 128:(g + 1) * 128], ot[:, q, g * CH:(g + 1) * CH], mem.c("ident"))
                    if q:
                        last.then_inc(ot_mm, 1)

            class Back:
                def __init__(self, n, lane):
                    self.lane, self.wait = lane, waiter(pe, n)

                def att_t(self):
                    self.wait(att_done)
                    transpose_rows(att[:, self.lane], 0, at_t)

                def project(self):
                    self.wait(rk_read)
                    self.wait(at_a)
                    rows_out(wproj, 2, xb, pr_mm)

                def norm2_t(self):
                    self.wait(xn2_done)
                    transpose_rows(xn2, 0, x2_t)

                def up(self, m):
                    if m == 0:
                        self.wait(x2_a)
                    if m == 3:
                        self.wait(f_d, 0, 4)
                    for j in range(2):
                        for kk in range(2):
                            last = MM(bank[FB[m] + j][:, 0:L], w12[:, kk, j, m * 128:(m + 1) * 128], xb[:, kk, :],
                                      start=(kk == 0), stop=(kk == 1))
                    last.then_inc(f_mm, 1)

                def down(self, m):
                    self.wait(f_d, m, 4)
                    for q in range(2):
                        MM(bank[2 + q][0:CH, 0:D], hid[:, m, q * CH:(q + 1) * CH], w3[:, m, :], start=(m == 0), stop=(m == 3))

                def down_last(self):
                    for m in range(4):
                        last = MM(bank[2][0:CH, D:2 * D], hid[:, m, 2 * CH:3 * CH], w3[:, m, :], start=(m == 0), stop=(m == 3))
                    last.then_inc(w3_mm, 1)

                def flat_t(self):
                    self.wait(flat_done)
                    transpose_rows(row[:, self.lane, 0], 2, fl_t)

                def logits(self):
                    self.wait(fl_a)
                    for q in range(NCH):
                        for kk in range(2):
                            last = MM(bank[2][0:CH, q * CW:(q + 1) * CW], xb[:, kk, q * CH:(q + 1) * CH], wr[:, kk, :],
                                      start=(kk == 0), stop=(kk == 1))
                    last.then_inc(lg_mm, 1)

                def ranks(self):
                    self.wait(oh_done)
                    src = ohs[:, :, :].rearrange("p c e -> p (c e)")
                    MM(bank[3][0:CH, 0:NCH * E], c("before", CH), src, start=True, stop=True)
                    MM(bank[3][0:CH, 32:32 + NCH * E], c("ones", CH), src, start=True, stop=True).then_inc(rk_mm, 1)

            f = Front(0)
            f.x_t(); f.latent(); f.rest(0, 1, 2); f.qk(); f.qk_t(0, 1, 2); f.heads(Front(1))
            f.sums_t(0); f.sums_t(1); f.sums_t(2)
            with pe.Fori(0, NP) as i:
                for b in range(2):
                    f, k = Front(i * 2 + (b + 1)), Back(i * 2 + b, b)
                    f.rest(0, 1)
                    k.att_t()
                    k.project()
                    f.rest(2)
                    f.qk()
                    keep_clock(0, 5)
                    k.norm2_t()
                    keep_clock(2, 3)
                    for m in range(4):
                        if m == 1:
                            f.wait(qk_sq, 2, NCH)
                        if m == 2:
                            f.wait(rest_d, 2, NCH)
                        k.up(m)
                        if m > 1:
                            k.down(m - 2)
                    f.qk_t(0)
                    k.down(2)
                    f.qk_t(1)
                    k.down(3)
                    f.qk_t(2)
                    k.down_last()
                    f.heads(Front(i * 2 + (b + 2)), k)
                    f.sums_t(0)
                    f.sums_t(1)
                    f.sums_t(2)
                    k.ranks()


def experts(nc, mem, I, out):
    NM = F // 128
    NPAIR, LAST = NTASK // 2, NTASK % 2
    assert LAST == 1
    with ExitStack() as ctx:
        mem.ctx = ctx
        sb, sem, X, Y, c = mem.sb, mem.sem, mem.X, mem.Y, mem.c
        xr = sb("task_rows", [128, 2, TC, ROW])
        w1, w2 = sb("task_w1", [KD, 2, 2, F]), sb("task_w2", [128, 2, NM, D])
        b1, b2 = sb("task_b1", [128, 2, NM]), sb("task_b2", [128, 2, D])
        w1s = [sb(f"task_w1_{n}", [KD, 2, 2, F], f32r) for n in ("hi", "lo")]
        xts = [sb(f"task_x_t_{n}", [KD, 2, 2, T], f32r) for n in ("hi", "lo")]
        hid = sb("task_hidden", [128, 2, NM, T])
        wt, ids = sb("task_weight", [128, 2, TC]), sb("task_ids", [128, 2, TC], i32)
        ys = sb("task_out", [128, 2, TC, D])
        table = mem.table
        ld_x, ld_1, ld_2 = ([sem(f"{n}{p}") for p in range(2)] for n in ("task_rows_loaded", "task_w1_loaded", "task_w2_loaded"))
        x_free, w1_free, b1_free, w2_free, y_free = (sem("task_rows_free"), sem("w1_free"), sem("b1_free"), sem("w2_free"),
                                                     sem("task_out_free"))
        tr, xt_hi, xt_lo = sem("task_transposed"), sem("task_xt_hi"), sem("task_xt_lo")
        w1_hi, w1_lo = sem("task_w1_hi"), sem("task_w1_lo")
        l1, gelu, l2, y_add, y_done = sem("up_mm"), sem("gelu_done"), sem("down_mm"), sem("bias_added"), sem("task_out_done")
        waited = sem("task_waits_apart")
        added = [sem(f"out_added{p}") for p in range(2)]
        block = ctx.enter_context(nc.Block())
        UP = [X[2], X[3], Y[0][0], Y[0][1]]
        DOWN = Y[1]

        @block.sync
        def _(sp):
            def expert_of(j):
                return sp.value_load(table[0:1, 1, bass.ds(j, 1)], min_val=0, max_val=E - 1)

            def load_1(j, p):
                row0 = sp.value_load(table[0:1, 0, bass.ds(j, 1)], min_val=0, max_val=E * CAP + IDLE * T)
                e = expert_of(j)
                sp.wait_ge(x_free, j + 1)
                sp.dma_start(xr[:, p], mem.xs[bass.ds(row0, T), :].rearrange("(c p) d -> p c d", c=TC)).then_inc(ld_x[p], 16)
                sp.wait_ge(w1_free, j + 1)
                sp.dma_start(w1[:, p], I["ffn_w1"][bass.ds(e, 1), :, :].rearrange("o (k p) n -> p (o k) n", k=2)).then_inc(ld_1[p], 16)
                sp.wait_ge(b1_free, j + 1)
                sp.dma_start(b1[:, p], I["ffn_b1"][bass.ds(e, 1), :].rearrange("o (p m) -> p (o m)", m=NM)).then_inc(ld_1[p], 16)

            def load_2(j, p):
                e = expert_of(j)
                sp.wait_ge(w2_free, j + 1)
                sp.dma_start(w2[:, p], I["ffn_w2"][bass.ds(e, 1), :, :].rearrange("o (p m) n -> p (o m) n", m=NM)).then_inc(ld_2[p], 16)
                sp.dma_start(b2[:, p, :], I["ffn_b2"][bass.ds(e, 1), :].rearrange("o n -> (o n)").partition_broadcast(128)).then_inc(ld_2[p], 16)
            load_1(0, 0)
            with sp.Fori(0, NPAIR) as i:
                for p in range(2):
                    load_1(i * 2 + (p + 1), 1 - p)
                    load_2(i * 2 + p, p)
            load_2(NTASK - 1, 0)

        @block.vector
        def _(dve):
            V = nc.vector

            def split_w1(j, p):
                for kk in range(2):
                    dve.wait_ge(w1_hi, j * 2 + kk + 1)
                    V.tensor_tensor(w1s[1][:, p, kk, :], w1[:, p, kk, :], w1s[0][:, p, kk, :].bitcast(f32),
                                    ALU.subtract).then_inc(w1_lo, 1)
                dve.wait_ge(w1_lo, j * 2 + 2)
                dve.sem_inc(w1_free, 1)

            def rows_in(j, p):
                for kk in range(2):
                    dve.wait_ge(xt_hi, j * 2 + kk + 1)
                    V.tensor_tensor(xts[1][:, p, kk, :], X[kk][0:KD, 0:T], xts[0][:, p, kk, :].bitcast(f32),
                                    ALU.subtract).then_inc(xt_lo, 1)

            def rows_read(j, p):
                V.tensor_copy(wt[:, p, :], xr[:, p, :, D + 1])
                dve.wait_ge(y_free, j + 1)
                V.tensor_copy(ids[:, p, :], xr[:, p, :, D]).then_inc(x_free, 1)

            def rows_out(j, p, loads):
                dve.wait_ge(ld_2[p], loads)
                for q in range(TC):
                    dve.wait_ge(l2, j * TC + q + 1)
                    V.tensor_tensor(ys[:, p, q, :], DOWN[q % 2][:, 0:D], b2[:, p, :], ALU.add).then_inc(y_add, 1)
                    dve.wait_ge(y_add, j * TC + q + 1)
                    V.tensor_scalar(ys[:, p, q, :], ys[:, p, q, :], wt[:, p, q:q + 1], None, ALU.mult).then_inc(y_done, 1)
                dve.wait_ge(y_done, j * TC + TC)
                dve.sem_inc(w2_free, 1)
            for j in range(2):
                split_w1(j, j)
                rows_in(j, j)
                rows_read(j, j)
            with dve.Fori(0, NPAIR - 1) as i:
                for p in range(2):
                    split_w1(i * 2 + (p + 2), p)
                    rows_in(i * 2 + (p + 2), p)
                    rows_out(i * 2 + p, p, i * 32 + 32)
                    rows_read(i * 2 + (p + 2), p)
            split_w1(NTASK - 1, 0)
            rows_in(NTASK - 1, 0)
            rows_out(NTASK - 3, 0, NPAIR * 32)
            rows_read(NTASK - 1, 0)
            rows_out(NTASK - 2, 1, NPAIR * 32)
            rows_out(NTASK - 1, 0, (NPAIR + 1) * 32)

        @block.scalar
        def _(act):
            def split_w1(j, p, loads):
                act.wait_ge(ld_1[p], loads)
                for kk in range(2):
                    nc.scalar.activation(w1s[0][:, p, kk, :], w1[:, p, kk, :], ACT.Copy).then_inc(w1_hi, 1)

            def rows_in(j, p):
                act.wait_ge(tr, j + 1)
                for kk in range(2):
                    nc.scalar.activation(xts[0][:, p, kk, :], X[kk][0:KD, 0:T], ACT.Copy).then_inc(xt_hi, 1)

            def up(j, p):
                for m in range(NM):
                    act.wait_ge(l1, j * NM + m + 1)
                    nc.scalar.activation(hid[:, p, m, :], UP[m % 4][:, 0:T], ACT.Gelu, bias=b1[:, p, m:m + 1]).then_inc(gelu, 1)
                act.wait_ge(gelu, j * NM + NM)
                act.sem_inc(b1_free, 1)
            split_w1(0, 0, 32)
            rows_in(0, 0)
            split_w1(1, 1, 32)
            up(0, 0)
            rows_in(1, 1)
            with act.Fori(0, NPAIR - 1) as i:
                for p in range(2):
                    split_w1(i * 2 + (p + 2), p, i * 32 + 64)
                    up(i * 2 + (p + 1), 1 - p)
                    rows_in(i * 2 + (p + 2), p)
            split_w1(NTASK - 1, 0, (NPAIR + 1) * 32)
            up(NTASK - 2, 1)
            rows_in(NTASK - 1, 0)
            up(NTASK - 1, 0)

        @block.gpsimd
        def _(pool):
            pool.sem_inc(x_free, 2)
            pool.sem_inc(w1_free, 2)
            pool.sem_inc(b1_free, 2)
            pool.sem_inc(w2_free, 2)
            pool.sem_inc(y_free, 2)

            def add(j, p, sent):
                for q in range(TC):
                    pool.wait_ge(y_done, j * TC + q + 1)
                    pool.sem_inc(waited, 1)
                    nc.gpsimd.indirect_dma_start(out=out, out_offset=bass.IndirectOffsetOnAxis(ap=ids[:, p, q:q + 1], axis=0),
                                                 in_=ys[:, p, q, :], in_offset=None, compute_op=ALU.add).then_inc(added[p], 16)
                pool.wait_ge(added[p], sent)
                pool.sem_inc(y_free, 1)
            with pool.Fori(0, NPAIR) as i:
                for p in range(2):
                    add(i * 2 + p, p, i * (16 * TC) + 16 * TC)
            add(NTASK - 1, 0, (NPAIR + 1) * 16 * TC)

        @block.tensor
        def _(pe):
            MM, TR = nc.tensor.matmul, nc.tensor.transpose
            ident = c("ident")

            def rows_in(p, loads):
                pe.wait_ge(ld_x[p], loads)
                for kk in range(2):
                    for q in range(TC):
                        last = TR(X[kk][0:KD, q * 128:(q + 1) * 128], xr[:, p, q, kk * KD:(kk + 1) * KD], ident)
                last.then_inc(tr, 1)

            def up(j, p):
                pe.wait_ge(xt_lo, j * 2 + 2)
                pe.wait_ge(w1_lo, j * 2 + 2)
                pe.wait_ge(gelu, j * NM)
                parts = [(kk, w, x) for kk in range(2) for w, x in ((0, 0), (0, 1), (1, 0))]
                for m in range(NM):
                    if m >= 4:
                        pe.wait_ge(gelu, j * NM + (m - 3))
                    for n, (kk, w, x) in enumerate(parts):
                        last = MM(UP[m % 4][:, 0:T], w1s[w][:, p, kk, m::NM], xts[x][:, p, kk, :],
                                  start=(n == 0), stop=(n == len(parts) - 1))
                    last.then_inc(l1, 1)

            def down(j, p, loads):
                pe.wait_ge(ld_2[p], loads)
                pe.wait_ge(gelu, j * NM + NM)
                for q in range(TC):
                    if q != 1:
                        pe.wait_ge(y_add, j * TC + (q - 1 if q else 0))
                    for m in range(NM):
                        last = MM(DOWN[q % 2][:, 0:D], hid[:, p, m, q * 128:(q + 1) * 128], w2[:, p, m, :],
                                  start=(m == 0), stop=(m == NM - 1))
                    last.then_inc(l2, 1)
            rows_in(0, 16)
            up(0, 0)
            rows_in(1, 16)
            with pe.Fori(0, NPAIR - 1) as i:
                for p in range(2):
                    up(i * 2 + (p + 1), 1 - p)
                    rows_in(p, i * 16 + 32)
                    down(i * 2 + p, p, i * 32 + 32)
            up(NTASK - 2, 1)
            rows_in(0, (NPAIR + 1) * 16)
            down(NTASK - 3, 0, NPAIR * 32)
            up(NTASK - 1, 0)
            down(NTASK - 2, 1, NPAIR * 32)
            down(NTASK - 1, 0, (NPAIR + 1) * 32)


def program(nc, I, out):
    with ExitStack() as ctx:
        mem = Memory(nc, ctx)
        patches(nc, mem, I)
        sequences(nc, mem, I, out)
        experts(nc, mem, I, out)


_INS = {"x": "x", "txt": "txt"}
_INS |= {"L0_" + n: n for n in ["tok_W", "tok_b"] + ["attn_" + n for n in (
    "ln_w", "w_comp", "w_qkv", "w_reso", "qn_w", "kn_w", "w_outgate", "head_decay", "temperature", "w_proj", "memn_w",
    "ffn_ln_w", "w1", "w2", "w3")] + ["ffn_" + n for n in ("router_w", "w1", "b1", "w2", "b2")]}


def kernel(**inputs):
    import numpy as _np
    import concourse.bacc as _bacc
    from concourse import mybir as _mybir
    from concourse.bass_utils import run_bass_kernel_spmd as _run

    nc = _bacc.Bacc("TRN2", target_bir_lowering=False, num_devices=1)
    arrays = {f"in_{short}": _np.ascontiguousarray(inputs[name]) for name, short in _INS.items()}
    arrays["in_const"] = CONST
    aps = {k[3:]: nc.dram_tensor(k, a.shape, _mybir.dt.from_np(a.dtype), kind="ExternalInput").ap() for k, a in arrays.items()}
    out = nc.dram_tensor("out", (NTOK + T, D), _mybir.dt.float32, kind="ExternalOutput").ap()
    program(nc, aps, out)
    r = _run(nc, [arrays], core_ids=[0])
    return r.results[0]["out"][:NTOK].reshape(B, L, D)
```
